# Optimizing a Trainium2 kernel written in Bass

```python
import numpy as np
import jax
import jax.numpy as jnp

def _softmax(x, axis=-1):
    return jax.nn.softmax(x, axis=axis)

def _gelu(x):
    return jax.nn.gelu(x, approximate=True)

def _silu(x):
    return jax.nn.silu(x)

def _sigmoid(x):
    return jax.nn.sigmoid(x)

def _layernorm(x, axis=-1, eps=1e-05):
    m = jnp.mean(x, axis=axis, keepdims=True)
    v = jnp.var(x, axis=axis, keepdims=True)
    return (x - m) / jnp.sqrt(v + eps)

def _scatter_add(tgt, idx, src, axis=0):
    return tgt.at[idx].add(src)

def _segment_sum(src, seg, n):
    return jax.ops.segment_sum(src, seg, n)
kernel_name = 'mk_sandwich_d4_jaxref_r8_53e42c'

def setup_inputs(seed: int=0):
    np.random.seed(seed)
    _w = jnp.asarray

    def _L0_attn_setup():
        import jax, jax.numpy as jnp
        import numpy as np
        EMB_DIM = 512
        N_HEADS = 32
        QKV_DIM = EMB_DIM // N_HEADS
        B, S = (4, 512)
        key = jax.random.key(seed)
        ks = jax.random.split(key, 7)
        std = 1.0 / np.sqrt(EMB_DIM)
        x = jax.random.normal(ks[0], (B, S, EMB_DIM), dtype=jnp.float32)
        Wq = jax.random.normal(ks[1], (EMB_DIM, QKV_DIM, N_HEADS), dtype=jnp.float32) * std
        bq = jnp.zeros((QKV_DIM, N_HEADS), dtype=jnp.float32)
        Wk = jax.random.normal(ks[2], (EMB_DIM, QKV_DIM, 1), dtype=jnp.float32) * std
        bk = jnp.zeros((QKV_DIM, 1), dtype=jnp.float32)
        Wv = jax.random.normal(ks[3], (EMB_DIM, QKV_DIM, 1), dtype=jnp.float32) * std
        bv = jnp.zeros((QKV_DIM, 1), dtype=jnp.float32)
        return {'x': x, 'Wq': Wq, 'bq': bq, 'Wk': Wk, 'bk': bk, 'Wv': Wv, 'bv': bv}
    _L0_attn_in = _L0_attn_setup()

    def _L0_ffn_setup():
        import jax, jax.numpy as jnp
        import numpy as np
        B, S, H, I, R = (4, 32, 512, 1792, 4)

        def _anemll_linear(x, w, su, sv):
            w_eff = w * (su @ sv)
            return jnp.einsum('bsh,oh->bso', x, w_eff)
        key = jax.random.key(seed)
        ks = jax.random.split(key, 10)
        sd = 0.02
        return {'x': jax.random.normal(ks[0], (B, S, H), dtype=jnp.float32), 'gate_w': jax.random.normal(ks[1], (I, H), dtype=jnp.float32) * sd, 'gate_su': jax.random.normal(ks[2], (I, R), dtype=jnp.float32) * 0.5, 'gate_sv': jax.random.normal(ks[3], (R, H), dtype=jnp.float32) * 0.5, 'up_w': jax.random.normal(ks[4], (I, H), dtype=jnp.float32) * sd, 'up_su': jax.random.normal(ks[5], (I, R), dtype=jnp.float32) * 0.5, 'up_sv': jax.random.normal(ks[6], (R, H), dtype=jnp.float32) * 0.5, 'down_w': jax.random.normal(ks[7], (H, I), dtype=jnp.float32) * sd, 'down_su': jax.random.normal(ks[8], (H, R), dtype=jnp.float32) * 0.5, 'down_sv': jax.random.normal(ks[9], (R, I), dtype=jnp.float32) * 0.5}
    _L0_ffn_in = _L0_ffn_setup()

    def _L1_attn_setup():
        import math
        import jax, jax.numpy as jnp
        import numpy as np
        NUM_HEADS = 32
        HIDDEN = 512
        HEAD_DIM = HIDDEN // NUM_HEADS
        NEG_INF = -1e+30

        def _alibi_slopes(n: int) -> jnp.ndarray:
            cp2 = 2 ** math.floor(math.log2(n))
            base = 2.0 ** (-2.0 ** (-(math.log2(cp2) - 3)))
            slopes = base ** np.arange(1, cp2 + 1, dtype=np.float64)
            if cp2 != n:
                extra_base = 2.0 ** (-2.0 ** (-(math.log2(2 * cp2) - 3)))
                rem = min(cp2, n - cp2)
                extra = extra_base ** np.arange(1, 1 + 2 * rem, 2, dtype=np.float64)
                slopes = np.concatenate([slopes, extra])
            return jnp.asarray(slopes, dtype=jnp.float32)
        key = jax.random.key(seed)
        k1, k2, k3 = jax.random.split(key, 3)
        B, S = (2, 256)
        hidden_states = jax.random.normal(k1, (B, S, HIDDEN), dtype=jnp.float32)
        Wqkv = jax.random.normal(k2, (HIDDEN, NUM_HEADS * HEAD_DIM + 2 * HEAD_DIM), dtype=jnp.float32) * 0.02
        Wo = jax.random.normal(k3, (HIDDEN, HIDDEN), dtype=jnp.float32) * 0.02
        return {'hidden_states': hidden_states, 'Wqkv': Wqkv, 'Wo': Wo}
    _L1_attn_in = _L1_attn_setup()

    def _L1_ffn_setup():
        import jax, jax.numpy as jnp
        import numpy as np
        D_IN, D_OUT = (512, 512)
        B, S = (2, 256)
        key = jax.random.key(seed)
        kx, kw = jax.random.split(key)
        x = jax.random.normal(kx, (B, S, D_IN), dtype=jnp.float32)
        w = jax.random.normal(kw, (D_IN, D_OUT), dtype=jnp.float32)
        sign = jnp.where(w >= 0, 1.0, -1.0).astype(jnp.float32)
        scale = jnp.abs(w).mean().astype(jnp.float32)
        return {'x': x, 'sign': sign, 'scale': scale}
    _L1_ffn_in = _L1_ffn_setup()

    def _L2_attn_setup():
        import jax, jax.numpy as jnp
        import numpy as np
        from jax import lax
        H = 64
        P = 64
        N = 128
        G = 8
        K = 4
        D_MODEL = 512
        I = H * P
        GN = G * N
        CONV_DIM = I + 2 * GN
        PROJ = I + CONV_DIM + H
        EPS = 1e-05
        GROUP_SIZE = I // G

        def _reference_tuple_inner(hidden_states, in_proj_w, conv_weight, conv_bias, dt_bias, A_log, D, norm_weight, out_proj_w):
            B, L, _ = hidden_states.shape
            proj = jnp.einsum('bld,pd->blp', hidden_states, in_proj_w)
            gate = proj[..., :I]
            hbc = proj[..., I:I + CONV_DIM]
            dt = proj[..., -H:]
            pad = jnp.pad(hbc, ((0, 0), (K - 1, 0), (0, 0)))
            conv = conv_bias
            for k in range(K):
                conv = conv + pad[:, k:k + L, :] * conv_weight[:, k]
            xBC = jax.nn.silu(conv)
            x = xBC[..., :I].reshape(B, L, H, P)
            Bm = xBC[..., I:I + GN].reshape(B, L, G, N)
            Cm = xBC[..., I + GN:].reshape(B, L, G, N)
            hpg = H // G
            B_h = jnp.repeat(Bm, hpg, axis=2)
            C_h = jnp.repeat(Cm, hpg, axis=2)
            dt_p = jax.nn.softplus(dt + dt_bias)
            A = -jnp.exp(A_log)
            dA = jnp.exp(dt_p * A)
            dtx = dt_p[..., None] * x

            def step(state, inp):
                dA_t, dtx_t, B_t, C_t = inp
                state = state * dA_t[..., None, None] + dtx_t[..., None] * B_t[:, :, None, :]
                y_t = jnp.einsum('bhpn,bhn->bhp', state, C_t)
                return (state, y_t)
            xs = (jnp.moveaxis(dA, 1, 0), jnp.moveaxis(dtx, 1, 0), jnp.moveaxis(B_h, 1, 0), jnp.moveaxis(C_h, 1, 0))
            state0 = jnp.zeros((B, H, P, N), jnp.float32)
            final_state, ys = lax.scan(step, state0, xs)
            y = jnp.moveaxis(ys, 0, 1) + x * D[None, None, :, None]
            y = y.reshape(B, L, I)
            yg = y.reshape(B, L, G, GROUP_SIZE)
            var = jnp.mean(yg * yg, axis=-1, keepdims=True)
            yn = (yg * lax.rsqrt(var + EPS)).reshape(B, L, I) * norm_weight
            yn = yn * jax.nn.silu(gate)
            out = jnp.einsum('bli,di->bld', yn, out_proj_w)
            conv_state_new = jnp.moveaxis(hbc[:, L - (K - 1):, :], 1, 2)
            return (out, conv_state_new, final_state)
        key = jax.random.key(seed)
        ks = jax.random.split(key, 6)
        B, L = (2, 256)
        s = 0.02
        return {'hidden_states': jax.random.normal(ks[0], (B, L, D_MODEL), jnp.float32), 'in_proj_w': jax.random.normal(ks[1], (PROJ, D_MODEL), jnp.float32) * s, 'conv_weight': jax.random.normal(ks[2], (CONV_DIM, K), jnp.float32) * s, 'conv_bias': jnp.zeros((CONV_DIM,), jnp.float32), 'dt_bias': jnp.ones((H,), jnp.float32), 'A_log': jnp.log(jnp.arange(1, H + 1, dtype=jnp.float32)), 'D': jnp.ones((H,), jnp.float32), 'norm_weight': jnp.ones((I,), jnp.float32), 'out_proj_w': jax.random.normal(ks[3], (D_MODEL, I), jnp.float32) * s}
    _L2_attn_in = _L2_attn_setup()

    def _L2_ffn_setup():
        import jax, jax.numpy as jnp
        import numpy as np
        B, S, IN, MID, OUT = (4, 256, 512, 512, 512)
        key = jax.random.key(seed)
        ks = jax.random.split(key, 7)
        x = jax.random.normal(ks[0], (B, S, IN), dtype=jnp.float32)
        scaling0 = jax.random.uniform(ks[1], (IN,), dtype=jnp.float32)
        scaling2 = jax.random.uniform(ks[2], (MID,), dtype=jnp.float32)
        scaling4 = jax.random.uniform(ks[3], (OUT,), dtype=jnp.float32)
        bias = jax.random.normal(ks[4], (OUT,), dtype=jnp.float32)
        w1_bits = jax.random.randint(ks[5], (MID, IN), 0, 2, dtype=jnp.int32)
        w3_bits = jax.random.randint(ks[6], (OUT, MID), 0, 2, dtype=jnp.int32)
        return {'x': x, 'scaling0': scaling0, 'scaling2': scaling2, 'scaling4': scaling4, 'bias': bias, 'w1_bits': w1_bits, 'w3_bits': w3_bits}
    _L2_ffn_in = _L2_ffn_setup()

    def _L3_attn_setup():
        import jax, jax.numpy as jnp
        import numpy as np
        H = 512
        D = H // 4
        key = jax.random.key(seed)
        k1, k2, k3, k4, k5 = jax.random.split(key, 5)
        x = jax.random.normal(k1, (4, 512, H), dtype=jnp.float32)
        s_in = 1.0 / np.sqrt(H)
        Wqkv = jax.random.normal(k2, (H, 3 * D), dtype=jnp.float32) * s_in
        bqkv = jax.random.normal(k3, (3 * D,), dtype=jnp.float32) * 0.01
        Wo = jax.random.normal(k4, (D, H), dtype=jnp.float32) * (1.0 / np.sqrt(D))
        bo = jax.random.normal(k5, (H,), dtype=jnp.float32) * 0.01
        return {'x': x, 'Wqkv': Wqkv, 'bqkv': bqkv, 'Wo': Wo, 'bo': bo}
    _L3_attn_in = _L3_attn_setup()

    def _L3_ffn_setup():
        import jax, jax.numpy as jnp
        import numpy as np
        HIDDEN = 512
        INTER = 1376
        GROUPSIZE = 128
        PACK = 8

        def dequant_gptq(qweight, scales, zeros, groupsize):
            K = qweight.shape[0] * PACK
            N = qweight.shape[1]
            k = jnp.arange(K)
            q = qweight[k // PACK, :] >> (k % PACK * 4)[:, None] & 15
            n = jnp.arange(N)
            z = zeros[:, n // PACK] >> (n % PACK * 4)[None, :] & 15
            s = scales.astype(jnp.float32)
            zp = (z.astype(jnp.float32) + 1.0) * s
            g = k // groupsize
            return q.astype(jnp.float32) * s[g] - zp[g]
        key = jax.random.key(seed)
        ks = jax.random.split(key, 11)
        imax = 2147483647
        G_h = HIDDEN // GROUPSIZE
        G_i = (INTER + GROUPSIZE - 1) // GROUPSIZE
        x = (jax.random.normal(ks[0], (2, 256, HIDDEN), dtype=jnp.float32) * 0.5).astype(jnp.float16)
        return {'x': x, 'gate_qweight': jax.random.randint(ks[1], (HIDDEN // PACK, INTER), 0, imax, dtype=jnp.int32), 'gate_scales': (jax.random.uniform(ks[2], (G_h, INTER), dtype=jnp.float32) * 0.01 + 0.001).astype(jnp.float16), 'gate_zeros': jax.random.randint(ks[3], (G_h, INTER // PACK), 0, imax, dtype=jnp.int32), 'up_qweight': jax.random.randint(ks[4], (HIDDEN // PACK, INTER), 0, imax, dtype=jnp.int32), 'up_scales': (jax.random.uniform(ks[5], (G_h, INTER), dtype=jnp.float32) * 0.01 + 0.001).astype(jnp.float16), 'up_zeros': jax.random.randint(ks[6], (G_h, INTER // PACK), 0, imax, dtype=jnp.int32), 'down_qweight': jax.random.randint(ks[7], (INTER // PACK, HIDDEN), 0, imax, dtype=jnp.int32), 'down_scales': (jax.random.uniform(ks[8], (G_i, HIDDEN), dtype=jnp.float32) * 0.01 + 0.001).astype(jnp.float16), 'down_zeros': jax.random.randint(ks[9], (G_i, HIDDEN // PACK), 0, imax, dtype=jnp.int32)}
    _L3_ffn_in = _L3_ffn_setup()
    _d = {'L0_attn_x': _L0_attn_in['x'], 'L0_attn_Wq': _L0_attn_in['Wq'], 'L0_attn_bq': _L0_attn_in['bq'], 'L0_attn_Wk': _L0_attn_in['Wk'], 'L0_attn_bk': _L0_attn_in['bk'], 'L0_attn_Wv': _L0_attn_in['Wv'], 'L0_attn_bv': _L0_attn_in['bv'], 'L0_ffn_gate_w': _L0_ffn_in['gate_w'], 'L0_ffn_gate_su': _L0_ffn_in['gate_su'], 'L0_ffn_gate_sv': _L0_ffn_in['gate_sv'], 'L0_ffn_up_w': _L0_ffn_in['up_w'], 'L0_ffn_up_su': _L0_ffn_in['up_su'], 'L0_ffn_up_sv': _L0_ffn_in['up_sv'], 'L0_ffn_down_w': _L0_ffn_in['down_w'], 'L0_ffn_down_su': _L0_ffn_in['down_su'], 'L0_ffn_down_sv': _L0_ffn_in['down_sv'], 'L1_attn_Wqkv': _L1_attn_in['Wqkv'], 'L1_attn_Wo': _L1_attn_in['Wo'], 'L1_ffn_sign': _L1_ffn_in['sign'], 'L1_ffn_scale': _L1_ffn_in['scale'], 'L2_attn_in_proj_w': _L2_attn_in['in_proj_w'], 'L2_attn_conv_weight': _L2_attn_in['conv_weight'], 'L2_attn_conv_bias': _L2_attn_in['conv_bias'], 'L2_attn_dt_bias': _L2_attn_in['dt_bias'], 'L2_attn_A_log': _L2_attn_in['A_log'], 'L2_attn_D': _L2_attn_in['D'], 'L2_attn_norm_weight': _L2_attn_in['norm_weight'], 'L2_attn_out_proj_w': _L2_attn_in['out_proj_w'], 'L2_ffn_scaling0': _L2_ffn_in['scaling0'], 'L2_ffn_scaling2': _L2_ffn_in['scaling2'], 'L2_ffn_scaling4': _L2_ffn_in['scaling4'], 'L2_ffn_bias': _L2_ffn_in['bias'], 'L2_ffn_w1_bits': _L2_ffn_in['w1_bits'], 'L2_ffn_w3_bits': _L2_ffn_in['w3_bits'], 'L3_attn_Wqkv': _L3_attn_in['Wqkv'], 'L3_attn_bqkv': _L3_attn_in['bqkv'], 'L3_attn_Wo': _L3_attn_in['Wo'], 'L3_attn_bo': _L3_attn_in['bo'], 'L3_ffn_gate_qweight': _L3_ffn_in['gate_qweight'], 'L3_ffn_gate_scales': _L3_ffn_in['gate_scales'], 'L3_ffn_gate_zeros': _L3_ffn_in['gate_zeros'], 'L3_ffn_up_qweight': _L3_ffn_in['up_qweight'], 'L3_ffn_up_scales': _L3_ffn_in['up_scales'], 'L3_ffn_up_zeros': _L3_ffn_in['up_zeros'], 'L3_ffn_down_qweight': _L3_ffn_in['down_qweight'], 'L3_ffn_down_scales': _L3_ffn_in['down_scales'], 'L3_ffn_down_zeros': _L3_ffn_in['down_zeros']}
    _x0 = _d['L0_attn_x']
    _d['L0_attn_x'] = jax.random.normal(jax.random.fold_in(jax.random.key(seed), 1), (2, 1024, 512), dtype=_x0.dtype)
    del _x0
    return _d

def reference(L0_attn_x, L0_attn_Wq, L0_attn_bq, L0_attn_Wk, L0_attn_bk, L0_attn_Wv, L0_attn_bv, L0_ffn_gate_w, L0_ffn_gate_su, L0_ffn_gate_sv, L0_ffn_up_w, L0_ffn_up_su, L0_ffn_up_sv, L0_ffn_down_w, L0_ffn_down_su, L0_ffn_down_sv, L1_attn_Wqkv, L1_attn_Wo, L1_ffn_sign, L1_ffn_scale, L2_attn_in_proj_w, L2_attn_conv_weight, L2_attn_conv_bias, L2_attn_dt_bias, L2_attn_A_log, L2_attn_D, L2_attn_norm_weight, L2_attn_out_proj_w, L2_ffn_scaling0, L2_ffn_scaling2, L2_ffn_scaling4, L2_ffn_bias, L2_ffn_w1_bits, L2_ffn_w3_bits, L3_attn_Wqkv, L3_attn_bqkv, L3_attn_Wo, L3_attn_bo, L3_ffn_gate_qweight, L3_ffn_gate_scales, L3_ffn_gate_zeros, L3_ffn_up_qweight, L3_ffn_up_scales, L3_ffn_up_zeros, L3_ffn_down_qweight, L3_ffn_down_scales, L3_ffn_down_zeros):

    def _L0_attn_ref(x, Wq, bq, Wk, bk, Wv, bv):
        import jax, jax.numpy as jnp
        import numpy as np
        EMB_DIM = 512
        N_HEADS = 32
        QKV_DIM = EMB_DIM // N_HEADS
        B, S = (4, 512)
        q = jnp.einsum('bsD,Ddh->bsdh', x, Wq) + bq
        k = (jnp.einsum('bsD,Ddh->bsdh', x, Wk) + bk)[..., 0]
        v = (jnp.einsum('bsD,Ddh->bsdh', x, Wv) + bv)[..., 0]
        qkv_dim = q.shape[-2]
        n_heads = q.shape[-1]
        scale = 1.0 / jnp.sqrt(jnp.asarray(qkv_dim, dtype=q.dtype))
        scores = jnp.einsum('bsdh,bse->bsde', q, k) * scale
        p = jax.nn.softmax(scores, axis=-1)
        o = jnp.einsum('bsde,bse->bsd', p, v)
        out = jnp.broadcast_to(o[..., None], o.shape + (n_heads,))
        return out.reshape(x.shape[:-1] + (qkv_dim * n_heads,))

    def _L0_ffn_ref(x, gate_w, gate_su, gate_sv, up_w, up_su, up_sv, down_w, down_su, down_sv):
        import jax, jax.numpy as jnp
        import numpy as np
        B, S, H, I, R = (4, 32, 512, 1792, 4)

        def _anemll_linear(x, w, su, sv):
            w_eff = w * (su @ sv)
            return jnp.einsum('bsh,oh->bso', x, w_eff)
        a = _anemll_linear(x, gate_w, gate_su, gate_sv)
        b = _anemll_linear(x, up_w, up_su, up_sv)
        d = jax.nn.silu(a) * b
        return _anemll_linear(d, down_w, down_su, down_sv)

    def _L1_attn_ref(hidden_states, Wqkv, Wo):
        import math
        import jax, jax.numpy as jnp
        import numpy as np
        NUM_HEADS = 32
        HIDDEN = 512
        HEAD_DIM = HIDDEN // NUM_HEADS
        NEG_INF = -1e+30

        def _alibi_slopes(n: int) -> jnp.ndarray:
            cp2 = 2 ** math.floor(math.log2(n))
            base = 2.0 ** (-2.0 ** (-(math.log2(cp2) - 3)))
            slopes = base ** np.arange(1, cp2 + 1, dtype=np.float64)
            if cp2 != n:
                extra_base = 2.0 ** (-2.0 ** (-(math.log2(2 * cp2) - 3)))
                rem = min(cp2, n - cp2)
                extra = extra_base ** np.arange(1, 1 + 2 * rem, 2, dtype=np.float64)
                slopes = np.concatenate([slopes, extra])
            return jnp.asarray(slopes, dtype=jnp.float32)
        B, S, H = hidden_states.shape
        nH, d = (NUM_HEADS, HEAD_DIM)
        scale = d ** (-0.5)
        qkv = hidden_states @ Wqkv
        q = qkv[..., :nH * d].reshape(B, S, nH, d)
        k = qkv[..., nH * d:nH * d + d]
        v = qkv[..., nH * d + d:]
        scores = jnp.einsum('bqhd,bkd->bhqk', q, k) * scale
        pos_q = jnp.arange(S)[:, None]
        pos_k = jnp.arange(S)[None, :]
        slopes = _alibi_slopes(nH)
        alibi = slopes[:, None, None] * (pos_k - pos_q).astype(jnp.float32)
        causal = pos_k <= pos_q
        scores = jnp.where(causal[None, None], scores + alibi[None], NEG_INF)
        probs = jax.nn.softmax(scores, axis=-1)
        attn = jnp.einsum('bhqk,bkd->bqhd', probs, v).reshape(B, S, H)
        return attn @ Wo

    def _L1_ffn_ref(x, sign, scale):
        import jax, jax.numpy as jnp
        import numpy as np
        D_IN, D_OUT = (512, 512)
        B, S = (2, 256)
        s = jax.nn.softplus(scale)
        return jnp.einsum('bsi,io->bso', x, sign) * s

    def _L2_attn_ref(hidden_states, in_proj_w, conv_weight, conv_bias, dt_bias, A_log, D, norm_weight, out_proj_w):
        import jax, jax.numpy as jnp
        import numpy as np
        from jax import lax
        H = 64
        P = 64
        N = 128
        G = 8
        K = 4
        D_MODEL = 512
        I = H * P
        GN = G * N
        CONV_DIM = I + 2 * GN
        PROJ = I + CONV_DIM + H
        EPS = 1e-05
        GROUP_SIZE = I // G

        def _reference_tuple_inner(hidden_states, in_proj_w, conv_weight, conv_bias, dt_bias, A_log, D, norm_weight, out_proj_w):
            B, L, _ = hidden_states.shape
            proj = jnp.einsum('bld,pd->blp', hidden_states, in_proj_w)
            gate = proj[..., :I]
            hbc = proj[..., I:I + CONV_DIM]
            dt = proj[..., -H:]
            pad = jnp.pad(hbc, ((0, 0), (K - 1, 0), (0, 0)))
            conv = conv_bias
            for k in range(K):
                conv = conv + pad[:, k:k + L, :] * conv_weight[:, k]
            xBC = jax.nn.silu(conv)
            x = xBC[..., :I].reshape(B, L, H, P)
            Bm = xBC[..., I:I + GN].reshape(B, L, G, N)
            Cm = xBC[..., I + GN:].reshape(B, L, G, N)
            hpg = H // G
            B_h = jnp.repeat(Bm, hpg, axis=2)
            C_h = jnp.repeat(Cm, hpg, axis=2)
            dt_p = jax.nn.softplus(dt + dt_bias)
            A = -jnp.exp(A_log)
            dA = jnp.exp(dt_p * A)
            dtx = dt_p[..., None] * x

            def step(state, inp):
                dA_t, dtx_t, B_t, C_t = inp
                state = state * dA_t[..., None, None] + dtx_t[..., None] * B_t[:, :, None, :]
                y_t = jnp.einsum('bhpn,bhn->bhp', state, C_t)
                return (state, y_t)
            xs = (jnp.moveaxis(dA, 1, 0), jnp.moveaxis(dtx, 1, 0), jnp.moveaxis(B_h, 1, 0), jnp.moveaxis(C_h, 1, 0))
            state0 = jnp.zeros((B, H, P, N), jnp.float32)
            final_state, ys = lax.scan(step, state0, xs)
            y = jnp.moveaxis(ys, 0, 1) + x * D[None, None, :, None]
            y = y.reshape(B, L, I)
            yg = y.reshape(B, L, G, GROUP_SIZE)
            var = jnp.mean(yg * yg, axis=-1, keepdims=True)
            yn = (yg * lax.rsqrt(var + EPS)).reshape(B, L, I) * norm_weight
            yn = yn * jax.nn.silu(gate)
            out = jnp.einsum('bli,di->bld', yn, out_proj_w)
            conv_state_new = jnp.moveaxis(hbc[:, L - (K - 1):, :], 1, 2)
            return (out, conv_state_new, final_state)
        return _reference_tuple_inner(hidden_states, in_proj_w, conv_weight, conv_bias, dt_bias, A_log, D, norm_weight, out_proj_w)[0]

    def _L2_ffn_ref(x, scaling0, scaling2, scaling4, bias, w1_bits, w3_bits):
        import jax, jax.numpy as jnp
        import numpy as np
        B, S, IN, MID, OUT = (4, 256, 512, 512, 512)
        W1 = (2 * w1_bits - 1).astype(x.dtype)
        W3 = (2 * w3_bits - 1).astype(x.dtype)
        h = jnp.einsum('bsi,mi->bsm', x * scaling0, W1)
        h = h * scaling2
        out = jnp.einsum('bsm,om->bso', h, W3)
        out = out * scaling4 + bias
        return out

    def _L3_attn_ref(x, Wqkv, bqkv, Wo, bo):
        import jax, jax.numpy as jnp
        import numpy as np
        H = 512
        D = H // 4
        B, S, C = x.shape
        d = C // 4
        qkv = jnp.einsum('bsc,cf->bsf', x, Wqkv) + bqkv
        qkv = qkv.reshape(B, S, 3, d)
        q, k, v = (qkv[:, :, 0], qkv[:, :, 1], qkv[:, :, 2])
        scale = 1.0 / jnp.sqrt(jnp.float32(d)).astype(x.dtype)
        attn = jnp.einsum('bqd,bkd->bqk', q, k) * scale
        attn = jax.nn.softmax(attn, axis=-1)
        out = jnp.einsum('bqk,bkd->bqd', attn, v)
        return jnp.einsum('bqd,dc->bqc', out, Wo) + bo

    def _L3_ffn_ref(x, gate_qweight, gate_scales, gate_zeros, up_qweight, up_scales, up_zeros, down_qweight, down_scales, down_zeros):
        import jax, jax.numpy as jnp
        import numpy as np
        HIDDEN = 512
        INTER = 1376
        GROUPSIZE = 128
        PACK = 8

        def dequant_gptq(qweight, scales, zeros, groupsize):
            K = qweight.shape[0] * PACK
            N = qweight.shape[1]
            k = jnp.arange(K)
            q = qweight[k // PACK, :] >> (k % PACK * 4)[:, None] & 15
            n = jnp.arange(N)
            z = zeros[:, n // PACK] >> (n % PACK * 4)[None, :] & 15
            s = scales.astype(jnp.float32)
            zp = (z.astype(jnp.float32) + 1.0) * s
            g = k // groupsize
            return q.astype(jnp.float32) * s[g] - zp[g]
        B, S, H = x.shape
        x2 = x.reshape(-1, H).astype(jnp.float32)
        Wg = dequant_gptq(gate_qweight, gate_scales, gate_zeros, GROUPSIZE)
        Wu = dequant_gptq(up_qweight, up_scales, up_zeros, GROUPSIZE)
        Wd = dequant_gptq(down_qweight, down_scales, down_zeros, GROUPSIZE)
        gate = x2 @ Wg
        up = x2 @ Wu
        inter = gate * jax.nn.sigmoid(gate) * up
        out = (inter @ Wd).astype(jnp.float16)
        return out.reshape(B, S, H)
    x = L0_attn_x
    x = x + _layernorm(_L0_attn_ref(_layernorm(x, axis=-1), L0_attn_Wq, L0_attn_bq, L0_attn_Wk, L0_attn_bk, L0_attn_Wv, L0_attn_bv), axis=-1)
    x = x + _layernorm(_L0_ffn_ref(_layernorm(x, axis=-1), L0_ffn_gate_w, L0_ffn_gate_su, L0_ffn_gate_sv, L0_ffn_up_w, L0_ffn_up_su, L0_ffn_up_sv, L0_ffn_down_w, L0_ffn_down_su, L0_ffn_down_sv), axis=-1)
    x = x + _layernorm(_L1_attn_ref(_layernorm(x, axis=-1), L1_attn_Wqkv, L1_attn_Wo), axis=-1)
    x = x + _layernorm(_L1_ffn_ref(_layernorm(x, axis=-1), L1_ffn_sign, L1_ffn_scale), axis=-1)
    x = x + _layernorm(_L2_attn_ref(_layernorm(x, axis=-1), L2_attn_in_proj_w, L2_attn_conv_weight, L2_attn_conv_bias, L2_attn_dt_bias, L2_attn_A_log, L2_attn_D, L2_attn_norm_weight, L2_attn_out_proj_w), axis=-1)
    x = x + _layernorm(_L2_ffn_ref(_layernorm(x, axis=-1), L2_ffn_scaling0, L2_ffn_scaling2, L2_ffn_scaling4, L2_ffn_bias, L2_ffn_w1_bits, L2_ffn_w3_bits), axis=-1)
    x = x + _layernorm(_L3_attn_ref(_layernorm(x, axis=-1), L3_attn_Wqkv, L3_attn_bqkv, L3_attn_Wo, L3_attn_bo), axis=-1)
    x = x + _layernorm(_L3_ffn_ref(_layernorm(x, axis=-1), L3_ffn_gate_qweight, L3_ffn_gate_scales, L3_ffn_gate_zeros, L3_ffn_up_qweight, L3_ffn_up_scales, L3_ffn_up_zeros, L3_ffn_down_qweight, L3_ffn_down_scales, L3_ffn_down_zeros), axis=-1)
    return x

_drawn_inputs = setup_inputs


def setup_inputs(seed=0):
    import zlib

    import numpy as np

    out = dict(_drawn_inputs(seed))
    spreads = {'L0_attn_bq': (0.0, 0.1),
     'L0_attn_bk': (0.0, 0.1),
     'L0_attn_bv': (0.0, 0.1),
     'L2_attn_conv_bias': (0.0, 0.1),
     'L2_attn_dt_bias': (1.0, 0.6),
     'L2_attn_D': (1.0, 0.2),
     'L2_attn_norm_weight': (1.0, 0.2)}
    factors = {'L2_attn_A_log': 8.0, 'L2_ffn_bias': 7.081, 'L3_attn_bqkv': 3.113, 'L3_attn_bo': 3.487}
    for name, (base, spread) in spreads.items():
        noise = np.random.default_rng([zlib.crc32(name.encode()), seed]).standard_normal(out[name].shape)
        drawn = base * np.exp(spread * noise) if base else spread * noise
        out[name] = jnp.asarray(drawn.astype(out[name].dtype))
    for name, factor in factors.items():
        out[name] = (out[name] * factor).astype(out[name].dtype)
    return out
```

```python
from contextlib import ExitStack, contextmanager

import numpy as np

import concourse.bass as bass
from concourse import mybir

F32 = mybir.dt.float32
F16 = mybir.dt.float16
I32 = mybir.dt.int32
ALU = mybir.AluOpType
ACT = mybir.ActivationFunctionType
AXX = mybir.AxisListType.X
ds = bass.ds

P = 128
TOK = 2048
NT = TOK // P
NB = 2
TPB = NT // NB
NG = 4
GT = NT // NG
GW = GT * P
C = 512
KT = C // P
EPS = 1e-5
WS = 64.0
ACTS = 64.0

H0, D0 = 32, 16
F0 = 1792 // P
RANK = 4


class Tally:

    def __init__(self, base=0):
        self.base, self.off = base, 0

    def add(self, n=1):
        self.off += n

    def __call__(self, more=0):
        return self.base + (self.off + more)


class Chain(Tally):

    def __init__(self, eng, sem):
        super().__init__()
        self.eng, self.sem = eng, sem

    def mark(self, ins):
        ins.then_inc(self.sem, 1)
        self.add()
        return self()

    def wait(self, value):
        self.eng.wait_ge(self.sem, value)

    def link(self, ins, alone=None):
        self.wait(self.mark(ins))
        if alone:
            alone(self.eng)


@contextmanager
def loop(eng, n, *tallies):
    outside = [(t.base, t.off) for t, _ in tallies]
    with eng.Fori(0, n) as i:
        for (t, per), (base, off) in zip(tallies, outside):
            t.base, t.off = i * per + base + off if per else base + off, 0
        yield i
        for t, per in tallies:
            assert t.off == per, (t.off, per)
    for (t, per), (base, off) in zip(tallies, outside):
        t.base, t.off = base, off + n * per


def build(nc, A, start=0, stop=8):
    yb = 1 if start == 0 else 0
    ctx = ExitStack()
    with ctx:
        def sb(name, shape, dt):
            return ctx.enter_context(nc.sbuf_tensor(name, shape, dt))

        def sem(name):
            return ctx.enter_context(nc.semaphore(name))

        x = sb("x", [P, NT, C], F32)
        xt_hi = sb("xt_hi", [P, KT, TOK], F16)
        xt_lo = sb("xt_lo", [P, KT, TOK], F16)
        ident = sb("ident", [P, P], F32)
        tmp = sb("tmp", [P, 2, C], F32)
        xn = sb("xn", [P, 2, C], F32)
        st6 = sb("st6", [P, 2, 2, 6], F32)
        mv = sb("mv", [P, 2, 2, 2], F32)
        rs = sb("rs", [P, 2, 2, 2], F32)
        sd = sb("sd", [P, 2, 2], F32)
        epsc = sb("epsc", [P, 8], F32)
        arena = sb("arena", [P, 34213], F32)

        def carve(at, shape, dt):
            n = int(np.prod(shape))
            words = n if dt in (F32, I32) else n // 2
            v = arena[:, at // 4:at // 4 + words]
            if dt is not F32:
                v = v.bitcast(dt)
            if len(shape) > 1:
                names = "abcd"[:len(shape)]
                v = v.rearrange(f"p ({' '.join(names)}) -> p {' '.join(names)}",
                                **{k: s for k, s in zip(names[1:], shape[1:])})
            return v

        psum = ctx.enter_context(nc.psum_tensor("psum", [P, 8, 512], F32))
        ps_g = psum[:, 0:4, :]
        ps_y = psum[:, 4:6, :]
        ps_t = psum[:, 6, :].rearrange("p (k c) -> p k c", k=4)
        ps_m = psum[:, 7, :]

        act_seq, dve_seq, pool_seq = sem("act_seq"), sem("dve_seq"), sem("pool_seq")

        y_ready = sem("y_ready")
        y_mv = sem("y_mv")
        y_sd = sem("y_sd")
        y_rs = sem("y_rs")
        y_norm = sem("y_norm")
        x_new = sem("x_new")
        x_mv = sem("x_mv")
        x_sd = sem("x_sd")
        x_rs = sem("x_rs")
        x_norm = sem("x_norm")
        x_tr = sem("x_tr")
        xt_h = sem("xt_h")
        xt_ok = sem("xt_ok")

        x_in = [sem(f"x_in{q}") for q in range(4)]
        x_out = sem("x_out")
        consts_ok = sem("consts_ok")
        passed = sem("passed")

        def alone(eng):
            eng.sem_inc(passed, 1)

        class Tail:

            @staticmethod
            def dve_y(dve, ch, r, t, j, y):
                q = j % 2
                dve.wait_ge(y_ready, r + 1)
                ch.link(nc.vector.bn_stats(st6[:, 0, q, :], y), alone)
                nc.vector.bn_aggr(mv[:, 0, q, :], st6[:, 0, q, :]).then_inc(y_mv, 1)
                dve.wait_ge(y_sd, r + 1)
                ch.link(nc.vector.reciprocal(rs[:, 0, q, 0:1], sd[:, 0, q:q + 1]))
                nc.vector.tensor_scalar(rs[:, 0, q, 1:2], mv[:, 0, q, 0:1], -1.0, rs[:, 0, q, 0:1],
                                        ALU.mult, ALU.mult).then_inc(y_rs, 1)
                dve.wait_ge(y_norm, r + 1)
                nc.vector.tensor_tensor(x[:, t, :], x[:, t, :], tmp[:, q, :], ALU.add).then_inc(x_new, 1)

            @staticmethod
            def act_y(act, r, j, y, eps):
                q = j % 2
                act.wait_ge(y_mv, r + 1)
                nc.scalar.activation(sd[:, 0, q:q + 1], mv[:, 0, q, 1:2], ACT.Sqrt, bias=eps).then_inc(y_sd, 1)
                act.wait_ge(y_rs, r + 1)
                nc.scalar.activation(tmp[:, q, :], y, ACT.Identity, bias=rs[:, 0, q, 1:2],
                                     scale=rs[:, 0, q, 0:1]).then_inc(y_norm, 1)

            @staticmethod
            def dve_x(dve, ch, r, n, t, j):
                q = j % 2
                if r is not None:
                    dve.wait_ge(x_new, r + 1)
                    alone(dve)
                ch.link(nc.vector.bn_stats(st6[:, 1, q, :], x[:, t, :]), alone)
                nc.vector.bn_aggr(mv[:, 1, q, :], st6[:, 1, q, :]).then_inc(x_mv, 1)
                dve.wait_ge(x_sd, n + 1)
                ch.link(nc.vector.reciprocal(rs[:, 1, q, 0:1], sd[:, 1, q:q + 1]))
                nc.vector.tensor_scalar(rs[:, 1, q, 1:2], mv[:, 1, q, 0:1], -1.0, rs[:, 1, q, 0:1],
                                        ALU.mult, ALU.mult).then_inc(x_rs, 1)

            @staticmethod
            def act_x(act, n, t, j):
                q = j % 2
                act.wait_ge(x_mv, n + 1)
                nc.scalar.activation(sd[:, 1, q:q + 1], mv[:, 1, q, 1:2], ACT.Sqrt, bias=epsc[:, 0:1]).then_inc(x_sd, 1)
                act.wait_ge(x_rs, n + 1)
                nc.scalar.activation(xn[:, q, :], x[:, t, :], ACT.Identity, bias=rs[:, 1, q, 1:2],
                                     scale=rs[:, 1, q, 0:1]).then_inc(x_norm, 1)

            @staticmethod
            def pe_x(pe, n, j, first=False):
                pe.wait_ge(x_norm, n + 1)
                if not first:
                    pe.wait_ge(xt_ok, n)
                for k in range(KT):
                    last = nc.tensor.transpose(ps_t[:, k, :], xn[:, j % 2, k * P:(k + 1) * P], ident[:, :])
                last.then_inc(x_tr, 1)

            @staticmethod
            def act_hi(act, n, t):
                act.wait_ge(x_tr, n + 1)
                nc.scalar.activation(xt_hi[:, :, ds(t * P, P)], ps_t[:, :, :], ACT.Copy).then_inc(xt_h, 1)

            @staticmethod
            def dve_lo(dve, n, t):
                dve.wait_ge(xt_h, n + 1)
                nc.vector.tensor_tensor(xt_lo[:, :, ds(t * P, P)], ps_t[:, :, :], xt_hi[:, :, ds(t * P, P)],
                                        ALU.subtract).then_inc(xt_ok, 1)

        def y_psum(j):
            return ps_y[:, j % 2, :]

        def dve_group(dve, ch, s, g, y=y_psum, last_layer=False, before=None):
            for j in range(GT):
                if before:
                    before(j)
                i = g * GT + j
                Tail.dve_y(dve, ch, i + NT * (s - yb), i, j, y(j))
                if not last_layer:
                    Tail.dve_x(dve, ch, i + NT * (s - yb), i + NT * (s + 1), i, j)
                    if j:
                        Tail.dve_lo(dve, i + (NT * (s + 1) - 1), i - 1)
            if not last_layer:
                Tail.dve_lo(dve, i + NT * (s + 1), i)

        def act_group(act, s, g, eps, y=y_psum, last_layer=False, before=None):
            for j in range(GT):
                if before:
                    before(j)
                i = g * GT + j
                Tail.act_y(act, i + NT * (s - yb), j, y(j), eps)
                if not last_layer:
                    Tail.act_x(act, i + NT * (s + 1), i, j)
                    if j:
                        Tail.act_hi(act, i + (NT * (s + 1) - 1), i - 1)
            if not last_layer:
                Tail.act_hi(act, i + NT * (s + 1), i)

        def pe_group(pe, s, g, y_tile, last_layer=False):
            for j in range(GT):
                y_tile(j)
                if j and not last_layer:
                    Tail.pe_x(pe, g * GT + (NT * (s + 1) + j - 1), j - 1)
            if not last_layer:
                Tail.pe_x(pe, g * GT + (NT * (s + 1) + GT - 1), GT - 1)

        def three(pe, out, lh, ll, rh, rl, start, stop):
            nc.tensor.matmul(out, lh, rh, start=start, stop=False)
            nc.tensor.matmul(out, lh, rl, start=False, stop=False)
            return nc.tensor.matmul(out, ll, rh, start=False, stop=stop)

        QKV0 = 3 * D0
        A0 = 86016
        w0q = carve(A0, [KT, D0, H0], F32)
        w0 = carve(A0 + 8192, [KT, QKV0], F32)
        b0q = carve(A0 + 8960, [D0, H0], F32)
        b0 = carve(A0 + 11008, [QKV0], F32)
        qkv0 = carve(A0 + 11264, [GT, QKV0], F32)
        lg0 = carve(A0 + 12032, [GT, D0, D0], F32)
        pv0 = carve(A0 + 16128, [GT, D0, D0], F32)
        mx0 = carve(A0 + 20224, [GT, D0], F32)
        sm0 = carve(A0 + 20480, [GT, D0], F32)
        o0 = carve(A0 + 20736, [GT, D0], F32)
        sc0 = carve(A0 + 20992, [4, GT], F32)
        sq0 = carve(A0 + 21248, [GT, D0], F32)
        xt32 = carve(A0 + 21504, [KT, P], F32)
        a0_in = sem("a0_in")
        a0_w = sem("a0_w")
        a0_qkv = sem("a0_qkv")
        a0_lg = sem("a0_lg")
        a0_ex = sem("a0_ex")
        a0_var = sem("a0_var")
        a0_sd = sem("a0_sd")
        a0_wh = sem("a0_wh")
        x_sd0 = sem("a0_x")
        w0h = carve(A0 + 23552, [KT, QKV0], F16)
        w0l = carve(A0 + 23552 + 384, [KT, QKV0], F16)

        FW = F0 * P
        gh = carve(0, [KT, FW], F16)
        gl = carve(14336, [KT, FW], F16)
        uh = carve(2 * 14336, [KT, FW], F16)
        ul = carve(3 * 14336, [KT, FW], F16)
        dh = carve(4 * 14336, [F0, C], F16)
        dl = carve(5 * 14336, [F0, C], F16)
        hid_h = carve(86016, [F0, GW], F16)
        hid_l = carve(86016 + 14336, [F0, GW], F16)
        SCR = 114688
        sg1 = carve(SCR, [2, GW], F32)
        hd1 = carve(SCR + 4096, [2, GW], F32)
        raw1 = carve(SCR + 8192, [2, C], F32)
        we1 = carve(SCR + 12288, [2, C], F32)
        suT = carve(SCR, [FW], F32)
        svT = carve(SCR + 16384, [C], F32)
        QW = FW // 4
        chunks = []
        for m, (h_, l_) in enumerate(((gh, gl), (uh, ul))):
            for k in range(KT):
                for c in range(4):
                    chunks.append((m, k, slice(c * QW, (c + 1) * QW), h_[:, k, c * QW:(c + 1) * QW],
                                   l_[:, k, c * QW:(c + 1) * QW]))
        for f in range(F0):
            chunks.append((2, f, slice(0, C), dh[:, f, :], dl[:, f, :]))
        first_of = {0: 0, 1: 16, 2: 32}
        w1_raw = [sem("w1_raw0"), sem("w1_raw1")]
        w1_fac = sem("w1_fac")
        w1_ps = sem("w1_ps")
        w1_eff = sem("w1_eff")
        w1_hi = sem("w1_hi")
        w1_lo = sem("w1_lo")
        gate_ready = sem("gate_ready")
        up_ready = sem("up_ready")
        silu_ok = sem("silu_ok")
        hid_ok = sem("hid_ok")
        hid_hi = sem("hid_hi")
        hid_lo = sem("hid_lo")

        def pe_ffn(pe, s, F, gh, gl, uh, ul, dh, dl, hh, hl, w_ok, n_w, base, done=None, last_layer=False):
            pe.wait_ge(w_ok, n_w)
            with pe.Fori(0, NG) as g:
                pe.wait_ge(xt_ok, g * GT + (NT * s + GT))
                cols = ds(g * GW, GW)
                for f in range(F):
                    i = g * F + (base + f)
                    b = 2 * (f % 2)
                    if f >= 2:
                        pe.wait_ge(hid_ok, i - 1)
                    fc = slice(f * P, (f + 1) * P)
                    for k in range(KT):
                        last = three(pe, ps_g[:, b, :], gh[:, k, fc], gl[:, k, fc], xt_hi[:, k, cols],
                                     xt_lo[:, k, cols], k == 0, k == KT - 1)
                    last.then_inc(gate_ready, 1)
                    for k in range(KT):
                        last = three(pe, ps_g[:, b + 1, :], uh[:, k, fc], ul[:, k, fc], xt_hi[:, k, cols],
                                     xt_lo[:, k, cols], k == 0, k == KT - 1)
                    last.then_inc(up_ready, 1)

                def y_tile(j):
                    r = g * GT + (NT * (s - yb) + j)
                    if j >= 2:
                        pe.wait_ge(y_norm, r - 1)
                    tok = slice(j * P, (j + 1) * P)
                    for f in range(F):
                        if j == 0:
                            pe.wait_ge(hid_lo, g * F + (base + f + 1))
                        last = three(pe, ps_y[:, j % 2, :], hh[:, f, tok], hl[:, f, tok], dh[:, f, :], dl[:, f, :],
                                     f == 0, f == F - 1)
                    last.then_inc(done or y_ready, 1)
                pe_group(pe, s, g, y_tile, last_layer)

        def act_ffn(act, s, F, hh, base, eps, sg, hd, y=y_psum, last_layer=False, before=None):
            with act.Fori(0, NG) as g:
                for f in range(F):
                    i = g * F + (base + f)
                    b = 2 * (f % 2)
                    act.wait_ge(gate_ready, i + 1)
                    if f >= 2:
                        act.wait_ge(hid_ok, i - 1)
                    nc.scalar.activation(sg[:, f % 2, :], ps_g[:, b, :], ACT.Silu, scale=1.0 / WS).then_inc(silu_ok, 1)
                    if f:
                        act.wait_ge(hid_ok, i)
                        nc.scalar.activation(hh[:, f - 1, :], hd[:, (f - 1) % 2, :], ACT.Copy).then_inc(hid_hi, 1)
                act.wait_ge(hid_ok, g * F + (base + F))
                nc.scalar.activation(hh[:, F - 1, :], hd[:, (F - 1) % 2, :], ACT.Copy).then_inc(hid_hi, 1)
                act_group(act, s, g, eps, y, last_layer, before(g) if before else None)

        def dve_ffn(dve, ch, s, F, hh, hl, base, sg, hd, y=y_psum, last_layer=False):
            with loop(dve, NG, (ch, 2 * GT if last_layer else 4 * GT)) as g:
                for f in range(F):
                    i = g * F + (base + f)
                    b = 2 * (f % 2)
                    dve.wait_ge(up_ready, i + 1)
                    dve.wait_ge(silu_ok, i + 1)
                    if f >= 2:
                        dve.wait_ge(hid_lo, i - 1)
                    nc.vector.scalar_tensor_tensor(out=hd[:, f % 2, :], in0=ps_g[:, b + 1, :], scalar=ACTS / WS,
                                                   in1=sg[:, f % 2, :], op0=ALU.mult, op1=ALU.mult).then_inc(hid_ok, 1)
                    if f:
                        dve.wait_ge(hid_hi, i)
                        nc.vector.tensor_tensor(hl[:, f - 1, :], hd[:, (f - 1) % 2, :], hh[:, f - 1, :],
                                                ALU.subtract).then_inc(hid_lo, 1)
                dve.wait_ge(hid_hi, g * F + (base + F))
                nc.vector.tensor_tensor(hl[:, F - 1, :], hd[:, (F - 1) % 2, :], hh[:, F - 1, :],
                                        ALU.subtract).then_inc(hid_lo, 1)
                dve_group(dve, ch, s, g, y, last_layer)

        H2, D2 = 32, 16
        QR = 4 * D2
        a2_qs = carve(0, [H2, TPB * P], F16)
        a2_p = carve(65536, [8, 4 * P], F32)
        a2_wh = carve(81920, [KT, 544], F16)
        a2_wl = carve(86272, [KT, 544], F16)
        a2_oh = carve(90624, [KT, C], F16)
        a2_ol = carve(94720, [KT, C], F16)
        a2_qh = carve(98816, [KT, GW], F16)
        a2_ql = carve(102912, [KT, GW], F16)
        a2_ks = carve(107008, [TPB * P], F16)
        a2_kh = carve(109056, [TPB * P], F16)
        a2_kl = carve(111104, [TPB * P], F16)
        a2_v = carve(113152, [TPB, D2 + 1], F32)
        a2_ar = carve(113696, [H2, D2], F32)
        a2_ah = carve(115744, [KT, P], F16)
        a2_al = carve(116768, [KT, P], F16)
        a2_mx = carve(117792, [H2], F32)
        a2_mt = carve(117920, [P], F16)
        a2_rd = carve(118176, [H2], F32)
        a2_id = carve(118304, [P], F16)
        a2_mqk = carve(118560, [P], F16)
        a2_mkq = carve(118816, [P], F16)
        a2_raw = carve(119072, [KT, 544], F32)
        a2_rwo = carve(65536, [KT, C], F32)
        a2_in = sem("a2_in")
        a2_wo = sem("a2_wo")
        a2_whi = sem("a2_whi")
        a2_wlo = sem("a2_wlo")
        a2_kp = sem("a2_kp")
        a2_khi = sem("a2_khi")
        a2_klo = sem("a2_klo")
        a2_vp = sem("a2_vp")
        a2_vok = sem("a2_vok")
        a2_qp = sem("a2_qp")
        a2_qhi = sem("a2_qhi")
        a2_qlo = sem("a2_qlo")
        a2_dma = sem("a2_dma")
        a2_ms = sem("a2_ms")
        a2_md = sem("a2_md")
        a2_mt_p = sem("a2_mt_p")
        a2_mt_a = sem("a2_mt_a")
        a2_mrow = sem("a2_mrow")
        a2_s = sem("a2_s")
        a2_e = sem("a2_e")
        a2_pv = sem("a2_pv")
        a2_o = sem("a2_o")
        a2_tr = sem("a2_tr")
        a2_thi = sem("a2_thi")
        a2_tlo = sem("a2_tlo")
        QDMA = 2 * 32 + 4

        def max_units(t):
            return [[2 * u, 2 * u + 1] for u in range(4)] if t < 4 else [[u] for u in range(8)]

        s3_raw = carve(0, [KT, C], F32)
        s3_h = carve(8192, [KT, C], F16)
        s3_l = carve(12288, [KT, C], F16)
        s3_s = carve(16384, [8], F32)
        s3_in = sem("s3_in")
        s3_scale = sem("s3_scale")
        s3_hi = sem("s3_hi")
        s3_lo = sem("s3_lo")
        s3_sp = sem("s3_sp")
        s3_eps = sem("s3_eps")

        HS, PS, GS, KC = 64, 64, 8, 4
        HG = HS // GS
        GF = HG * PS
        IW = 2 * GF + 2 * P
        FT = IW // P
        CT = FT - GF // P
        SW = IW // 2
        m4_acc = carve(0, [NT, C], F32)
        m4_wh = carve(32768, [KT, IW + C], F16)
        m4_wl = carve(47104, [KT, IW + C], F16)
        m4_raw = carve(61440, [2, SW], F32)
        m4_hb = carve(66560, [CT, GW + KC - 1], F32)
        m4_xc = carve(78920, [CT, GW], F32)
        m4_sg = carve(91208, [4, GW], F32)
        m4_st = carve(99400, [GF], F32)
        m4_dtp = carve(101448, [NT * HS], F32)
        m4_dt2 = carve(105544, [NT * HS], F32)
        m4_ah = carve(109640, [NT * HS], F16)
        m4_al = carve(111688, [NT * HS], F16)
        m4_ar = carve(113736, [2, HG, P], F16)
        m4_ab = carve(117832, [2, GF], F16)
        m4_e1 = carve(119880, [HG, P], F32)
        m4_de = carve(123976, [2, 4, P], F32)
        m4_ty = carve(128072, [4, P], F32)
        m4_sq = carve(130120, [4, P], F32)
        m4_yh = carve(132168, [4, P], F16)
        m4_yl = carve(133192, [4, P], F16)
        m4_bt = carve(134216, [P], F32)
        m4_gm = carve(134728, [P], F32)
        m4_le = carve(135240, [P], F16)
        m4_gt = carve(135496, [P], F16)
        m4_on = carve(135752, [P], F16)
        m4_par = carve(136008, [CT * (KC + 1) + 8], F32)
        m4_nw = carve(136160, [4], F32)
        m4_dg = carve(136176, [NT * HG], F32)
        m4_pn = carve(136688, [CT * (KC + 1) + 8], F32)
        m4_sd = carve(136840, [1], F32)
        m4_rs = carve(136844, [1], F32)
        m4_o32 = carve(136848, [1], F32)
        m4_x12 = tmp.rearrange("p a c -> p (a c)")
        m4_e0 = xn.rearrange("p a (h t) -> p (a h) t", t=P)
        m4_e = [m4_e0, m4_e1]
        m4_u = carve(119880, [8 * HS], F32)
        m4_v = carve(121928, [8 * HS], F32)
        m4_db = carve(128072, [HS], F32)
        m4_na = carve(128328, [HS], F32)
        m4_dr = carve(130120, [KT, HS], F32)
        m4_dh = carve(131144, [KT, HS], F16)
        m4_dl = carve(131656, [KT, HS], F16)
        m4_cin = sem("m4_cin")
        m4_dw = sem("m4_dw")
        m4_dp = sem("m4_dp")
        m4_tv = sem("m4_tv")
        m4_ta = sem("m4_ta")
        m4_dq = sem("m4_dq")
        m4_ri = [sem("m4_ri0"), sem("m4_ri1")]
        m4_pi = sem("m4_pi")
        m4_nwk = sem("m4_nwk")
        m4_whi = sem("m4_whi")
        m4_wlo = sem("m4_wlo")
        m4_ip = sem("m4_ip")
        m4_hbk = sem("m4_hbk")
        m4_gk = sem("m4_gk")
        m4_cy = sem("m4_cy")
        m4_cv = sem("m4_cv")
        m4_xk = sem("m4_xk")
        m4_ak = sem("m4_ak")
        m4_gp = sem("m4_gp")
        m4_sp = sem("m4_sp")
        m4_dd = sem("m4_dd")
        m4_gd = sem("m4_gd")
        m4_ek = sem("m4_ek")
        m4_dk = sem("m4_dk")
        m4_mk = sem("m4_mk")
        m4_xp = sem("m4_xp")
        m4_bk = sem("m4_bk")
        m4_x2 = sem("m4_x2")
        m4_ii = sem("m4_ii")
        m4_ia = sem("m4_ia")
        m4_sn = sem("m4_sn")
        m4_sk = sem("m4_sk")
        m4_tk = sem("m4_tk")
        m4_yk = sem("m4_yk")
        m4_yn = sem("m4_yn")
        m4_yhi = sem("m4_yhi")
        m4_ylo = sem("m4_ylo")
        m4_qk = sem("m4_qk")
        m4_qp = sem("m4_qp")
        m4_sdk = sem("m4_sdk")
        m4_rk = sem("m4_rk")
        m4_op = sem("m4_op")
        m4_ok = sem("m4_ok")

        s5_raw = carve(0, [2, KT, C], I32)
        s5_w1 = carve(16384, [KT, C], F32)
        s5_w1h = carve(24576, [KT, C], F16)
        s5_w1l = carve(28672, [KT, C], F16)
        s5_w3 = carve(32768, [KT, C], F16)
        s5_s0 = carve(36864, [KT], F32)
        s5_s2 = carve(36880, [KT], F32)
        s5_s4 = carve(36896, [C], F32)
        s5_b = carve(36896 + 2048, [C], F32)
        s5_y = carve(40992, [2, C], F32)
        s5_hh = carve(45088, [KT, GW], F16)
        s5_hl = carve(49184, [KT, GW], F16)
        s5_in = sem("s5_in")
        s5_wf = sem("s5_wf")
        s5_hi = sem("s5_hi")
        s5_w = sem("s5_w")
        s5_h = sem("s5_h")
        s5_hhi = sem("s5_hhi")
        s5_hlo = sem("s5_hlo")
        s5_p = sem("s5_p")

        INTER = 1376
        F3 = -(-INTER // P)
        FW3 = F3 * P
        A7 = 0
        g7h = carve(A7, [KT, FW3], F16)
        g7l = carve(A7 + 11264, [KT, FW3], F16)
        u7h = carve(A7 + 2 * 11264, [KT, FW3], F16)
        u7l = carve(A7 + 3 * 11264, [KT, FW3], F16)
        d7h = carve(A7 + 4 * 11264, [F3, C], F16)
        d7l = carve(A7 + 5 * 11264, [F3, C], F16)
        hid7h = carve(67584, [F3, GW], F16)
        hid7l = carve(67584 + 11264, [F3, GW], F16)
        sg7 = carve(90112, [2, GW], F32)
        hd7 = carve(94208, [2, GW], F32)
        y7 = carve(98304, [2, C], F16)
        q7 = carve(100352, [2, INTER], I32)
        w7 = carve(100352 + 11008, [INTER], F32)
        z7p = carve(116864, [172], I32)
        z7 = carve(116864 + 688, [172, 8], I32)
        s7 = carve(123056, [INTER], F16)
        sh7 = carve(125808, [1], I32)
        q7_in = [sem("q7_in0"), sem("q7_in1")]
        z7_in = sem("z7_in")
        sh7_in = sem("sh7_in")
        q7_done = sem("q7_done")
        w7_f = sem("w7_f")
        w7_h = sem("w7_h")
        w7_l = sem("w7_l")
        p7_y = sem("p7_y")
        mats7 = [("gate", g7h, g7l, INTER), ("up", u7h, u7l, INTER), ("down", d7h, d7l, C)]
        pieces7 = [(m, k, 16) for m in range(2) for k in range(KT)] + \
                  [(2, k, 16 if k < F3 - 1 else (INTER - (F3 - 1) * P) // 8) for k in range(F3)]

        D3 = C // 4
        S6 = TPB * P
        a6_raw = carve(0, [KT, 3 * D3], F32)
        a6_rwo = carve(6144, [C], F32)
        a6_wh = carve(8192, [KT, 3 * D3], F16)
        a6_wl = carve(11264, [KT, 3 * D3], F16)
        a6_oh = carve(14336, [C], F16)
        a6_ol = carve(15360, [C], F16)
        a6_b = carve(16384, [2], F32)
        a6_bv = carve(16400, [D3], F32)
        a6_bo = carve(16912, [C], F32)
        a6_qk = carve(18960, [2, GW], F32)
        a6_qh = carve(23056, [2, TOK], F16)
        a6_ql = carve(31248, [2, TOK], F16)
        a6_v = carve(39440, [GT, D3], F32)
        a6_vh = carve(41488, [NT, D3], F16)
        a6_vl = carve(45584, [NT, D3], F16)
        a6_mx = carve(49680, [2, 4], F32)
        a6_p = carve(49712, [2, S6], F32)
        a6_ph = carve(57904, [TPB, P], F16)
        a6_pl = carve(59952, [TPB, P], F16)
        a6_th = carve(62000, [P], F16)
        a6_tl = carve(62256, [P], F16)
        a6_y = carve(62512, [2, C], F32)
        a6_in = sem("a6_in")
        a6_wok = sem("a6_wok")
        a6_who = sem("a6_who")
        a6_pp = sem("a6_pp")
        a6_pf = sem("a6_pf")
        a6_pho = sem("a6_pho")
        a6_plo = sem("a6_plo")
        a6_s = sem("a6_s")
        a6_m = sem("a6_m")
        a6_e = sem("a6_e")
        a6_t = sem("a6_t")
        a6_tho = sem("a6_tho")
        a6_tlo = sem("a6_tlo")
        a6_o = sem("a6_o")
        a6_oho = sem("a6_oho")
        a6_olo = sem("a6_olo")
        a6_yp = sem("a6_yp")
        a6_inv = sem("a6_inv")
        SC6 = float(np.float32(1.0) / np.sqrt(np.float32(D3)))

        def arena_free(eng, layer):
            if layer > start:
                if layer == 1:
                    eng.wait_ge(xt_ok, 2 * NT)
                else:
                    eng.wait_ge(y_ready, NT * (layer - start - yb))

        def on(layer):
            return start <= layer < stop

        def sp_x(sp):
            xin = A["L0_attn_x"].rearrange("b (t p) c -> p (b t) c", p=P)
            for q in range(4):
                sp.dma_start(x[:, q * 4:(q + 1) * 4, :], xin[:, q * 4:(q + 1) * 4, :]).then_inc(x_in[q], 16)

        def sp_l0_attn(sp):
            sp.dma_start(w0q, A["L0_attn_Wq"].rearrange("(k p) d h -> p k d h", p=P)).then_inc(a0_in, 16)
            sp.dma_start(w0[:, :, D0:2 * D0], A["L0_attn_Wk"].rearrange("(k p) d h -> p k (d h)", p=P)).then_inc(a0_in, 16)
            sp.dma_start(w0[:, :, 2 * D0:], A["L0_attn_Wv"].rearrange("(k p) d h -> p k (d h)", p=P)).then_inc(a0_in, 16)
            row = lambda n, w: A[n].rearrange("a b -> (a b)").rearrange("(o n) -> o n", o=1).broadcast_to([P, w])
            sp.dma_start(b0q.rearrange("p d h -> p (d h)"), row("L0_attn_bq", C)).then_inc(a0_in, 16)
            sp.dma_start(b0[:, D0:2 * D0], row("L0_attn_bk", D0)).then_inc(a0_in, 16)
            sp.dma_start(b0[:, 2 * D0:], row("L0_attn_bv", D0)).then_inc(a0_in, 16)

        def sp_l0_ffn(sp):
            names = [("gate_wT", "gate_suT", "gate_sv"), ("up_wT", "up_suT", "up_sv"), ("down_wT", "down_svT", "down_su")]
            for i, (m, k, cols, _, _) in enumerate(chunks):
                if i == first_of[m]:
                    if m:
                        sp.wait_ge(w1_ps, i)
                    wn, fr, fc = names[m]
                    if m < 2:
                        sp.dma_start(suT[0:RANK, :], A[fr]).then_inc(w1_fac, 16)
                        sp.dma_start(svT[0:RANK, :], A[fc]).then_inc(w1_fac, 16)
                    else:
                        sp.dma_start(suT[0:RANK, :], A["down_sv"]).then_inc(w1_fac, 16)
                        sp.dma_start(svT[0:RANK, :], A["down_suT"]).then_inc(w1_fac, 16)
                if i >= 2:
                    sp.wait_ge(w1_eff, i - 1)
                w = cols.stop - cols.start
                sp.dma_start(raw1[:, i % 2, 0:w], A[wn][k * P:(k + 1) * P, cols]).then_inc(w1_raw[i % 2], 16)

        def sp_out(sp):
            xout = A["out"].rearrange("b (t p) c -> p (b t) c", p=P)
            for q in range(4):
                if stop > 1:
                    sp.wait_ge(x_new, (stop - start - yb - 1) * NT + (q + 1) * 4)
                else:
                    sp.wait_ge(xt_ok, 2 * NT)
                sp.dma_start(xout[:, q * 4:(q + 1) * 4, :], x[:, q * 4:(q + 1) * 4, :]).then_inc(x_out, 16)
            sp.wait_ge(x_out, 64)

        def pool_consts(pool, ch):
            ch.link(nc.gpsimd.memset(ident[:, :], 0.0))
            nc.gpsimd.affine_select(out=ident[:, :], in_=ident[:, :], compare_op=ALU.not_equal, fill=1.0, base=0,
                                    pattern=[[-1, P]], channel_multiplier=1).then_inc(consts_ok, 1)
            for i, e in enumerate((EPS, EPS * (WS * ACTS) ** 2, EPS * WS ** 2)):
                nc.gpsimd.memset(epsc[:, i:i + 1], float(e)).then_inc(consts_ok, 1)

        def pool_l0_ffn(pool):
            for i, (m, k, cols, h_, l_) in enumerate(chunks):
                w = cols.stop - cols.start
                pool.wait_ge(w1_hi, i + 1)
                nc.gpsimd.tensor_tensor(l_, we1[:, i % 2, 0:w], h_, ALU.subtract).then_inc(w1_lo, 1)

        def pe_x0(pe):
            pe.wait_ge(consts_ok, 4)
            for t in range(NT):
                Tail.pe_x(pe, t, t, first=(t == 0))

        def pe_l0_attn(pe):
            pe.wait_ge(a0_wh, 2)
            with pe.Fori(0, NG) as g:
                pe.wait_ge(xt_ok, g * GT + GT)
                pe.wait_ge(a0_lg, g + 1)
                for j in range(GT):
                    for k in range(KT):
                        cols = ds(g * GW + j * P, P)
                        last = three(pe, ps_m[:, j * QKV0:(j + 1) * QKV0], xt_hi[:, k, cols], xt_lo[:, k, cols],
                                     w0h[:, k, :], w0l[:, k, :], k == 0, k == KT - 1)
                last.then_inc(a0_qkv, 1)
                for j in range(GT):
                    Tail.pe_x(pe, g * GT + (NT + j), j)


        def pe_l0_ffn(pe):
            for i, (m, k, cols, _, _) in enumerate(chunks):
                w = cols.stop - cols.start
                if i == first_of[m]:
                    pe.wait_ge(w1_fac, 32 * (m + 1))
                if i >= 2:
                    pe.wait_ge(w1_eff, i - 1)
                if m < 2:
                    nc.tensor.matmul(ps_y[:, i % 2, 0:w], svT[0:RANK, k * P:(k + 1) * P], suT[0:RANK, cols],
                                     start=True, stop=True).then_inc(w1_ps, 1)
                else:
                    nc.tensor.matmul(ps_y[:, i % 2, 0:w], suT[0:RANK, k * P:(k + 1) * P], svT[0:RANK, 0:C],
                                     start=True, stop=True).then_inc(w1_ps, 1)
            pe_ffn(pe, 1 - start, F0, gh, gl, uh, ul, dh, dl, hid_h, hid_l, w1_lo, len(chunks), 0)

        def act_x0(act):
            act.wait_ge(consts_ok, 4)
            for t in range(NT):
                if t % 4 == 0:
                    act.wait_ge(x_in[t // 4], 16)
                Tail.act_x(act, t, t, t)
                if t:
                    Tail.act_hi(act, t - 1, t - 1)
            Tail.act_hi(act, NT - 1, NT - 1)


        def act_l0_attn(act, ch):
            act.wait_ge(a0_w, 2)
            nc.scalar.activation(w0h, w0, ACT.Copy, scale=WS).then_inc(a0_wh, 1)
            with loop(act, NG, (ch, 0)) as g:
                act.wait_ge(a0_lg, g * 1 + 2)
                nc.scalar.activation(lg0, lg0, ACT.Exp).then_inc(a0_ex, 1)
                act.wait_ge(a0_var, g + 1)
                nc.scalar.activation(sc0[:, 2, :], sc0[:, 1, :], ACT.Sqrt, bias=epsc[:, 0:1]).then_inc(a0_sd, 1)
                for j in range(GT):
                    Tail.act_x(act, g * GT + (NT + j), g * GT + j, j)
                    if j:
                        Tail.act_hi(act, g * GT + (NT + j - 1), g * GT + (j - 1))
                Tail.act_hi(act, g * GT + (NT + GT - 1), g * GT + (GT - 1))

        def act_l0_ffn(act):
            for i, (m, k, cols, h_, l_) in enumerate(chunks):
                w = cols.stop - cols.start
                act.wait_ge(w1_eff, i + 1)
                nc.scalar.activation(h_, we1[:, i % 2, 0:w], ACT.Copy).then_inc(w1_hi, 1)
            act_ffn(act, 1 - start, F0, hid_h, 0, epsc[:, 1:2], sg1, hd1)

        def dve_x0(dve, ch):
            for t in range(NT):
                if t % 4 == 0:
                    dve.wait_ge(x_in[t // 4], 16)
                Tail.dve_x(dve, ch, None, t, t, t)
                if t:
                    Tail.dve_lo(dve, t - 1, t - 1)
            Tail.dve_lo(dve, NT - 1, NT - 1)


        def dve_l0_attn(dve, ch):
            dve.wait_ge(a0_in, 96)
            nc.vector.tensor_reduce(w0[:, :, 0:D0], w0q, AXX, ALU.add).then_inc(a0_w, 1)
            nc.vector.tensor_reduce(b0[:, 0:D0], b0q, AXX, ALU.add).then_inc(a0_w, 1)
            dve.wait_ge(a0_wh, 1)
            nc.vector.scalar_tensor_tensor(out=w0l, in0=w0, scalar=WS, in1=w0h, op0=ALU.mult,
                                           op1=ALU.subtract).then_inc(a0_wh, 1)
            nc.vector.memset(sc0, 0.0).then_inc(a0_lg, 1)
            with loop(dve, NG, (ch, 16 + 2 * GT)) as g:
                dve.wait_ge(a0_qkv, g + 1)
                psq = ps_m[:, 0:GT * QKV0].rearrange("p (j w) -> p j w", j=GT)
                ch.link(nc.vector.scalar_tensor_tensor(out=qkv0, in0=psq, scalar=1.0 / WS,
                                                       in1=b0.unsqueeze(1).broadcast_to([P, GT, QKV0]),
                                                       op0=ALU.mult, op1=ALU.add))
                ch.link(nc.vector.tensor_tensor(lg0, qkv0[:, :, 0:D0].unsqueeze(3).broadcast_to([P, GT, D0, D0]),
                                                qkv0[:, :, D0:2 * D0].unsqueeze(2).broadcast_to([P, GT, D0, D0]), ALU.mult))
                ch.link(nc.vector.tensor_reduce(mx0, lg0, AXX, ALU.max))
                ch.link(nc.vector.tensor_tensor(lg0, lg0, mx0.unsqueeze(3).broadcast_to([P, GT, D0, D0]), ALU.subtract))
                nc.vector.tensor_scalar(lg0, lg0, float(D0) ** -0.5, None, ALU.mult).then_inc(a0_lg, 1)
                dve.wait_ge(a0_ex, g + 1)
                ch.link(nc.vector.tensor_reduce(sm0, lg0, AXX, ALU.add))
                ch.link(nc.vector.tensor_tensor(pv0, lg0, qkv0[:, :, 2 * D0:].unsqueeze(2).broadcast_to([P, GT, D0, D0]), ALU.mult))
                ch.link(nc.vector.tensor_reduce(o0, pv0, AXX, ALU.add))
                ch.link(nc.vector.reciprocal(sm0, sm0))
                ch.link(nc.vector.tensor_tensor(o0, o0, sm0, ALU.mult))
                ch.link(nc.vector.tensor_reduce(sc0[:, 0, :], o0, AXX, ALU.add))
                ch.link(nc.vector.tensor_scalar(sc0[:, 0, :], sc0[:, 0, :], 1.0 / D0, None, ALU.mult))
                ch.link(nc.vector.tensor_tensor(o0, o0, sc0[:, 0, :].unsqueeze(2).broadcast_to([P, GT, D0]), ALU.subtract))
                ch.link(nc.vector.tensor_tensor(sq0, o0, o0, ALU.mult))
                nc.vector.tensor_reduce(sc0[:, 3, :], sq0, AXX, ALU.add).then_inc(dve_seq, 1); ch.off += 1
                ch.wait(ch.base + ch.off)
                nc.vector.tensor_scalar(sc0[:, 1, :], sc0[:, 3, :], 1.0 / D0, None, ALU.mult).then_inc(a0_var, 1)
                dve.wait_ge(a0_sd, g + 1)
                ch.link(nc.vector.reciprocal(sc0[:, 3, :], sc0[:, 2, :]))
                ch.link(nc.vector.tensor_tensor(o0, o0, sc0[:, 3, :].unsqueeze(2).broadcast_to([P, GT, D0]), ALU.mult))
                for j in range(GT):
                    xv = x[:, g * GT + j, :].rearrange("p (d h) -> p d h", h=H0)
                    v = nc.vector.tensor_tensor(xv, xv, o0[:, j, :].unsqueeze(2).broadcast_to([P, D0, H0]), ALU.add)
                ch.off -= 0
                v.then_inc(x_sd0, 1)
                for j in range(GT):
                    if j == 0:
                        dve.wait_ge(x_sd0, g + 1)
                        alone(dve)
                    Tail.dve_x(dve, ch, None, g * GT + (NT + j), g * GT + j, j)
                    if j:
                        Tail.dve_lo(dve, g * GT + (NT + j - 1), g * GT + (j - 1))
                Tail.dve_lo(dve, g * GT + (NT + GT - 1), g * GT + (GT - 1))

        def dve_l0_ffn(dve, ch):
            for i, (m, k, cols, h_, l_) in enumerate(chunks):
                w = cols.stop - cols.start
                dve.wait_ge(w1_ps, i + 1)
                dve.wait_ge(w1_raw[i % 2], 16 * (i // 2 + 1))
                if i >= 2:
                    dve.wait_ge(w1_lo, i - 1)
                nc.vector.scalar_tensor_tensor(out=we1[:, i % 2, 0:w], in0=ps_y[:, i % 2, 0:w], scalar=WS,
                                               in1=raw1[:, i % 2, 0:w], op0=ALU.mult, op1=ALU.mult).then_inc(w1_eff, 1)
            dve_ffn(dve, ch, 1 - start, F0, hid_h, hid_l, 0, sg1, hd1)

        def sp_l1_attn(sp):
            s = 2 - start
            arena_free(sp, 2)
            sp.dma_start(a2_raw, A["L1_attn_Wqkv"].rearrange("(k p) n -> p k n", p=P)).then_inc(a2_in, 16)
            sp.dma_start(a2_rwo, A["L1_attn_Wo"].rearrange("(k p) n -> p k n", p=P)).then_inc(a2_in, 16)
            sp.dma_start(a2_qs[QR:QR + 2], A["alibi_q"]).then_inc(a2_in, 16)
            sp.dma_start(a2_ks[QR:QR + 3], A["alibi_k"]).then_inc(a2_in, 16)
            sp.dma_start(a2_id, A["ident16"]).then_inc(a2_in, 16)
            sp.dma_start(a2_mqk, A["mask_qk"]).then_inc(a2_in, 16)
            sp.dma_start(a2_mkq, A["mask_kq"]).then_inc(a2_in, 16)
            for b in range(NB):
                sp.wait_ge(a2_klo, 2 * (b + 1))
                if b:
                    sp.wait_ge(y_ready, NT * (s - yb) + TPB * b)
                for rep, src in enumerate((a2_kh, a2_kl, a2_kh, a2_kl)):
                    sp.dma_start(a2_ks[rep * D2:(rep + 1) * D2], src[0:D2]).then_inc(a2_dma, 16)
                for gg in range(2):
                    sp.wait_ge(a2_qlo, KT * (2 * b + gg + 1))
                    for h in range(8):
                        for rep, src in enumerate((a2_qh, a2_qh, a2_ql, a2_ql)):
                            sp.dma_start(a2_qs[rep * D2:(rep + 1) * D2, h:H2:8, gg * GW:(gg + 1) * GW],
                                         src[h * D2:(h + 1) * D2]).then_inc(a2_dma, 16)
                for t in range(TPB):
                    sp.wait_ge(a2_mt_a, TPB * b + t + 1)
                    sp.dma_start(a2_qs[QR + 2:QR + 3, :, t * P:(t + 1) * P], a2_mt[0:H2]).then_inc(a2_mrow, 16)

        def pe_l1_attn(pe):
            s = 2 - start
            pe.wait_ge(a2_wlo, 2)
            pe.wait_ge(a2_in, 16 * 7)
            um, ue = Tally(), Tally()
            per_m, per_e = 4 * sum(len(max_units(t)) for t in range(TPB)), 8 * sum(t + 1 for t in range(TPB))

            def max_unit(t, u, heads, hp):
                pair = 2 * (u % 2)
                n = (t + 1) * P
                pe.wait_ge(a2_md, um(1))
                for a, h in enumerate(heads):
                    q = a2_qs[0:QR + 2, hp * 8 + h, t * P:(t + 1) * P]
                    for c in range(0, n, 512):
                        w = min(512, n - c)
                        bank = pair + a + c // 512
                        diag = c + w == n
                        last = nc.tensor.matmul(ps_g[:, bank, 0:w], q, a2_ks[0:QR + 2, c:c + w], start=True, stop=not diag)
                        if diag:
                            last = nc.tensor.matmul(ps_g[:, bank, w - P:w], a2_id, a2_mqk, start=False, stop=True)
                last.then_inc(a2_ms, 1)
                um.add()

            def score_unit(t, k, i, h4):
                pe.wait_ge(a2_e, ue(1))
                out = psum[:, 6 + i % 2, :]
                last = nc.tensor.matmul(out, a2_ks[0:QR + 3, k * P:(k + 1) * P],
                                        a2_qs[0:QR + 3, h4 * 4:h4 * 4 + 4, t * P:(t + 1) * P], start=True, stop=(k < t))
                if k == t:
                    last = nc.tensor.matmul(out, a2_id, a2_mkq.unsqueeze(1).broadcast_to([P, 4, P]), start=False, stop=True)
                last.then_inc(a2_s, 1)
                ue.add()

            def value_unit(k, i, h4):
                pe.wait_ge(a2_e, ue(1))
                acc = ps_y.rearrange("p a b -> p (a b)")
                for h in range(4):
                    last = nc.tensor.matmul(acc[:, h4 * P + h * (D2 + 1):h4 * P + (h + 1) * (D2 + 1)], a2_p[:, i % 8, h * P:(h + 1) * P],
                                            a2_v[:, k, :], start=(k == 0 and h == 0), stop=True, skip_group_check=True)
                last.then_inc(a2_pv, 1)

            def maximum_alone(t):
                for hp in range(4):
                    for u, heads in enumerate(max_units(t)):
                        max_unit(t, u, heads, hp)

            def attend(t):
                units = [(h4, k) for h4 in range(8) for k in range(t + 1)]
                ms = [(u, heads, hp) for hp in range(4) for u, heads in enumerate(max_units(t + 1))] if t + 1 < TPB else []
                done = 0
                for i, (h4, k) in enumerate(units):
                    want = len(ms) * (i + 1) // len(units)
                    for u, heads, hp in ms[done:want]:
                        max_unit(t + 1, u, heads, hp)
                    done = want
                    score_unit(t, k, i, h4)
                    if i:
                        value_unit(units[i - 1][1], i - 1, units[i - 1][0])
                ue.add()
                value_unit(units[-1][1], len(units) - 1, units[-1][0])
                ue.add(-1)

            def max_row(i):
                pe.wait_ge(a2_md, um(2))
                nc.tensor.transpose(ps_m[0:H2, 0:P], a2_mx, ident[:, :]).then_inc(a2_mt_p, 1)

            with loop(pe, NB, (um, per_m), (ue, per_e)) as b:
                pe.wait_ge(xt_ok, b * TPB + (NT * s + TPB))
                for gg in range(2):
                    for k in range(KT):
                        cols = ds(b * (TPB * P) + gg * GW, GW)
                        last = three(pe, ps_y[0:D2, gg, :], a2_wh[:, k, C:C + D2], a2_wl[:, k, C:C + D2],
                                     xt_hi[:, k, cols], xt_lo[:, k, cols], k == 0, k == KT - 1)
                    last.then_inc(a2_kp, 1)
                for t in range(TPB):
                    tok = ds(b * (TPB * P) + t * P, P)
                    for k in range(KT):
                        last = three(pe, ps_m[:, t * D2:(t + 1) * D2], xt_hi[:, k, tok], xt_lo[:, k, tok],
                                     a2_wh[:, k, C + D2:], a2_wl[:, k, C + D2:], k == 0, k == KT - 1)
                last.then_inc(a2_vp, 1)
                for gg in range(2):
                    for f in range(KT):
                        if gg:
                            pe.wait_ge(a2_qlo, b * (2 * KT) + (f + 1))
                        for k in range(KT):
                            cols = ds(b * (TPB * P) + gg * GW, GW)
                            fc = slice(f * P, (f + 1) * P)
                            last = three(pe, ps_g[:, f, :], a2_wh[:, k, fc], a2_wl[:, k, fc], xt_hi[:, k, cols],
                                         xt_lo[:, k, cols], k == 0, k == KT - 1)
                        last.then_inc(a2_qp, 1)
                pe.wait_ge(a2_dma, b * (16 * QDMA) + 16 * QDMA)
                pe.wait_ge(a2_qlo, b * (2 * KT) + 2 * KT)
                pe.wait_ge(a2_vok, b + 1)
                maximum_alone(0)
                max_row(0)
                for t in range(TPB):
                    i = b * TPB + t
                    pe.wait_ge(a2_mrow, i * 16 + 16)
                    if t:
                        pe.wait_ge(y_norm, i + NT * (s - yb))
                    alone(pe)
                    attend(t)
                    if t + 1 < TPB:
                        max_row(t + 1)
                    pe.wait_ge(a2_o, i + 1)
                    for k in range(KT):
                        last = nc.tensor.transpose(ps_t[:, k, :], a2_ar[:, 8 * k:8 * k + 8, :].rearrange("p h d -> p (h d)"),
                                                   ident[:, :])
                    last.then_inc(a2_tr, 1)
                    pe.wait_ge(a2_tlo, i + 1)
                    if t + 1 < TPB:
                        pe.wait_ge(a2_mt_a, i + 2)
                    for k in range(KT):
                        last = three(pe, ps_m, a2_ah[:, k, :], a2_al[:, k, :], a2_oh[:, k, :], a2_ol[:, k, :],
                                     k == 0, k == KT - 1)
                    last.then_inc(y_ready, 1)
                    if t:
                        Tail.pe_x(pe, i + (NT * (s + 1) - 1), t - 1)
                        pe.wait_ge(xt_ok, i + NT * (s + 1))
                Tail.pe_x(pe, i + NT * (s + 1), TPB - 1)

        def act_l1_attn(act):
            s = 2 - start
            act.wait_ge(a2_in, 16 * 7)
            nc.scalar.activation(a2_wh, a2_raw, ACT.Copy, scale=WS).then_inc(a2_whi, 1)
            nc.scalar.activation(a2_oh, a2_rwo, ACT.Copy, scale=WS).then_inc(a2_whi, 1)
            act.sem_inc(a2_e, 2)
            ue = Tally()
            with loop(act, NB, (ue, 8 * sum(t + 1 for t in range(TPB)))) as b:
                for gg in range(2):
                    act.wait_ge(a2_kp, b * 2 + (gg + 1))
                    nc.scalar.activation(a2_kh[0:D2, gg * GW:(gg + 1) * GW], ps_y[0:D2, gg, :], ACT.Copy,
                                         scale=1.0 / WS).then_inc(a2_khi, 1)
                act.wait_ge(a2_vp, b + 1)
                nc.scalar.activation(a2_v[:, :, 0:D2], ps_m[:, 0:TPB * D2].rearrange("p (t d) -> p t d", t=TPB), ACT.Copy,
                                     scale=1.0 / WS).then_inc(a2_vok, 1)
                for gg in range(2):
                    if gg:
                        act.wait_ge(a2_dma, b * (16 * QDMA) + 16 * (4 + 32))
                    for f in range(KT):
                        act.wait_ge(a2_qp, b * (2 * KT) + (gg * KT + f + 1))
                        nc.scalar.activation(a2_qh[:, f, :], ps_g[:, f, :], ACT.Copy, scale=0.25 / WS).then_inc(a2_qhi, 1)

                def max_row(i):
                    act.wait_ge(a2_mt_p, i)
                    nc.scalar.activation(a2_mt[0:H2], ps_m[0:H2, 0:P], ACT.Copy, scale=-1.0).then_inc(a2_mt_a, 1)

                max_row(b * TPB + 1)
                for t in range(TPB):
                    i = b * TPB + t
                    n = 8 * (t + 1)
                    for u in range(n):
                        act.wait_ge(a2_s, ue(1))
                        if u >= 8:
                            act.wait_ge(a2_pv, ue(-7))
                        nc.scalar.activation(a2_p[:, u % 8, :], psum[:, 6 + u % 2, :], ACT.Exp).then_inc(a2_e, 1)
                        ue.add()
                    if t + 1 < TPB:
                        max_row(i + 2)
                    act.wait_ge(a2_tr, i + 1)
                    nc.scalar.activation(a2_ah, ps_t, ACT.Copy, scale=ACTS).then_inc(a2_thi, 1)
                    Tail.act_y(act, i + NT * (s - yb), t, ps_m, epsc[:, 1:2])
                    Tail.act_x(act, i + NT * (s + 1), i, t)
                    if t:
                        Tail.act_hi(act, i + (NT * (s + 1) - 1), i - 1)
                Tail.act_hi(act, i + NT * (s + 1), i)

        def dve_l1_attn(dve, ch):
            s = 2 - start
            dve.wait_ge(a2_whi, 2)
            nc.vector.scalar_tensor_tensor(out=a2_wl, in0=a2_raw, scalar=WS, in1=a2_wh, op0=ALU.mult,
                                           op1=ALU.subtract).then_inc(a2_wlo, 1)
            nc.vector.scalar_tensor_tensor(out=a2_ol, in0=a2_rwo, scalar=WS, in1=a2_oh, op0=ALU.mult,
                                           op1=ALU.subtract).then_inc(a2_wlo, 1)
            nc.vector.memset(a2_v[:, :, D2:D2 + 1], 1.0).then_inc(a2_md, 2)
            um, uv = Tally(), Tally()
            with loop(dve, NB, (um, 4 * sum(len(max_units(t)) for t in range(TPB))),
                      (uv, 8 * sum(t + 1 for t in range(TPB))), (ch, TPB * 5)) as b:
                for gg in range(2):
                    dve.wait_ge(a2_khi, b * 2 + (gg + 1))
                    w = slice(gg * GW, (gg + 1) * GW)
                    nc.vector.scalar_tensor_tensor(out=a2_kl[0:D2, w], in0=ps_y[0:D2, gg, :], scalar=1.0 / WS,
                                                   in1=a2_kh[0:D2, w], op0=ALU.mult, op1=ALU.subtract).then_inc(a2_klo, 1)
                for gg in range(2):
                    for f in range(KT):
                        dve.wait_ge(a2_qhi, b * (2 * KT) + (gg * KT + f + 1))
                        nc.vector.scalar_tensor_tensor(out=a2_ql[:, f, :], in0=ps_g[:, f, :], scalar=0.25 / WS,
                                                       in1=a2_qh[:, f, :], op0=ALU.mult,
                                                       op1=ALU.subtract).then_inc(a2_qlo, 1)

                def maxima(t):
                    units = max_units(t)
                    for hp in range(4):
                        for u, heads in enumerate(units):
                            pair = 2 * (u % 2)
                            n = (t + 1) * P
                            dve.wait_ge(a2_ms, um(1))
                            if len(heads) == 2:
                                src = ps_g[:, pair:pair + 2, 0:n]
                            else:
                                src = ps_g[:, pair:pair + 2, :].rearrange("p a b -> p (a b)")[:, 0:n].unsqueeze(1)
                            h = hp * 8 + heads[0]
                            nc.vector.tensor_reduce(a2_mx[:, h:h + len(heads)], src, AXX, ALU.max).then_inc(a2_md, 1)
                            um.add()

                maxima(0)
                for t in range(TPB):
                    i = b * TPB + t
                    if t + 1 < TPB:
                        maxima(t + 1)
                    uv.add(8 * (t + 1))
                    dve.wait_ge(a2_pv, uv())
                    acc = ps_y.rearrange("p a (c w) -> p (a c) w", w=P)[:, :, 0:4 * (D2 + 1)].rearrange("p g (h d) -> p g h d", h=4)
                    rd = a2_rd.rearrange("p (g h) -> p g h", h=4)
                    ch.link(nc.vector.reciprocal(rd, acc[:, :, :, D2]))
                    nc.vector.tensor_tensor(a2_ar.rearrange("p (g h) d -> p g h d", h=4), acc[:, :, :, 0:D2],
                                            rd.unsqueeze(3).broadcast_to([P, 8, 4, D2]), ALU.mult).then_inc(a2_o, 1)
                    dve.wait_ge(a2_thi, i + 1)
                    nc.vector.scalar_tensor_tensor(out=a2_al, in0=ps_t, scalar=ACTS, in1=a2_ah, op0=ALU.mult,
                                                   op1=ALU.subtract).then_inc(a2_tlo, 1)
                    Tail.dve_y(dve, ch, i + NT * (s - yb), i, t, ps_m)
                    Tail.dve_x(dve, ch, i + NT * (s - yb), i + NT * (s + 1), i, t)
                    if t:
                        Tail.dve_lo(dve, i + (NT * (s + 1) - 1), i - 1)
                Tail.dve_lo(dve, i + NT * (s + 1), i)

        def sp_l1_ffn(sp):
            arena_free(sp, 3)
            sp.dma_start(s3_raw, A["L1_ffn_sign"].rearrange("(k p) n -> p k n", p=P)).then_inc(s3_in, 16)
            sp.dma_start(s3_s[:, 0:1], A["L1_ffn_scale"].broadcast_to([P, 1])).then_inc(s3_scale, 16)

        def act_l1_ffn(act):
            act.wait_ge(s3_in, 16)
            nc.scalar.activation(s3_h, s3_raw, ACT.Copy, scale=WS).then_inc(s3_hi, 1)
            act.wait_ge(s3_scale, 16)
            nc.scalar.activation(s3_s[:, 1:2], s3_s[:, 0:1], ACT.Abs).then_inc(s3_sp, 1)
            act.wait_ge(s3_sp, 1)
            nc.scalar.activation(s3_s[:, 2:3], s3_s[:, 1:2], ACT.Exp, scale=-1.0).then_inc(s3_sp, 1)
            act.wait_ge(s3_sp, 2)
            nc.scalar.activation(s3_s[:, 3:4], s3_s[:, 2:3], ACT.Ln, bias=1.0).then_inc(s3_sp, 1)
            act.wait_ge(s3_eps, 4)
            with act.Fori(0, NG) as g:
                act_group(act, 3 - start, g, epsc[:, 3:4])

        def dve_l1_ffn(dve, ch):
            dve.wait_ge(s3_hi, 1)
            nc.vector.scalar_tensor_tensor(out=s3_l, in0=s3_raw, scalar=WS, in1=s3_h, op0=ALU.mult,
                                           op1=ALU.subtract).then_inc(s3_lo, 1)
            dve.wait_ge(s3_sp, 3)
            nc.vector.scalar_tensor_tensor(out=s3_s[:, 4:5], in0=s3_s[:, 0:1], scalar=0.0, in1=s3_s[:, 3:4],
                                           op0=ALU.max, op1=ALU.add).then_inc(s3_eps, 1)
            dve.wait_ge(s3_eps, 1)
            nc.vector.reciprocal(s3_s[:, 5:6], s3_s[:, 4:5]).then_inc(s3_eps, 1)
            dve.wait_ge(s3_eps, 2)
            nc.vector.tensor_scalar(s3_s[:, 6:7], s3_s[:, 5:6], WS * EPS ** 0.5, None, ALU.mult).then_inc(s3_eps, 1)
            dve.wait_ge(s3_eps, 3)
            nc.vector.tensor_tensor(epsc[:, 3:4], s3_s[:, 6:7], s3_s[:, 6:7], ALU.mult).then_inc(s3_eps, 1)
            with loop(dve, NG, (ch, 4 * GT)) as g:
                dve_group(dve, ch, 3 - start, g)

        def pe_l1_ffn(pe):
            pe.wait_ge(s3_lo, 1)
            s = 3 - start
            with pe.Fori(0, NG) as g:
                pe.wait_ge(xt_ok, g * GT + (NT * s + GT))

                def y_tile(j):
                    r = g * GT + (NT * (s - yb) + j)
                    if j >= 2:
                        pe.wait_ge(y_norm, r - 1)
                    tok = ds(g * GW + j * P, P)
                    for k in range(KT):
                        last = three(pe, ps_y[:, j % 2, :], xt_hi[:, k, tok], xt_lo[:, k, tok], s3_h[:, k, :],
                                     s3_l[:, k, :], k == 0, k == KT - 1)
                    last.then_inc(y_ready, 1)
                pe_group(pe, s, g, y_tile)

        HF = 4
        CG = NT
        QI, QS = 2 * KT, 3 * KT

        def sp_l2_attn(sp):
            arena_free(sp, 4)
            row = lambda n: A[n].rearrange("(o n) -> o n", o=1).broadcast_to([P, HS])
            sp.dma_start(m4_dr, A["m4_dt"]).then_inc(m4_cin, 16)
            sp.dma_start(m4_db, row("L2_attn_dt_bias")).then_inc(m4_cin, 16)
            sp.dma_start(m4_na, row("L2_attn_A_log")).then_inc(m4_cin, 16)
            for v, n in ((m4_le, "tri_le"), (m4_gt, "tri_gt"), (m4_on, "ones16")):
                sp.dma_start(v, A[n]).then_inc(m4_cin, 16)
            wi = A["m4_wi"].rearrange("g q p n -> p (g q) n")
            wo = A["m4_wo"].rearrange("g q p n -> p (g q) n")

            def fetch(q, src, at, w):
                sp.dma_start(m4_raw[:, q % 2:q % 2 + 1, 0:w], src[:, ds(at, 1), :]).then_inc(m4_ri[q % 2], 16)

            for q in range(QI):
                if q >= 2:
                    sp.wait_ge(m4_wlo, q + 1)
                fetch(q, wi, q, SW)
            with sp.Fori(0, GS) as gi:
                sp.wait_ge(m4_nwk, gi * 2 + 1)
                sp.dma_start(m4_pn.unsqueeze(1), A["m4_par"][:, ds(gi, 1), :]).then_inc(m4_pi, 16)
                for q in range(KT):
                    sp.wait_ge(m4_wlo, gi * QS + (QI + q + 1))
                    fetch(q, wo, gi * KT + q, C)
                for q in range(QI):
                    sp.wait_ge(m4_wlo, gi * QS + (QS + q + 1))
                    fetch(q, wi, gi * QI + (QI + q), SW)

        def act_piece(act, gi, j):
            act.wait_ge(m4_ri[j % 2], (gi * (QS // 2) + (j // 2 + 1)) * 16)
            q = j % QS
            if q < QI:
                v = nc.scalar.activation(m4_wh[:, q // 2, q % 2 * SW:(q % 2 + 1) * SW], m4_raw[:, j % 2, :], ACT.Copy,
                                         scale=WS)
            else:
                v = nc.scalar.activation(m4_wh[:, q - QI, IW:], m4_raw[:, j % 2, 0:C], ACT.Copy,
                                         scale=m4_nw[:, q - QI:q - QI + 1])
            v.then_inc(m4_whi, 1)

        def dve_piece(dve, gi, j):
            dve.wait_ge(m4_whi, gi * QS + (j + 1))
            q = j % QS
            if q < QI:
                wc, raw, w = (q // 2, slice(q % 2 * SW, (q % 2 + 1) * SW)), m4_raw[:, j % 2, :], WS
            else:
                wc, raw, w = (q - QI, slice(IW, IW + C)), m4_raw[:, j % 2, 0:C], m4_nw[:, q - QI:q - QI + 1]
            nc.vector.scalar_tensor_tensor(out=m4_wl[:, wc[0], wc[1]], in0=raw, scalar=w, in1=m4_wh[:, wc[0], wc[1]],
                                           op0=ALU.mult, op1=ALU.subtract).then_inc(m4_wlo, 1)

        def act_l2_attn(act):
            for c in (m4_qk, m4_ek, m4_dk, m4_sdk, m4_bk):
                act.sem_inc(c, 1)
            act.wait_ge(m4_cin, 6 * 16)
            nc.scalar.activation(m4_na, m4_na, ACT.Exp).then_inc(m4_dw, 1)
            nc.scalar.activation(m4_dh, m4_dr, ACT.Copy, scale=WS).then_inc(m4_dw, 1)
            for j in range(QI):
                act_piece(act, 0, j)
            for n in range(2):
                act.wait_ge(m4_tv, 4 * n + 1)
                nc.scalar.activation(m4_v, m4_u, ACT.Abs).then_inc(m4_ta, 1)
                act.wait_ge(m4_ta, 5 * n + 1)
                nc.scalar.activation(m4_v, m4_v, ACT.Exp, scale=-1.0).then_inc(m4_ta, 1)
                act.wait_ge(m4_ta, 5 * n + 2)
                nc.scalar.activation(m4_v, m4_v, ACT.Ln, bias=1.0).then_inc(m4_ta, 1)
                act.wait_ge(m4_tv, 4 * n + 2)
                hc = slice(n * 8 * HS, (n + 1) * 8 * HS)
                nc.scalar.activation(m4_ah[:, hc], m4_u, ACT.Copy).then_inc(m4_ta, 1)
                act.wait_ge(m4_dq, n + 1)
                nc.scalar.activation(m4_v, psum[:, 6, :], ACT.Exp).then_inc(m4_ta, 1)
                act.wait_ge(m4_tv, 4 * n + 4)

            with act.Fori(0, GS) as gi:
                act.wait_ge(m4_gd, gi * 2 + 1)
                act.wait_ge(m4_sk, gi * (CG + 2) + 1)
                nc.scalar.activation(m4_dg, psum[:, 7, 0:NT * HG], ACT.Exp).then_inc(m4_gd, 1)
                act.wait_ge(m4_nwk, gi * 2 + 3)
                act.wait_ge(m4_op, gi * CG + 1)
                for j in range(QI, QI + 2):
                    act_piece(act, gi, j)
                for x in range(HF):
                    act_before(act, gi, x, range(2 if x else 0, 6))
                    if x == 0:
                        for j in range(QI + 2, QS):
                            act_piece(act, gi, j)
                    act_gates(act, gi, x)
                    for c in range(4):
                        if c:
                            deviation(act, gi, x, c - 1)
                        square(act, gi, x, c)
                        if c < 3:
                            b_tokens(act, gi, x, c + 1)
                        if x == HF - 1:
                            if c == 0:
                                act.wait_ge(m4_ip, (gi + 1) * (HF * FT))
                            act_piece(act, gi, QS + 2 * c)
                        gated(act, gi, x, c)
                        if c < 2:
                            decays(act, gi, x, c + 2)
                        if x == HF - 1:
                            act_piece(act, gi, QS + 2 * c + 1)
                    if x < HF - 1:
                        act_before(act, gi, x + 1, range(0, 2))
                    deviation(act, gi, x, 3)
            s = 4 - start
            with act.Fori(0, NG) as g:
                act_group(act, s, g, epsc[:, 2:3], y=lambda j: m4_acc_tile(g, j))

        def m4_acc_tile(g, j):
            return m4_acc[:, ds(g * GT + j, 1), :].rearrange("p a c -> p (a c)")

        BANK = (0, 1, 2, 3, 0, 1, 2, 3, 2, 3)

        def act_before(act, gi, x, tiles):
            for i in tiles:
                if i == 0:
                    act.wait_ge(m4_cy, gi * HF + (x + 1))
                act.wait_ge(m4_ip, gi * (HF * FT) + (x * FT + i + 1))
                nc.scalar.activation(m4_hb[:, i, KC - 1:], ps_g[:, BANK[i], :], ACT.Copy,
                                     scale=1.0 / WS).then_inc(m4_hbk, 1)

        def act_gates(act, gi, x):
            def gate(i):
                act.wait_ge(m4_ip, gi * (HF * FT) + (x * FT + i + 1))
                nc.scalar.activation(m4_sg[:, i - CT, :], ps_g[:, BANK[i], :], ACT.Silu,
                                     scale=1.0 / WS).then_inc(m4_gk, 1)

            def convolved(i):
                act.wait_ge(m4_cv, gi * (HF * CT) + (x * CT + i + 1))
                nc.scalar.activation(m4_xc[:, i, :], m4_xc[:, i, :], ACT.Silu).then_inc(m4_xk, 1)
            act.wait_ge(m4_ylo, gi * CG + (x * 4 + 1))
            for i in range(3):
                convolved(i)
            gate(6)
            convolved(3)
            gate(7)
            convolved(4)
            convolved(5)
            decays(act, gi, x, 0)
            gate(8)
            gate(9)
            b_tokens(act, gi, x, 0)
            decays(act, gi, x, 1)

        def decays(act, gi, x, c):
            k = gi * CG + (x * 4 + c + 1)
            act.wait_ge(m4_sp, k + 1)
            act.wait_ge(m4_ia, k)
            nc.scalar.activation(m4_e[c % 2].rearrange("p h t -> p (h t)"),
                                 psum[:, 0:2, :].rearrange("p a t -> p (a t)"), ACT.Exp).then_inc(m4_ek, 1)
            act.wait_ge(m4_dd, k + 1)
            act.wait_ge(m4_tk, k)
            nc.scalar.activation(m4_de[:, c % 2].rearrange("p i t -> p (i t)"), psum[:, 4, :], ACT.Exp).then_inc(m4_dk, 1)

        def b_tokens(act, gi, x, c):
            k = gi * CG + (x * 4 + c + 1)
            act.wait_ge(m4_xp, k)
            act.wait_ge(m4_sn, k)
            nc.scalar.activation(m4_bt, psum[:, 3, 0:P], ACT.Copy).then_inc(m4_bk, 1)

        def square(act, gi, x, c):
            k = gi * CG + (x * 4 + c + 1)
            tok = slice(c * P, (c + 1) * P)
            act.wait_ge(m4_yk, k + 1)
            act.wait_ge(m4_qp, k)
            nc.scalar.activation(m4_sq, m4_xc[:, 0:4, tok], ACT.Square).then_inc(m4_qk, 1)

        def gated(act, gi, x, c):
            k = gi * CG + (x * 4 + c + 1)
            act.wait_ge(m4_yn, k + 1)
            act.wait_ge(m4_op, k)
            nc.scalar.activation(m4_yh, m4_sg[:, :, c * P:(c + 1) * P], ACT.Copy).then_inc(m4_yhi, 1)

        def deviation(act, gi, x, c):
            k = gi * CG + (x * 4 + c + 1)
            act.wait_ge(m4_qp, k + 1)
            act.wait_ge(m4_rk, k)
            nc.scalar.activation(m4_sd, psum[:, 7, 3 * P:3 * P + 1], ACT.Sqrt, scale=1.0 / GF,
                                 bias=epsc[:, 0:1]).then_inc(m4_sdk, 1)

        def dve_l2_attn(dve, ch):
            for c in (m4_ok, m4_mk, m4_rk, m4_yk, m4_sk, m4_nwk):
                dve.sem_inc(c, 1)
            dve.sem_inc(m4_wlo, 2)
            dve.sem_inc(m4_tk, 2)
            dve.wait_ge(m4_cin, 6 * 16)
            dve.wait_ge(m4_dw, 2)
            nc.vector.scalar_tensor_tensor(out=m4_dl, in0=m4_dr, scalar=WS, in1=m4_dh, op0=ALU.mult,
                                           op1=ALU.subtract).then_inc(m4_dw, 1)
            nc.vector.memset(m4_acc, 0.0)
            nc.vector.memset(m4_o32, 1.0)
            nc.vector.memset(m4_hb[:, :, 0:KC - 1], 0.0).then_inc(m4_cy, 1)
            for j in range(QI):
                dve_piece(dve, 0, j)
            for n in range(2):
                hc = slice(n * 8 * HS, (n + 1) * 8 * HS)
                by_tile = lambda v: v.rearrange("p (t h) -> p t h", h=HS)
                dve.wait_ge(m4_dp, n + 1)
                nc.vector.scalar_tensor_tensor(out=by_tile(m4_u), in0=by_tile(ps_m), scalar=1.0 / WS,
                                               in1=m4_db.unsqueeze(1).broadcast_to([P, 8, HS]), op0=ALU.mult,
                                               op1=ALU.add).then_inc(m4_tv, 1)
                dve.wait_ge(m4_ta, 5 * n + 3)
                ch.link(nc.vector.scalar_tensor_tensor(out=m4_dtp[:, hc], in0=m4_u, scalar=0.0, in1=m4_v, op0=ALU.max,
                                                       op1=ALU.add))
                ch.link(nc.vector.scalar_tensor_tensor(out=by_tile(m4_u), in0=by_tile(m4_dtp[:, hc]), scalar=-1.0,
                                                       in1=m4_na.unsqueeze(1).broadcast_to([P, 8, HS]), op0=ALU.mult,
                                                       op1=ALU.mult))
                nc.vector.tensor_scalar(m4_u, m4_u, -1000.0, None, ALU.max).then_inc(m4_tv, 1)
                dve.wait_ge(m4_ta, 5 * n + 4)
                nc.vector.tensor_tensor(m4_al[:, hc], m4_u, m4_ah[:, hc], ALU.subtract).then_inc(m4_tv, 1)
                dve.wait_ge(m4_ta, 5 * n + 5)
                nc.vector.tensor_tensor(m4_dt2[:, hc], m4_dtp[:, hc], m4_v, ALU.mult).then_inc(m4_tv, 1)
            dve.wait_ge(m4_tv, 8)

            with loop(dve, GS, (ch, HF * (CT * (KC - 1) + 4 * 3))) as gi:
                dve.wait_ge(m4_pi, gi * 16 + 16)
                dve.wait_ge(m4_wlo, gi * QS + (QI + 2))
                dve.wait_ge(m4_ok, gi * CG + 1)
                nc.vector.tensor_scalar(m4_par, m4_pn, 1.0, None, ALU.mult).then_inc(m4_nwk, 1)
                dve.wait_ge(m4_nwk, gi * 2 + 2)
                nc.vector.tensor_scalar(m4_nw, m4_par[:, CT * (KC + 1) + 4:], WS, None, ALU.mult).then_inc(m4_nwk, 1)
                dve.wait_ge(m4_nwk, gi * 2 + 3)
                for j in range(QI, QI + 2):
                    dve_piece(dve, gi, j)
                for x in range(HF):
                    if x % 2 == 0:
                        dve.wait_ge(m4_sn, gi * CG + (x * 4 + 1))
                        dve.wait_ge(m4_sk, gi * (CG + 2) + (x * 4 + x // 2 + 1))
                        nc.vector.memset(m4_st, 0.0).then_inc(m4_sk, 1)
                    convolve(dve, ch, gi, x)
                    if x == 0:
                        for j in range(QI + 2, QS):
                            dve_piece(dve, gi, j)
                        dve.wait_ge(m4_gd, gi * 2 + 2)
                    masked(dve, ch, gi, x, 0)
                    stepped(dve, gi, x, 0)
                    masked(dve, ch, gi, x, 1)
                    for c in range(4):
                        from_state(dve, gi, x, c)
                        state(dve, ch, gi, x, c)
                        outputs(dve, ch, gi, x, c)
                        if x == HF - 1:
                            dve_piece(dve, gi, QS + 2 * c)
                        if c < 3:
                            stepped(dve, gi, x, c + 1)
                        if c:
                            add_out(dve, gi, x, c - 1)
                        if c < 2:
                            masked(dve, ch, gi, x, c + 2)
                        if x == HF - 1:
                            dve_piece(dve, gi, QS + 2 * c + 1)
                    add_out(dve, gi, x, 3)
            s = 4 - start
            with loop(dve, NG, (ch, 4 * GT)) as g:
                def summed(j):
                    dve.wait_ge(m4_ok, GS * CG + 1)
                    dve.sem_inc(y_ready, 1)
                dve_group(dve, ch, s, g, y=lambda j: m4_acc_tile(g, j), before=summed)

        def convolve(dve, ch, gi, x):
            dve.wait_ge(m4_qk, gi * CG + (x * 4 + 1))
            dve.wait_ge(m4_yn, gi * CG + (x * 4 + 1))
            dve.wait_ge(m4_cy, gi * HF + (x + 1))
            for i in range(CT):
                dve.wait_ge(m4_hbk, gi * (HF * CT) + (x * CT + i + 1))
                tap = lambda j: m4_par[:, i * KC + j:i * KC + j + 1]
                out = m4_xc[:, i, :]
                ch.link(nc.vector.tensor_scalar(out, m4_hb[:, i, 0:GW], tap(0), m4_par[:, CT * KC + i:CT * KC + i + 1],
                                                ALU.mult, ALU.add))
                for j in range(1, KC):
                    v = nc.vector.scalar_tensor_tensor(out=out, in0=m4_hb[:, i, j:j + GW], scalar=tap(j), in1=out,
                                                       op0=ALU.mult, op1=ALU.add)
                    if j < KC - 1:
                        ch.link(v)
                v.then_inc(m4_cv, 1)
            dve.wait_ge(m4_cv, gi * (HF * CT) + (x + 1) * CT)
            if x % 2 == 0:
                nc.vector.tensor_scalar(m4_hb[:, :, 0:KC - 1], m4_hb[:, :, GW:GW + KC - 1], 1.0, None,
                                        ALU.mult).then_inc(m4_cy, 1)
            else:
                nc.vector.memset(m4_hb[:, :, 0:KC - 1], 0.0).then_inc(m4_cy, 1)

        def masked(dve, ch, gi, x, c):
            k = gi * CG + (x * 4 + c + 1)
            dve.wait_ge(m4_gp, k)
            dve.wait_ge(m4_mk, k)
            ch.link(nc.vector.tensor_tensor(m4_gm, psum[:, 7, P:2 * P], m4_le, ALU.mult))
            dve.wait_ge(m4_ek, k + 1)
            e = m4_e[c % 2]
            nc.vector.tensor_tensor(e, e, m4_gm.unsqueeze(1).broadcast_to([P, HG, P]), ALU.mult).then_inc(m4_mk, 1)

        def stepped(dve, gi, x, c):
            k = gi * CG + (x * 4 + c + 1)
            dve.wait_ge(m4_xp, k)
            dve.wait_ge(m4_sn, k)
            xs = psum[:, 6, :].rearrange("p (h c) -> p h c", h=HG)
            for n, d in enumerate((m4_dtp, m4_dt2)):
                steps = d[:, ds(gi * HG + (x * 4 + c) * HS, HG)]
                nc.vector.tensor_tensor(m4_x12[:, n * GF:(n + 1) * GF].rearrange("p (h c) -> p h c", h=HG), xs,
                                        steps.unsqueeze(2).broadcast_to([P, HG, PS]), ALU.mult).then_inc(m4_x2, 1)

        def from_state(dve, gi, x, c):
            k = gi * CG + (x * 4 + c + 1)
            dve.wait_ge(m4_ii, k)
            dve.wait_ge(m4_dk, k + 1)
            dve.wait_ge(m4_yk, k)
            nc.vector.tensor_tensor(m4_ty.rearrange("p i t -> p (i t)"), psum[:, 3, :],
                                    m4_de[:, c % 2].rearrange("p i t -> p (i t)"), ALU.mult).then_inc(m4_tk, 1)

        def outputs(dve, ch, gi, x, c):
            k = gi * CG + (x * 4 + c + 1)
            tok = slice(c * P, (c + 1) * P)
            flat = m4_ty.rearrange("p i t -> p (i t)")
            dve.wait_ge(m4_ia, k + 2)
            dve.wait_ge(m4_tk, k + 2)
            ch.link(nc.vector.tensor_tensor(flat, flat, psum[:, 2, :], ALU.add))
            for i in range(4):
                d = CT * (KC + 1) + i
                v = nc.vector.scalar_tensor_tensor(out=m4_xc[:, i, tok], in0=m4_xc[:, i, tok], scalar=m4_par[:, d:d + 1],
                                                   in1=m4_ty[:, i, :], op0=ALU.mult, op1=ALU.add)
            v.then_inc(m4_yk, 1)

        def state(dve, ch, gi, x, c):
            dve.wait_ge(m4_sn, gi * CG + (x * 4 + c + 2))
            dve.wait_ge(m4_sk, gi * (CG + 2) + (x * 4 + c + x // 2 + 2))
            by_head = m4_st.rearrange("p (h c) -> p h c", h=HG)
            da = m4_dg[:, (x * 4 + c) * HG:(x * 4 + c + 1) * HG]
            ch.link(nc.vector.tensor_tensor(by_head, by_head, da.unsqueeze(2).broadcast_to([P, HG, PS]), ALU.mult))
            nc.vector.tensor_tensor(m4_st, m4_st, psum[:, 6, :], ALU.add).then_inc(m4_sk, 1)

        def add_out(dve, gi, x, c):
            k = gi * CG + (x * 4 + c + 1)
            dve.wait_ge(m4_sdk, k + 1)
            dve.wait_ge(m4_ok, k)
            nc.vector.reciprocal(m4_rs, m4_sd).then_inc(m4_rk, 1)
            dve.wait_ge(m4_rk, k + 1)
            dve.wait_ge(m4_op, k + 1)
            acc = m4_acc[:, x * 4 + c, :]
            nc.vector.scalar_tensor_tensor(out=acc, in0=psum[:, 5, :], scalar=m4_rs, in1=acc, op0=ALU.mult,
                                           op1=ALU.add).then_inc(m4_ok, 1)

        def pool_l2_attn(pool):
            for c in (m4_yn, m4_ylo):
                pool.sem_inc(c, 1)
            pool.wait_ge(m4_tv, 4 + 3)

            def spread(gi, j):
                pool.wait_ge(m4_sp, gi * CG + (j + 1))
                alone(pool)
                heads = [a[:, ds(gi * HG + (j * HS), HG)].unsqueeze(2) for a in (m4_ah, m4_al)]
                for n in range(2):
                    nc.gpsimd.tensor_tensor(m4_ar[:, n], heads[n].broadcast_to([P, HG, P]),
                                            m4_le.unsqueeze(1).broadcast_to([P, HG, P]), ALU.mult).then_inc(m4_ak, 1)
                pool.wait_ge(m4_dd, gi * CG + (j + 1))
                alone(pool)
                for n in range(2):
                    nc.gpsimd.tensor_tensor(m4_ab[:, n].rearrange("p (h c) -> p h c", c=PS),
                                            heads[n].broadcast_to([P, HG, PS]),
                                            m4_on[:, 0:PS].unsqueeze(1).broadcast_to([P, HG, PS]),
                                            ALU.mult).then_inc(m4_ak, 1)

            with pool.Fori(0, GS) as gi:
                spread(gi, 0)
                for x in range(HF):
                    spread(gi, x * 4 + 1)
                    for c in range(4):
                        k = gi * CG + (x * 4 + c + 1)
                        tok = slice(c * P, (c + 1) * P)
                        if c < 2 or (c == 2 and x < HF - 1):
                            spread(gi, x * 4 + c + 2)
                        pool.wait_ge(m4_yk, k + 1)
                        pool.wait_ge(m4_gk, gi * (HF * 4) + (x * 4 + 4))
                        nc.gpsimd.tensor_tensor(m4_sg[:, :, tok], m4_xc[:, 0:4, tok], m4_sg[:, :, tok],
                                                ALU.mult).then_inc(m4_yn, 1)
                        pool.wait_ge(m4_yn, k + 1)
                        pool.wait_ge(m4_yhi, k)
                        nc.gpsimd.tensor_tensor(m4_yl, m4_sg[:, :, tok], m4_yh, ALU.subtract).then_inc(m4_ylo, 1)

        def pe_l2_attn(pe):
            s = 4 - start
            for c in (m4_op, m4_sp, m4_dd, m4_sn, m4_qp, m4_ia, m4_ia):
                pe.sem_inc(c, 1)
            pe.wait_ge(xt_ok, NT * (s + 1))
            pe.wait_ge(m4_dw, 3)
            for n in range(2):
                if n:
                    pe.wait_ge(m4_tv, 4 * n - 3)
                for j in range(8):
                    tok = slice((n * 8 + j) * P, (n * 8 + j + 1) * P)
                    for k in range(KT):
                        last = three(pe, ps_m[:, j * HS:(j + 1) * HS], xt_hi[:, k, tok], xt_lo[:, k, tok],
                                     m4_dh[:, k, :], m4_dl[:, k, :], k == 0, k == KT - 1)
                last.then_inc(m4_dp, 1)
            for n in range(2):
                hc = slice(n * 8 * HS, (n + 1) * 8 * HS)
                pe.wait_ge(m4_tv, 4 * n + 3)
                if n:
                    pe.wait_ge(m4_ta, 5 * n)
                nc.tensor.matmul(psum[:, 6, :], m4_gt, m4_ah[:, hc], start=True, stop=False)
                nc.tensor.matmul(psum[:, 6, :], m4_gt, m4_al[:, hc], start=False, stop=True).then_inc(m4_dq, 1)
            pe.wait_ge(m4_ta, 10)

            with pe.Fori(0, GS) as gi:
                pe.wait_ge(m4_sdk, gi * CG + 1)
                for n, a in enumerate((m4_ah, m4_al)):
                    v = nc.tensor.matmul(psum[:, 7, 0:NT * HG], m4_on,
                                         a.rearrange("p (t h) -> p t h", h=HS)[:, :, ds(gi * HG, HG)],
                                         start=(n == 0), stop=(n == 1))
                v.then_inc(m4_gd, 1)
                pe.wait_ge(m4_wlo, gi * QS + (QI + 2))
                for x in range(HF):
                    in_proj(pe, gi, x, range(2 if x else 0, 8))
                    between(pe, gi, x, 0)
                    in_proj(pe, gi, x, range(8, 9))
                    b_dot_c(pe, gi, x, 0)
                    in_proj(pe, gi, x, range(9, 10))
                    to_tokens(pe, gi, x, 0)
                    between(pe, gi, x, 1)
                    b_dot_c(pe, gi, x, 1)
                    for c in range(4):
                        chunk(pe, gi, x, c)
                        if c:
                            out_proj(pe, gi, x, c - 1)
                        if c < 3:
                            to_tokens(pe, gi, x, c + 1)
                        if c < 2:
                            between(pe, gi, x, c + 2)
                            b_dot_c(pe, gi, x, c + 2)
                    if x < HF - 1:
                        in_proj(pe, gi, x + 1, range(0, 2))
                    out_proj(pe, gi, x, 3)
            with pe.Fori(0, NG) as g:
                pe_group(pe, s, g, lambda j: None)

        def in_proj(pe, gi, x, tiles):
            for i in tiles:
                if 4 <= i < 8:
                    pe.wait_ge(m4_hbk, gi * (HF * CT) + (x * CT + i - 3))
                if i >= 8:
                    pe.wait_ge(m4_gk, gi * (HF * 4) + (x * 4 + i - 7))
                for k in range(KT):
                    fc = slice(i * P, (i + 1) * P)
                    tok = slice(x * GW, (x + 1) * GW)
                    last = three(pe, ps_g[:, BANK[i], :], m4_wh[:, k, fc], m4_wl[:, k, fc], xt_hi[:, k, tok],
                                 xt_lo[:, k, tok], k == 0, k == KT - 1)
                last.then_inc(m4_ip, 1)

        def b_dot_c(pe, gi, x, c):
            k = gi * CG + (x * 4 + c + 1)
            tok = slice(c * P, (c + 1) * P)
            if c == 0:
                pe.wait_ge(m4_gd, gi * 2 + 2)
                pe.wait_ge(m4_xk, gi * (HF * CT) + (x * CT + CT))
            pe.wait_ge(m4_sdk, gi * CG + (x * 4 + max(0, c - 2) + 1))
            pe.wait_ge(m4_mk, k)
            nc.tensor.matmul(psum[:, 7, P:2 * P], m4_xc[:, 4, tok], m4_xc[:, 5, tok], start=True,
                             stop=True).then_inc(m4_gp, 1)

        def between(pe, gi, x, c):
            k = gi * CG + (x * 4 + c + 1)
            ak = gi * (4 * CG) + (x * 4 + c) * 4
            if c == 0:
                pe.wait_ge(m4_hbk, gi * (HF * CT) + (x * CT + CT))
            pe.wait_ge(m4_ek, k)
            pe.wait_ge(m4_ak, ak + 2)
            for q in range(2):
                for n in range(2):
                    last = nc.tensor.matmul(psum[:, q, :], m4_gt, m4_ar[:, n, 4 * q:4 * q + 4, :], start=(n == 0),
                                            stop=(n == 1))
            last.then_inc(m4_sp, 1)
            pe.wait_ge(m4_dk, k)
            pe.wait_ge(m4_ak, ak + 4)
            for i in range(4):
                for n in range(2):
                    last = nc.tensor.matmul(psum[:, 4, i * P:(i + 1) * P], m4_ab[:, n, i * P:(i + 1) * P], m4_le,
                                            start=(n == 0), stop=(n == 1))
            last.then_inc(m4_dd, 1)

        def to_tokens(pe, gi, x, c):
            k = gi * CG + (x * 4 + c + 1)
            tok = slice(c * P, (c + 1) * P)
            if c == 0:
                pe.wait_ge(m4_xk, gi * (HF * CT) + (x * CT + CT))
            pe.wait_ge(m4_sk, gi * (CG + 2) + (x * 4 + c + x // 2 + 2))
            for i in range(4):
                nc.tensor.transpose(psum[:, 6, i * P:(i + 1) * P], m4_xc[:, i, tok], ident[:, :])
            pe.wait_ge(m4_tk, k + 1)
            if c == 0:
                pe.wait_ge(m4_gk, gi * (HF * 4) + (x * 4 + 4))
            nc.tensor.transpose(psum[:, 3, 0:P], m4_xc[:, 4, tok], ident[:, :]).then_inc(m4_xp, 1)

        def chunk(pe, gi, x, c):
            k = gi * CG + (x * 4 + c + 1)
            tok = slice(c * P, (c + 1) * P)
            pe.wait_ge(m4_sk, gi * (CG + 2) + (x * 4 + c + x // 2 + 2))
            pe.wait_ge(m4_bk, k + 1)
            for i in range(4):
                last = nc.tensor.matmul(psum[:, 3, i * P:(i + 1) * P], m4_st[:, i * P:(i + 1) * P], m4_xc[:, 5, tok],
                                        start=True, stop=True)
            last.then_inc(m4_ii, 1)
            pe.wait_ge(m4_mk, k + 1)
            pe.wait_ge(m4_x2, gi * (2 * CG) + (2 * (x * 4 + c) + 1))
            pe.wait_ge(m4_yk, k)
            for i in range(HG):
                e = i % 2
                last = nc.tensor.matmul(psum[e * PS:(e + 1) * PS, 2, (i // 2) * P:(i // 2 + 1) * P],
                                        m4_x12[:, i * PS:(i + 1) * PS], m4_e[c % 2][:, i, :], start=True, stop=True)
            last.then_inc(m4_ia, 1)
            pe.wait_ge(m4_x2, gi * (2 * CG) + (2 * (x * 4 + c) + 2))
            nc.tensor.matmul(psum[:, 6, :], m4_bt, m4_x12[:, GF:], start=True, stop=True).then_inc(m4_sn, 1)

        def out_proj(pe, gi, x, c):
            k = gi * CG + (x * 4 + c + 1)
            ahead = gi * CG + (x * 4 + min(c + 2, 3) + 2)
            pe.wait_ge(m4_qk, k + 1)
            pe.wait_ge(m4_sdk, k)
            pe.wait_ge(m4_mk, ahead)
            for i in range(4):
                last = nc.tensor.matmul(psum[:, 7, 3 * P:3 * P + 1], m4_sq[:, i, :], m4_o32, start=(i == 0), stop=(i == 3))
            last.then_inc(m4_qp, 1)
            pe.wait_ge(m4_ylo, k + 1)
            pe.wait_ge(m4_ok, k)
            if x == 0 and c == 0:
                pe.wait_ge(m4_wlo, gi * QS + (QS + 2))
            for i in range(4):
                last = three(pe, psum[:, 5, :], m4_yh[:, i, :], m4_yl[:, i, :], m4_wh[:, i, IW:], m4_wl[:, i, IW:],
                             i == 0, i == 3)
            last.then_inc(m4_op, 1)

        def sp_l2_ffn(sp):
            arena_free(sp, 5)
            row = lambda n: A[n].rearrange("(o n) -> o n", o=1).broadcast_to([P, C])
            sp.dma_start(s5_raw[:, 0], A["w1T"].rearrange("(k p) n -> p k n", p=P)).then_inc(s5_in, 16)
            sp.dma_start(s5_raw[:, 1], A["w3T"].rearrange("(k p) n -> p k n", p=P)).then_inc(s5_in, 16)
            sp.dma_start(s5_s0, A["scaling0_p"]).then_inc(s5_in, 16)
            sp.dma_start(s5_s2, A["scaling2_p"]).then_inc(s5_in, 16)
            sp.dma_start(s5_s4, row("L2_ffn_scaling4")).then_inc(s5_in, 16)
            sp.dma_start(s5_b, row("L2_ffn_bias")).then_inc(s5_in, 16)

        def dve_l2_ffn(dve, ch):
            dve.wait_ge(s5_in, 96)
            ch.link(nc.vector.tensor_scalar(s5_w1, s5_raw[:, 0], 2.0, -1.0, ALU.mult, ALU.add))
            for k in range(KT):
                nc.vector.tensor_scalar(s5_w1[:, k, :], s5_w1[:, k, :], s5_s0[:, k:k + 1], WS, ALU.mult,
                                        ALU.mult).then_inc(s5_wf, 1)
            nc.vector.tensor_scalar(s5_w3, s5_raw[:, 1], 2.0, -1.0, ALU.mult, ALU.add).then_inc(s5_w, 1)
            nc.vector.tensor_scalar(s5_s4, s5_s4, 1.0 / ACTS, None, ALU.mult).then_inc(s5_w, 1)
            dve.wait_ge(s5_hi, 1)
            nc.vector.tensor_tensor(s5_w1l, s5_w1, s5_w1h, ALU.subtract).then_inc(s5_w, 1)
            s = 5 - start
            dve.wait_ge(s5_w, 2)
            with loop(dve, NG, (ch, 5 * GT)) as g:
                for f in range(KT):
                    dve.wait_ge(s5_hhi, g * KT + (f + 1))
                    nc.vector.scalar_tensor_tensor(out=s5_hl[:, f, :], in0=ps_g[:, f, :], scalar=s5_s2[:, f:f + 1],
                                                   in1=s5_hh[:, f, :], op0=ALU.mult,
                                                   op1=ALU.subtract).then_inc(s5_hlo, 1)

                def affine(j):
                    dve.wait_ge(s5_p, g * GT + (j + 1))
                    ch.link(nc.vector.tensor_tensor(s5_y[:, j % 2, :], ps_y[:, j % 2, :], s5_s4, ALU.mult))
                    nc.vector.tensor_tensor(s5_y[:, j % 2, :], s5_y[:, j % 2, :], s5_b, ALU.add).then_inc(y_ready, 1)
                dve_group(dve, ch, s, g, y=lambda j: s5_y[:, j % 2, :], before=affine)

        def act_l2_ffn(act):
            act.wait_ge(s5_wf, KT)
            nc.scalar.activation(s5_w1h, s5_w1, ACT.Copy).then_inc(s5_hi, 1)
            s = 5 - start
            with act.Fori(0, NG) as g:
                for f in range(KT):
                    act.wait_ge(s5_h, g * KT + (f + 1))
                    nc.scalar.activation(s5_hh[:, f, :], ps_g[:, f, :], ACT.Copy,
                                         scale=s5_s2[:, f:f + 1]).then_inc(s5_hhi, 1)
                act_group(act, s, g, epsc[:, 0:1], y=lambda j: s5_y[:, j % 2, :])

        def pe_l2_ffn(pe):
            pe.wait_ge(s5_w, 3)
            s = 5 - start
            with pe.Fori(0, NG) as g:
                pe.wait_ge(xt_ok, g * GT + (NT * s + GT))
                for f in range(KT):
                    for k in range(KT):
                        fc = slice(f * P, (f + 1) * P)
                        last = three(pe, ps_g[:, f, :], s5_w1h[:, k, fc], s5_w1l[:, k, fc],
                                     xt_hi[:, k, ds(g * GW, GW)], xt_lo[:, k, ds(g * GW, GW)], k == 0, k == KT - 1)
                    last.then_inc(s5_h, 1)

                def y_tile(j):
                    r = g * GT + (NT * (s - yb) + j)
                    if j >= 2:
                        pe.wait_ge(y_ready, r - 1)
                    tok = slice(j * P, (j + 1) * P)
                    for k in range(KT):
                        if j == 0:
                            pe.wait_ge(s5_hlo, g * KT + (k + 1))
                        nc.tensor.matmul(ps_y[:, j % 2, :], s5_hh[:, k, tok], s5_w3[:, k, :], start=(k == 0), stop=False)
                        last = nc.tensor.matmul(ps_y[:, j % 2, :], s5_hl[:, k, tok], s5_w3[:, k, :], start=False,
                                                stop=(k == KT - 1))
                    last.then_inc(s5_p, 1)
                pe_group(pe, s, g, y_tile)

        def sp_l3_ffn(sp):
            arena_free(sp, 7)
            sp.dma_start(sh7, A["shifts"]).then_inc(sh7_in, 16)
            for i, (m, k, rows) in enumerate(pieces7):
                name, _, _, w = mats7[m]
                if i >= 2:
                    sp.wait_ge(q7_done, i - 1)
                qw = A[f"L3_ffn_{name}_qweight"]
                for j in range(8):
                    sp.dma_start(q7[j:rows * 8:8, i % 2, 0:w], qw[16 * k:16 * k + rows, :]).then_inc(q7_in[i % 2], 16)
                if i:
                    sp.wait_ge(w7_f, i)
                sp.dma_start(z7p[:, 0:w // 8], A[f"L3_ffn_{name}_zeros"][k:k + 1, :].broadcast_to([P, w // 8])).then_inc(z7_in, 16)
                sp.dma_start(s7[:, 0:w], A[f"L3_ffn_{name}_scales"][k:k + 1, :].broadcast_to([P, w])).then_inc(z7_in, 16)

        def dve_l3_ffn(dve, ch):
            for t in (g7h, g7l, u7h, u7l):
                nc.vector.memset(t[:, :, INTER:FW3], 0.0).then_inc(w7_l, 1)
            for t in (d7h, d7l):
                nc.vector.memset(t[96:P, F3 - 1, :], 0.0).then_inc(w7_l, 1)
            dve.wait_ge(sh7_in, 16)
            for i, (m, k, rows) in enumerate(pieces7):
                _, h_, l_, w = mats7[m]
                n = rows * 8
                word = q7[0:n, i % 2, 0:w]
                dve.wait_ge(z7_in, 32 * (i + 1))
                for j in range(8):
                    v = nc.vector.tensor_scalar(z7[:, 0:w // 8, j], z7p[:, 0:w // 8], 4 * j, 15, ALU.logical_shift_right,
                                                ALU.bitwise_and)
                ch.mark(v)
                dve.wait_ge(q7_in[i % 2], 128 * (i // 2 + 1))
                ch.link(nc.vector.tensor_scalar(word, word, sh7[0:n, :], 15, ALU.logical_shift_right, ALU.bitwise_and))
                if i:
                    dve.wait_ge(w7_l, 6 + i)
                z = z7[0:n, 0:w // 8, :].rearrange("p a b -> p (a b)")
                nc.vector.scalar_tensor_tensor(out=w7[0:n, 0:w], in0=word, scalar=1.0, in1=z, op0=ALU.subtract,
                                               op1=ALU.subtract).then_inc(q7_done, 1)
                dve.wait_ge(q7_done, i + 1)
                nc.vector.scalar_tensor_tensor(out=w7[0:n, 0:w], in0=w7[0:n, 0:w], scalar=WS, in1=s7[0:n, 0:w],
                                               op0=ALU.mult, op1=ALU.mult).then_inc(w7_f, 1)
                dve.wait_ge(w7_h, i + 1)
                nc.vector.tensor_tensor(l_[0:n, k, 0:w], w7[0:n, 0:w], h_[0:n, k, 0:w], ALU.subtract).then_inc(w7_l, 1)
            dve_ffn(dve, ch, 7 - start, F3, hid7h, hid7l, F0 * NG if on(1) else 0, sg7, hd7,
                    y=lambda j: y7[:, j % 2, :], last_layer=True)

        def act_l3_ffn(act):
            for i, (m, k, rows) in enumerate(pieces7):
                _, h_, l_, w = mats7[m]
                n = rows * 8
                act.wait_ge(w7_f, i + 1)
                nc.scalar.activation(h_[0:n, k, 0:w], w7[0:n, 0:w], ACT.Copy).then_inc(w7_h, 1)

            def to_f16(g):
                def go(j):
                    act.wait_ge(p7_y, g * GT + (j + 1))
                    if j >= 2:
                        act.wait_ge(y_norm, g * GT + (NT * (7 - start - yb) + j - 1))
                    nc.scalar.activation(y7[:, j % 2, :], ps_y[:, j % 2, :], ACT.Copy,
                                         scale=1.0 / (WS * ACTS)).then_inc(y_ready, 1)
                return go
            act_ffn(act, 7 - start, F3, hid7h, F0 * NG if on(1) else 0, epsc[:, 0:1], sg7, hd7,
                    y=lambda j: y7[:, j % 2, :], last_layer=True, before=to_f16)

        def pe_l3_ffn(pe):
            pe_ffn(pe, 7 - start, F3, g7h, g7l, u7h, u7l, d7h, d7l, hid7h, hid7l, w7_l, 6 + len(pieces7),
                   F0 * NG if on(1) else 0, done=p7_y, last_layer=True)

        def sp_l3_attn(sp):
            arena_free(sp, 6)
            row = lambda n, a, w: A[n][a:a + w].rearrange("(o n) -> o n", o=1).broadcast_to([P, w])
            sp.dma_start(a6_raw, A["L3_attn_Wqkv"].rearrange("(k p) n -> p k n", p=P)).then_inc(a6_in, 16)
            sp.dma_start(a6_rwo, A["L3_attn_Wo"]).then_inc(a6_in, 16)
            sp.dma_start(a6_b, A["bqk_p"]).then_inc(a6_in, 16)
            sp.dma_start(a6_bv, row("L3_attn_bqkv", 2 * D3, D3)).then_inc(a6_in, 16)
            sp.dma_start(a6_bo, row("L3_attn_bo", 0, C)).then_inc(a6_in, 16)

        def dve_l3_attn(dve, ch):
            s = 6 - start
            dve.wait_ge(a6_who, 2)
            nc.vector.scalar_tensor_tensor(out=a6_wl, in0=a6_raw, scalar=WS, in1=a6_wh, op0=ALU.mult,
                                           op1=ALU.subtract).then_inc(a6_wok, 1)
            nc.vector.scalar_tensor_tensor(out=a6_ol, in0=a6_rwo, scalar=WS, in1=a6_oh, op0=ALU.mult,
                                           op1=ALU.subtract).then_inc(a6_wok, 1)
            dve.sem_inc(a6_pf, 1)
            with loop(dve, NG, (ch, 0)) as g:
                for f in range(3):
                    i = g * 3 + f
                    dve.wait_ge(a6_pp, i + 1)
                    if f < 2:
                        nc.vector.tensor_scalar(a6_qk[:, f, :], ps_g[:, f, :], 1.0 / WS, a6_b[:, f:f + 1], ALU.mult,
                                                ALU.add).then_inc(a6_pf, 1)
                        dve.wait_ge(a6_pho, i + 1)
                        nc.vector.tensor_tensor(a6_ql[:, f, ds(g * GW, GW)], a6_qk[:, f, :],
                                                a6_qh[:, f, ds(g * GW, GW)], ALU.subtract).then_inc(a6_plo, 1)
                    else:
                        nc.vector.scalar_tensor_tensor(out=a6_v, in0=ps_g[:, f, :].rearrange("p (j d) -> p j d", j=GT),
                                                       scalar=1.0 / WS, in1=a6_bv.unsqueeze(1).broadcast_to([P, GT, D3]),
                                                       op0=ALU.mult, op1=ALU.add).then_inc(a6_pf, 1)
                        dve.wait_ge(a6_pho, i + 1)
                        nc.vector.tensor_tensor(a6_vl[:, ds(g * GT, GT), :], a6_v, a6_vh[:, ds(g * GT, GT), :],
                                                ALU.subtract).then_inc(a6_plo, 1)
            with loop(dve, NG, (ch, 6 * GT)) as g:
                def maximum(j):
                    i = g * GT + j
                    b = 2 * (j % 2)
                    dve.wait_ge(a6_s, i + 1)
                    ch.link(nc.vector.tensor_reduce(a6_mx[:, j % 2, 0:1], ps_g[:, b:b + 2, :].rearrange("p a b -> p (a b)"),
                                                    AXX, ALU.max))
                    nc.vector.tensor_scalar(a6_mx[:, j % 2, 1:2], a6_mx[:, j % 2, 0:1], -SC6, None,
                                            ALU.mult).then_inc(a6_m, 1)

                def attend(j):
                    i = g * GT + j
                    if j == 0:
                        maximum(0)
                    if j < GT - 1:
                        maximum(j + 1)
                    dve.wait_ge(a6_tho, i + 1)
                    nc.vector.tensor_tensor(a6_pl.rearrange("p a b -> p (a b)"), psum[:, 6:8, :].rearrange("p a b -> p (a b)"),
                                            a6_ph.rearrange("p a b -> p (a b)"), ALU.subtract).then_inc(a6_tlo, 1)
                    dve.wait_ge(a6_oho, i + 1)
                    nc.vector.tensor_tensor(a6_tl, ps_y[:, 1, 0:P], a6_th, ALU.subtract).then_inc(a6_olo, 1)
                    dve.wait_ge(a6_e, i + 2)
                    nc.vector.reciprocal(a6_mx[:, j % 2, 3:4], a6_mx[:, j % 2, 2:3]).then_inc(dve_seq, 1)
                    ch.add()
                    ch.wait(ch())
                    nc.vector.tensor_scalar(a6_mx[:, j % 2, 1:2], a6_mx[:, j % 2, 3:4], 1.0 / WS, None,
                                            ALU.mult).then_inc(a6_inv, 1)
                    dve.wait_ge(a6_inv, i + 1)
                    dve.wait_ge(a6_yp, i + 1)
                    nc.vector.scalar_tensor_tensor(out=a6_y[:, j % 2, :], in0=ps_y[:, 0, :], scalar=a6_mx[:, j % 2, 1:2],
                                                   in1=a6_bo, op0=ALU.mult, op1=ALU.add).then_inc(y_ready, 1)
                dve_group(dve, ch, s, g, y=lambda j: a6_y[:, j % 2, :], before=attend)

        def act_l3_attn(act):
            s = 6 - start
            act.wait_ge(a6_in, 80)
            nc.scalar.activation(a6_wh, a6_raw, ACT.Copy, scale=WS).then_inc(a6_who, 1)
            nc.scalar.activation(a6_oh, a6_rwo, ACT.Copy, scale=WS).then_inc(a6_who, 1)
            act.sem_inc(a6_e, 1)
            with act.Fori(0, NG) as g:
                for f in range(3):
                    act.wait_ge(a6_pf, g * 3 + (f + 2))
                    if f < 2:
                        nc.scalar.activation(a6_qh[:, f, ds(g * GW, GW)], a6_qk[:, f, :], ACT.Copy).then_inc(a6_pho, 1)
                    else:
                        nc.scalar.activation(a6_vh[:, ds(g * GT, GT), :], a6_v, ACT.Copy).then_inc(a6_pho, 1)
            with act.Fori(0, NG) as g:
                def exps(j):
                    b = 2 * (j % 2)
                    act.wait_ge(a6_m, g * GT + (j + 1))
                    nc.scalar.activation(a6_p[:, j % 2, :], ps_g[:, b:b + 2, :].rearrange("p a b -> p (a b)"), ACT.Exp,
                                         bias=a6_mx[:, j % 2, 1:2], scale=SC6,
                                         accum_out=a6_mx[:, j % 2, 2:3]).then_inc(a6_e, 1)

                def attend(j):
                    i = g * GT + j
                    if j == 0:
                        exps(0)
                    if j < GT - 1:
                        exps(j + 1)
                    act.wait_ge(a6_t, i + 1)
                    nc.scalar.activation(a6_ph.rearrange("p a b -> p (a b)"), psum[:, 6:8, :].rearrange("p a b -> p (a b)"),
                                         ACT.Copy).then_inc(a6_tho, 1)
                    act.wait_ge(a6_o, i + 1)
                    nc.scalar.activation(a6_th, ps_y[:, 1, 0:P], ACT.Copy).then_inc(a6_oho, 1)
                act_group(act, s, g, epsc[:, 0:1], y=lambda j: a6_y[:, j % 2, :], before=attend)

        def pe_l3_attn(pe):
            s = 6 - start
            pe.wait_ge(a6_wok, 2)
            with pe.Fori(0, NG) as g:
                pe.wait_ge(xt_ok, g * GT + (NT * s + GT))
                pe.wait_ge(a6_pf, g * 3 + 1)
                for f in range(2):
                    for k in range(KT):
                        fc = slice(f * D3, (f + 1) * D3)
                        last = three(pe, ps_g[:, f, :], a6_wh[:, k, fc], a6_wl[:, k, fc], xt_hi[:, k, ds(g * GW, GW)],
                                     xt_lo[:, k, ds(g * GW, GW)], k == 0, k == KT - 1)
                    last.then_inc(a6_pp, 1)
                for j in range(GT):
                    tok = ds(g * GW + j * P, P)
                    for k in range(KT):
                        last = three(pe, ps_g[:, 2, j * D3:(j + 1) * D3], xt_hi[:, k, tok], xt_lo[:, k, tok],
                                     a6_wh[:, k, 2 * D3:], a6_wl[:, k, 2 * D3:], k == 0, k == KT - 1)
                last.then_inc(a6_pp, 1)
            pe.wait_ge(a6_plo, 3 * NG)
            for b in range(NB):
                with pe.Fori(0, NG // NB) as gb:
                    g = gb + b * (NG // NB)

                    def scores(j):
                        i = g * GT + j
                        bank = 2 * (j % 2)
                        tok = ds(g * GW + j * P, P)
                        for half in range(2):
                            keys = slice(b * S6 + half * 512, b * S6 + (half + 1) * 512)
                            last = three(pe, ps_g[:, bank + half, :], a6_qh[:, 0, tok], a6_ql[:, 0, tok],
                                         a6_qh[:, 1, keys], a6_ql[:, 1, keys], True, True)
                        last.then_inc(a6_s, 1)

                    def y_tile(j):
                        i = g * GT + j
                        if j == 0:
                            pe.wait_ge(a6_e, i + 1)
                            scores(0)
                        if j < GT - 1:
                            pe.wait_ge(a6_e, i + 1)
                            scores(j + 1)
                        pe.wait_ge(a6_e, i + 2)
                        pe.wait_ge(xt_ok, g * GT + (NT * (s + 1) + (0 if j == 0 else j - 1)))
                        for k in range(TPB):
                            last = nc.tensor.transpose(psum[:, 6 + k // 4, (k % 4) * P:(k % 4 + 1) * P],
                                                       a6_p[:, j % 2, k * P:(k + 1) * P], ident[:, :])
                        last.then_inc(a6_t, 1)
                        pe.wait_ge(a6_tlo, i + 1)
                        for k in range(TPB):
                            last = three(pe, ps_y[:, 1, 0:P], a6_vh[:, b * TPB + k, :], a6_vl[:, b * TPB + k, :],
                                         a6_ph[:, k, :], a6_pl[:, k, :], k == 0, k == TPB - 1)
                        last.then_inc(a6_o, 1)
                        pe.wait_ge(a6_olo, i + 1)
                        last = three(pe, ps_y[:, 0, :], a6_th, a6_tl, a6_oh, a6_ol, True, True)
                        last.then_inc(a6_yp, 1)
                    pe_group(pe, s, g, y_tile)

        block = ctx.enter_context(nc.Block())

        @block.sync
        def _(sp):
            sp_x(sp)
            if on(0):
                sp_l0_attn(sp)
            if on(1):
                sp_l0_ffn(sp)
            if on(2):
                sp_l1_attn(sp)
            if on(3):
                sp_l1_ffn(sp)
            if on(4):
                sp_l2_attn(sp)
            if on(5):
                sp_l2_ffn(sp)
            if on(6):
                sp_l3_attn(sp)
            if on(7):
                sp_l3_ffn(sp)
            sp_out(sp)

        @block.gpsimd
        def _(pool):
            ch = Chain(pool, pool_seq)
            pool_consts(pool, ch)
            if on(1):
                pool_l0_ffn(pool)
            if on(4):
                pool_l2_attn(pool)

        @block.tensor
        def _(pe):
            pe_x0(pe)
            if on(0):
                pe_l0_attn(pe)
            if on(1):
                pe_l0_ffn(pe)
            if on(2):
                pe_l1_attn(pe)
            if on(3):
                pe_l1_ffn(pe)
            if on(4):
                pe_l2_attn(pe)
            if on(5):
                pe_l2_ffn(pe)
            if on(6):
                pe_l3_attn(pe)
            if on(7):
                pe_l3_ffn(pe)

        @block.scalar
        def _(act):
            ch = Chain(act, act_seq)
            act_x0(act)
            if on(0):
                act_l0_attn(act, ch)
            if on(1):
                act_l0_ffn(act)
            if on(2):
                act_l1_attn(act)
            if on(3):
                act_l1_ffn(act)
            if on(4):
                act_l2_attn(act)
            if on(5):
                act_l2_ffn(act)
            if on(6):
                act_l3_attn(act)
            if on(7):
                act_l3_ffn(act)

        @block.vector
        def _(dve):
            ch = Chain(dve, dve_seq)
            dve_x0(dve, ch)
            if on(0):
                dve_l0_attn(dve, ch)
            if on(1):
                dve_l0_ffn(dve, ch)
            if on(2):
                dve_l1_attn(dve, ch)
            if on(3):
                dve_l1_ffn(dve, ch)
            if on(4):
                dve_l2_attn(dve, ch)
            if on(5):
                dve_l2_ffn(dve, ch)
            if on(6):
                dve_l3_attn(dve, ch)
            if on(7):
                dve_l3_ffn(dve, ch)



def constants():
    h = np.arange(1, 33)
    slope = (2.0 ** -0.25) ** h
    slope = slope.astype(np.float32)
    hi = slope.astype(np.float16)
    lo = (slope - hi.astype(np.float32)).astype(np.float16)
    pos = (np.arange(1024) - 512).astype(np.float16)
    above = np.triu(np.ones((P, P), np.float16), 1) * np.float16(-30000)
    return {
        "alibi_q": np.ascontiguousarray(np.broadcast_to(np.stack([hi, lo])[:, :, None], (2, 32, 1024))),
        "alibi_k": np.stack([pos, pos, np.ones(1024, np.float16)]),
        "ident16": np.eye(P, dtype=np.float16),
        "mask_qk": above, "mask_kq": np.ascontiguousarray(above.T),
        "tri_le": np.triu(np.ones((P, P), np.float16)), "tri_gt": np.tril(np.ones((P, P), np.float16), -1),
        "ones16": np.ones((P, P), np.float16),
        "shifts": (np.arange(P, dtype=np.int32) % 8 * 4).reshape(P, 1),
    }


def l2_attn_arrays(i):
    w, wo = np.asarray(i["L2_attn_in_proj_w"]), np.asarray(i["L2_attn_out_proj_w"])
    inner = wo.shape[1]
    n = w.shape[1]
    gs = inner // n
    bc = (w.shape[0] - 2 * inner) // (2 * gs)
    bc -= bc % P
    gate, xw = w[:inner], w[inner:2 * inner]
    bw, cw = w[2 * inner:2 * inner + gs * bc], w[2 * inner + gs * bc:2 * inner + 2 * gs * bc]
    cwt, cb = np.asarray(i["L2_attn_conv_weight"]), np.asarray(i["L2_attn_conv_bias"])
    nw = np.asarray(i["L2_attn_norm_weight"])
    d = np.repeat(np.asarray(i["L2_attn_D"]), inner // np.asarray(i["L2_attn_D"]).shape[0])
    ws, ps = [], []
    for g in range(gs):
        f, e = slice(g * n, (g + 1) * n), slice(g * bc, (g + 1) * bc)
        m = np.concatenate([xw[f], bw[e], cw[e], gate[f]]).T
        ws.append(m.reshape(n // P, P, 2, -1).transpose(0, 2, 1, 3).reshape(-1, P, m.shape[1] // 2))
        pick = lambda v: np.concatenate([v[:inner][f], v[inner:inner + gs * bc][e], v[inner + gs * bc:][e]])
        taps = pick(cwt).reshape(-1, P, cwt.shape[1]).transpose(1, 0, 2).reshape(P, -1)
        ps.append(np.concatenate([taps, pick(cb).reshape(-1, P).T, d[f].reshape(-1, P).T, nw[f].reshape(-1, P).T],
                                 axis=1))
    dt = w[2 * inner + 2 * gs * bc:].T.reshape(n // P, P, -1).transpose(1, 0, 2)
    ws.append(np.zeros_like(ws[0]))
    return {"m4_wi": np.ascontiguousarray(np.stack(ws)),
            "m4_wo": np.ascontiguousarray(wo.T.reshape(gs, n // P, P, -1)),
             "m4_par": np.ascontiguousarray(np.stack(ps, axis=1)),
            "m4_dt": np.ascontiguousarray(dt), "L2_attn_dt_bias": i["L2_attn_dt_bias"],
            "L2_attn_A_log": i["L2_attn_A_log"]}


def lay_out(i):
    t = lambda a: np.ascontiguousarray(np.asarray(a).T)
    cols = lambda a: np.ascontiguousarray(np.asarray(a).reshape(-1, P).T)
    return {
        "L0_attn_x": i["L0_attn_x"], "L0_attn_Wq": i["L0_attn_Wq"], "L0_attn_bq": i["L0_attn_bq"],
        "L0_attn_Wk": i["L0_attn_Wk"], "L0_attn_bk": i["L0_attn_bk"], "L0_attn_Wv": i["L0_attn_Wv"],
        "L0_attn_bv": i["L0_attn_bv"],
        "gate_wT": t(i["L0_ffn_gate_w"]), "gate_suT": t(i["L0_ffn_gate_su"]), "gate_sv": i["L0_ffn_gate_sv"],
        "up_wT": t(i["L0_ffn_up_w"]), "up_suT": t(i["L0_ffn_up_su"]), "up_sv": i["L0_ffn_up_sv"],
        "L1_ffn_sign": i["L1_ffn_sign"], "L1_ffn_scale": np.asarray(i["L1_ffn_scale"]).reshape(1, 1),
        "w1T": t(i["L2_ffn_w1_bits"]), "w3T": t(i["L2_ffn_w3_bits"]),
        **{k: i[k] for k in ("L2_ffn_scaling0", "L2_ffn_scaling2", "L2_ffn_scaling4", "L2_ffn_bias", "L3_attn_Wqkv",
                             "L3_attn_bqkv", "L3_attn_Wo", "L3_attn_bo")},
        **{f"L3_ffn_{m}_{w}": i[f"L3_ffn_{m}_{w}"] for m in ("gate", "up", "down")
           for w in ("qweight", "scales", "zeros")},
        "scaling0_p": cols(i["L2_ffn_scaling0"]), "scaling2_p": cols(i["L2_ffn_scaling2"]),
        "bqk_p": cols(np.asarray(i["L3_attn_bqkv"])[:C // 2]),
        "L1_attn_Wqkv": i["L1_attn_Wqkv"], "L1_attn_Wo": i["L1_attn_Wo"],
        **constants(), **l2_attn_arrays(i),
        "down_wT": t(i["L0_ffn_down_w"]), "down_suT": t(i["L0_ffn_down_su"]), "down_sv": i["L0_ffn_down_sv"],
    }


def kernel(**inputs):
    import concourse.bacc as bacc
    from concourse.bass_utils import run_bass_kernel_spmd

    nc = bacc.Bacc("TRN2", target_bir_lowering=False, num_devices=1)
    arrays = {k: np.ascontiguousarray(v) for k, v in lay_out(inputs).items()}
    A = {k: nc.dram_tensor(k, a.shape, mybir.dt.from_np(a.dtype), kind="ExternalInput").ap()
         for k, a in arrays.items()}
    A["out"] = nc.dram_tensor("out", (2, 1024, 512), F32, kind="ExternalOutput").ap()
    build(nc, A)
    return run_bass_kernel_spmd(nc, [arrays], core_ids=[0]).results[0]["out"]
```

```python
from contextlib import ExitStack, contextmanager

import numpy as np

import concourse.bass as bass
from concourse import mybir

F32 = mybir.dt.float32
F16 = mybir.dt.float16
I32 = mybir.dt.int32
ALU = mybir.AluOpType
ACT = mybir.ActivationFunctionType
AXX = mybir.AxisListType.X
ds = bass.ds

P = 128
TOK = 2048
NT = TOK // P
NB = 2
TPB = NT // NB
NG = 4
GT = NT // NG
GW = GT * P
C = 512
KT = C // P
EPS = 1e-5
WS = 64.0
ACTS = 64.0

H0, D0 = 32, 16
F0 = 1792 // P
RANK = 4


class Tally:

    def __init__(self, base=0):
        self.base, self.off = base, 0

    def add(self, n=1):
        self.off += n

    def __call__(self, more=0):
        return self.base + (self.off + more)


class Chain(Tally):

    def __init__(self, eng, sem):
        super().__init__()
        self.eng, self.sem = eng, sem

    def mark(self, ins):
        ins.then_inc(self.sem, 1)
        self.add()
        return self()

    def wait(self, value):
        self.eng.wait_ge(self.sem, value)

    def link(self, ins, alone=None):
        self.wait(self.mark(ins))
        if alone:
            alone(self.eng)


@contextmanager
def loop(eng, n, *tallies):
    outside = [(t.base, t.off) for t, _ in tallies]
    with eng.Fori(0, n) as i:
        for (t, per), (base, off) in zip(tallies, outside):
            t.base, t.off = i * per + base + off if per else base + off, 0
        yield i
        for t, per in tallies:
            assert t.off == per, (t.off, per)
    for (t, per), (base, off) in zip(tallies, outside):
        t.base, t.off = base, off + n * per


def build(nc, A, start=0, stop=8):
    yb = 1 if start == 0 else 0
    ctx = ExitStack()
    with ctx:
        def sb(name, shape, dt):
            return ctx.enter_context(nc.sbuf_tensor(name, shape, dt))

        def sem(name):
            return ctx.enter_context(nc.semaphore(name))

        x = sb("x", [P, NT, C], F32)
        xt_hi = sb("xt_hi", [P, KT, TOK], F16)
        xt_lo = sb("xt_lo", [P, KT, TOK], F16)
        ident = sb("ident", [P, P], F32)
        tmp = sb("tmp", [P, 2, C], F32)
        xn = sb("xn", [P, 2, C], F32)
        st6 = sb("st6", [P, 2, 2, 6], F32)
        mv = sb("mv", [P, 2, 2, 2], F32)
        rs = sb("rs", [P, 2, 2, 2], F32)
        sd = sb("sd", [P, 2, 2], F32)
        epsc = sb("epsc", [P, 8], F32)
        arena = sb("arena", [P, 34213], F32)

        def carve(at, shape, dt):
            n = int(np.prod(shape))
            words = n if dt in (F32, I32) else n // 2
            v = arena[:, at // 4:at // 4 + words]
            if dt is not F32:
                v = v.bitcast(dt)
            if len(shape) > 1:
                names = "abcd"[:len(shape)]
                v = v.rearrange(f"p ({' '.join(names)}) -> p {' '.join(names)}",
                                **{k: s for k, s in zip(names[1:], shape[1:])})
            return v

        psum = ctx.enter_context(nc.psum_tensor("psum", [P, 8, 512], F32))
        ps_g = psum[:, 0:4, :]
        ps_y = psum[:, 4:6, :]
        ps_t = psum[:, 6, :].rearrange("p (k c) -> p k c", k=4)
        ps_m = psum[:, 7, :]

        act_seq, dve_seq, pool_seq = sem("act_seq"), sem("dve_seq"), sem("pool_seq")

        y_ready = sem("y_ready")
        y_mv = sem("y_mv")
        y_sd = sem("y_sd")
        y_rs = sem("y_rs")
        y_norm = sem("y_norm")
        x_new = sem("x_new")
        x_mv = sem("x_mv")
        x_sd = sem("x_sd")
        x_rs = sem("x_rs")
        x_norm = sem("x_norm")
        x_tr = sem("x_tr")
        xt_h = sem("xt_h")
        xt_ok = sem("xt_ok")

        x_in = [sem(f"x_in{q}") for q in range(4)]
        x_out = sem("x_out")
        consts_ok = sem("consts_ok")
        passed = sem("passed")

        def alone(eng):
            eng.sem_inc(passed, 1)

        class Tail:

            @staticmethod
            def dve_y_stats(dve, ch, r, j, y):
                dve.wait_ge(y_ready, r + 1)
                ch.link(nc.vector.bn_stats(st6[:, 0, j % 2, :], y), alone)
                nc.vector.bn_aggr(mv[:, 0, j % 2, :], st6[:, 0, j % 2, :]).then_inc(y_mv, 1)

            @staticmethod
            def act_y_sd(act, r, j, eps):
                act.wait_ge(y_mv, r + 1)
                nc.scalar.activation(sd[:, 0, j % 2:j % 2 + 1], mv[:, 0, j % 2, 1:2], ACT.Sqrt,
                                     bias=eps).then_inc(y_sd, 1)

            @staticmethod
            def dve_y_scale(dve, ch, r, j):
                q = j % 2
                dve.wait_ge(y_sd, r + 1)
                ch.link(nc.vector.reciprocal(rs[:, 0, q, 0:1], sd[:, 0, q:q + 1]))
                nc.vector.tensor_scalar(rs[:, 0, q, 1:2], mv[:, 0, q, 0:1], -1.0, rs[:, 0, q, 0:1],
                                        ALU.mult, ALU.mult).then_inc(y_rs, 1)

            @staticmethod
            def act_y_norm(act, r, j, y):
                q = j % 2
                act.wait_ge(y_rs, r + 1)
                nc.scalar.activation(tmp[:, q, :], y, ACT.Identity, bias=rs[:, 0, q, 1:2],
                                     scale=rs[:, 0, q, 0:1]).then_inc(y_norm, 1)

            @staticmethod
            def dve_add(dve, r, t, j):
                dve.wait_ge(y_norm, r + 1)
                nc.vector.tensor_tensor(x[:, t, :], x[:, t, :], tmp[:, j % 2, :], ALU.add).then_inc(x_new, 1)

            @staticmethod
            def dve_x_stats(dve, ch, r, n, t, j):
                if r is not None:
                    dve.wait_ge(x_new, r + 1)
                    alone(dve)
                ch.link(nc.vector.bn_stats(st6[:, 1, j % 2, :], x[:, t, :]), alone)
                nc.vector.bn_aggr(mv[:, 1, j % 2, :], st6[:, 1, j % 2, :]).then_inc(x_mv, 1)

            @staticmethod
            def act_x_sd(act, n, j):
                act.wait_ge(x_mv, n + 1)
                nc.scalar.activation(sd[:, 1, j % 2:j % 2 + 1], mv[:, 1, j % 2, 1:2], ACT.Sqrt,
                                     bias=epsc[:, 0:1]).then_inc(x_sd, 1)

            @staticmethod
            def dve_x_scale(dve, ch, n, j):
                q = j % 2
                dve.wait_ge(x_sd, n + 1)
                ch.link(nc.vector.reciprocal(rs[:, 1, q, 0:1], sd[:, 1, q:q + 1]))
                nc.vector.tensor_scalar(rs[:, 1, q, 1:2], mv[:, 1, q, 0:1], -1.0, rs[:, 1, q, 0:1],
                                        ALU.mult, ALU.mult).then_inc(x_rs, 1)

            @staticmethod
            def act_x_norm(act, n, t, j):
                q = j % 2
                act.wait_ge(x_rs, n + 1)
                nc.scalar.activation(xn[:, q, :], x[:, t, :], ACT.Identity, bias=rs[:, 1, q, 1:2],
                                     scale=rs[:, 1, q, 0:1]).then_inc(x_norm, 1)

            @staticmethod
            def dve_x(dve, ch, r, n, t, j):
                Tail.dve_x_stats(dve, ch, r, n, t, j)
                Tail.dve_x_scale(dve, ch, n, j)

            @staticmethod
            def act_x(act, n, t, j):
                Tail.act_x_sd(act, n, j)
                Tail.act_x_norm(act, n, t, j)

            @staticmethod
            def pe_x(pe, n, j, first=False):
                pe.wait_ge(x_norm, n + 1)
                if not first:
                    pe.wait_ge(xt_ok, n)
                for k in range(KT):
                    last = nc.tensor.transpose(ps_t[:, k, :], xn[:, j % 2, k * P:(k + 1) * P], ident[:, :])
                last.then_inc(x_tr, 1)

            @staticmethod
            def act_hi(act, n, t):
                act.wait_ge(x_tr, n + 1)
                nc.scalar.activation(xt_hi[:, :, ds(t * P, P)], ps_t[:, :, :], ACT.Copy).then_inc(xt_h, 1)

            @staticmethod
            def dve_lo(dve, n, t):
                dve.wait_ge(xt_h, n + 1)
                nc.vector.tensor_tensor(xt_lo[:, :, ds(t * P, P)], ps_t[:, :, :], xt_hi[:, :, ds(t * P, P)],
                                        ALU.subtract).then_inc(xt_ok, 1)

        def y_psum(j):
            return ps_y[:, j % 2, :]

        def dve_group(dve, ch, s, g, y=y_psum, last_layer=False, before=None, tiles=GT):
            for j in range(tiles + 1):
                i = g * tiles + j
                r, n = i + NT * (s - yb), i + NT * (s + 1)
                if j < tiles:
                    if before:
                        before(j)
                    Tail.dve_y_stats(dve, ch, r, j, y(j))
                if j:
                    Tail.dve_add(dve, r - 1, i - 1, j - 1)
                    if not last_layer:
                        Tail.dve_x_stats(dve, ch, r - 1, n - 1, i - 1, j - 1)
                if j < tiles:
                    Tail.dve_y_scale(dve, ch, r, j)
                if j and not last_layer:
                    Tail.dve_x_scale(dve, ch, n - 1, j - 1)
                if j >= 2 and not last_layer:
                    Tail.dve_lo(dve, n - 2, i - 2)
            if not last_layer:
                Tail.dve_lo(dve, n - 1, i - 1)

        def act_group(act, s, g, eps, y=y_psum, last_layer=False, before=None, tiles=GT):
            for j in range(tiles + 1):
                i = g * tiles + j
                r, n = i + NT * (s - yb), i + NT * (s + 1)
                if j < tiles:
                    if before:
                        before(j)
                    Tail.act_y_sd(act, r, j, eps)
                if j and not last_layer:
                    Tail.act_x_sd(act, n - 1, j - 1)
                if j < tiles:
                    Tail.act_y_norm(act, r, j, y(j))
                if j and not last_layer:
                    Tail.act_x_norm(act, n - 1, i - 1, j - 1)
                if j >= 2 and not last_layer:
                    Tail.act_hi(act, n - 2, i - 2)
            if not last_layer:
                Tail.act_hi(act, n - 1, i - 1)

        def dve_group_apart(dve, ch, s, g, y, before):
            for j in range(GT):
                before(j)
                i = g * GT + j
                r, n = i + NT * (s - yb), i + NT * (s + 1)
                Tail.dve_y_stats(dve, ch, r, j, y(j))
                Tail.dve_y_scale(dve, ch, r, j)
                Tail.dve_add(dve, r, i, j)
                Tail.dve_x(dve, ch, r, n, i, j)
                if j:
                    Tail.dve_lo(dve, n - 1, i - 1)
            Tail.dve_lo(dve, n, i)

        def act_group_apart(act, s, g, eps, y, before):
            for j in range(GT):
                before(j)
                i = g * GT + j
                r, n = i + NT * (s - yb), i + NT * (s + 1)
                Tail.act_y_sd(act, r, j, eps)
                Tail.act_y_norm(act, r, j, y(j))
                Tail.act_x(act, n, i, j)
                if j:
                    Tail.act_hi(act, n - 1, i - 1)
            Tail.act_hi(act, n, i)

        def pe_group(pe, s, g, y_tile, last_layer=False, late=2, tiles=GT):
            for j in range(tiles + late):
                if j < tiles:
                    y_tile(j)
                if j >= late and not last_layer:
                    Tail.pe_x(pe, g * tiles + (NT * (s + 1) + j - late), j - late)

        def three(pe, out, lh, ll, rh, rl, start, stop):
            nc.tensor.matmul(out, lh, rh, start=start, stop=False)
            nc.tensor.matmul(out, lh, rl, start=False, stop=False)
            return nc.tensor.matmul(out, ll, rh, start=False, stop=stop)

        QKV0 = 3 * D0
        A0 = 86016
        w0q = carve(A0, [KT, D0, H0], F32)
        w0 = carve(A0 + 8192, [KT, QKV0], F32)
        b0q = carve(A0 + 8960, [D0, H0], F32)
        b0 = carve(A0 + 11008, [QKV0], F32)
        qkv0 = carve(A0 + 11264, [GT, QKV0], F32)
        lg0 = carve(A0 + 12032, [GT, D0, D0], F32)
        pv0 = carve(A0 + 16128, [GT, D0, D0], F32)
        mx0 = carve(A0 + 20224, [GT, D0], F32)
        sm0 = carve(A0 + 20480, [GT, D0], F32)
        o0 = carve(A0 + 20736, [GT, D0], F32)
        sc0 = carve(A0 + 20992, [4, GT], F32)
        sq0 = carve(A0 + 21248, [GT, D0], F32)
        xt32 = carve(A0 + 21504, [KT, P], F32)
        a0_in = sem("a0_in")
        a0_w = sem("a0_w")
        a0_qkv = sem("a0_qkv")
        a0_lg = sem("a0_lg")
        a0_ex = sem("a0_ex")
        a0_var = sem("a0_var")
        a0_sd = sem("a0_sd")
        a0_wh = sem("a0_wh")
        x_sd0 = sem("a0_x")
        w0h = carve(A0 + 23552, [KT, QKV0], F16)
        w0l = carve(A0 + 23552 + 384, [KT, QKV0], F16)

        FW = F0 * P
        gh = carve(0, [KT, FW], F16)
        gl = carve(14336, [KT, FW], F16)
        uh = carve(2 * 14336, [KT, FW], F16)
        ul = carve(3 * 14336, [KT, FW], F16)
        dh = carve(4 * 14336, [F0, C], F16)
        dl = carve(5 * 14336, [F0, C], F16)
        hid_h = carve(86016, [F0, GW], F16)
        hid_l = carve(86016 + 14336, [F0, GW], F16)
        SCR = 114688
        sg1 = carve(SCR, [2, GW], F32)
        hd1 = carve(SCR + 4096, [2, GW], F32)
        raw1 = carve(SCR + 8192, [2, C], F32)
        we1 = carve(SCR + 12288, [2, C], F32)
        suT = carve(SCR, [FW], F32)
        svT = carve(SCR + 16384, [C], F32)
        QW = FW // 4
        chunks = []
        for m, (h_, l_) in enumerate(((gh, gl), (uh, ul))):
            for k in range(KT):
                for c in range(4):
                    chunks.append((m, k, slice(c * QW, (c + 1) * QW), h_[:, k, c * QW:(c + 1) * QW],
                                   l_[:, k, c * QW:(c + 1) * QW]))
        for f in range(F0):
            chunks.append((2, f, slice(0, C), dh[:, f, :], dl[:, f, :]))
        first_of = {0: 0, 1: 16, 2: 32}
        w1_raw = [sem("w1_raw0"), sem("w1_raw1")]
        w1_fac = sem("w1_fac")
        w1_ps = sem("w1_ps")
        w1_eff = sem("w1_eff")
        w1_hi = sem("w1_hi")
        w1_lo = sem("w1_lo")
        gate_ready = sem("gate_ready")
        up_ready = sem("up_ready")
        silu_ok = sem("silu_ok")
        hid_ok = sem("hid_ok")
        hid_hi = sem("hid_hi")
        hid_lo = sem("hid_lo")

        def pe_ffn(pe, s, F, gh, gl, uh, ul, dh, dl, hh, hl, w_ok, n_w, base, done=None, last_layer=False, n_down=None):
            pe.wait_ge(w_ok, n_w)

            def group(g):
                pe.wait_ge(xt_ok, g * GT + (NT * s + GT))
                cols = ds(g * GW, GW)
                for f in range(F):
                    i = g * F + (base + f)
                    b = 2 * (f % 2)
                    if f >= 2:
                        pe.wait_ge(hid_ok, i - 1)
                    fc = slice(f * P, (f + 1) * P)
                    for k in range(KT):
                        last = three(pe, ps_g[:, b, :], gh[:, k, fc], gl[:, k, fc], xt_hi[:, k, cols],
                                     xt_lo[:, k, cols], k == 0, k == KT - 1)
                    last.then_inc(gate_ready, 1)
                    for k in range(KT):
                        last = three(pe, ps_g[:, b + 1, :], uh[:, k, fc], ul[:, k, fc], xt_hi[:, k, cols],
                                     xt_lo[:, k, cols], k == 0, k == KT - 1)
                    last.then_inc(up_ready, 1)

                if n_down and isinstance(g, int):
                    pe.wait_ge(w_ok, n_down)

                def y_tile(j):
                    r = g * GT + (NT * (s - yb) + j)
                    if j >= 2:
                        pe.wait_ge(y_norm, r - 1)
                    tok = slice(j * P, (j + 1) * P)
                    for f in range(F):
                        if j == 0:
                            pe.wait_ge(hid_lo, g * F + (base + f + 1))
                        last = three(pe, ps_y[:, j % 2, :], hh[:, f, tok], hl[:, f, tok], dh[:, f, :], dl[:, f, :],
                                     f == 0, f == F - 1)
                    last.then_inc(done or y_ready, 1)
                pe_group(pe, s, g, y_tile, last_layer, late=1)

            if n_down:
                group(0)
                with pe.Fori(0, NG - 1) as i:
                    group(i + 1)
            else:
                with pe.Fori(0, NG) as g:
                    group(g)

        def act_ffn(act, s, F, hh, base, eps, sg, hd, y=y_psum, last_layer=False, before=None, beside=None):
            def group(g):
                for f in range(F):
                    i = g * F + (base + f)
                    b = 2 * (f % 2)
                    act.wait_ge(gate_ready, i + 1)
                    if f >= 2:
                        act.wait_ge(hid_ok, i - 1)
                    nc.scalar.activation(sg[:, f % 2, :], ps_g[:, b, :], ACT.Silu, scale=1.0 / WS).then_inc(silu_ok, 1)
                    if f:
                        act.wait_ge(hid_ok, i)
                        nc.scalar.activation(hh[:, f - 1, :], hd[:, (f - 1) % 2, :], ACT.Copy).then_inc(hid_hi, 1)
                    if beside and isinstance(g, int):
                        beside(f)
                act.wait_ge(hid_ok, g * F + (base + F))
                nc.scalar.activation(hh[:, F - 1, :], hd[:, (F - 1) % 2, :], ACT.Copy).then_inc(hid_hi, 1)
                if last_layer:
                    act_group(act, s, g, eps, y, True, before(g) if before else None)
                else:
                    act_group_apart(act, s, g, eps, y, lambda j: None)

            if beside:
                group(0)
                with act.Fori(0, NG - 1) as i:
                    group(i + 1)
            else:
                with act.Fori(0, NG) as g:
                    group(g)

        def dve_ffn(dve, ch, s, F, hh, hl, base, sg, hd, y=y_psum, last_layer=False, beside=None):
            def group(g):
                for f in range(F):
                    i = g * F + (base + f)
                    b = 2 * (f % 2)
                    dve.wait_ge(up_ready, i + 1)
                    dve.wait_ge(silu_ok, i + 1)
                    if f >= 2:
                        dve.wait_ge(hid_lo, i - 1)
                    nc.vector.scalar_tensor_tensor(out=hd[:, f % 2, :], in0=ps_g[:, b + 1, :], scalar=ACTS / WS,
                                                   in1=sg[:, f % 2, :], op0=ALU.mult, op1=ALU.mult).then_inc(hid_ok, 1)
                    if f:
                        dve.wait_ge(hid_hi, i)
                        nc.vector.tensor_tensor(hl[:, f - 1, :], hd[:, (f - 1) % 2, :], hh[:, f - 1, :],
                                                ALU.subtract).then_inc(hid_lo, 1)
                    if beside and isinstance(g, int):
                        beside(f)
                dve.wait_ge(hid_hi, g * F + (base + F))
                nc.vector.tensor_tensor(hl[:, F - 1, :], hd[:, (F - 1) % 2, :], hh[:, F - 1, :],
                                        ALU.subtract).then_inc(hid_lo, 1)
                if last_layer:
                    dve_group(dve, ch, s, g, y, True)
                else:
                    dve_group_apart(dve, ch, s, g, y, lambda j: None)

            links = 2 * GT if last_layer else 4 * GT
            if beside:
                group(0)
                with loop(dve, NG - 1, (ch, links)) as i:
                    group(i + 1)
            else:
                with loop(dve, NG, (ch, links)) as g:
                    group(g)

        H2, D2 = 32, 16
        QR = 4 * D2
        a2_qs = carve(0, [H2, TPB * P], F16)
        a2_p = carve(65536, [8, 4 * P], F32)
        a2_wh = carve(81920, [KT, 544], F16)
        a2_wl = carve(86272, [KT, 544], F16)
        a2_oh = carve(90624, [KT, C], F16)
        a2_ol = carve(94720, [KT, C], F16)
        a2_qh = carve(98816, [KT, GW], F16)
        a2_ql = carve(102912, [KT, GW], F16)
        a2_ks = carve(107008, [TPB * P], F16)
        a2_kh = carve(109056, [TPB * P], F16)
        a2_kl = carve(111104, [TPB * P], F16)
        VW = 32
        a2_v = carve(127776, [TPB, VW], F32)
        a2_mx = carve(128800, [2, 2, H2], F32)
        a2_z = carve(129312, [P], F16)
        a2_p2 = carve(119072, [4, 4 * P], F32)
        a2_ps = [a2_p[:, 0:4], a2_p[:, 4:8], a2_p2]
        a2_ac = carve(129568, [2, 4 * P], F32)
        a2_ar = carve(113696, [H2, D2], F32)
        a2_ah = carve(115744, [KT, P], F16)
        a2_al = carve(116768, [KT, P], F16)
        a2_mt = carve(117920, [P], F16)
        a2_rd = carve(118176, [H2], F32)
        a2_id = carve(118304, [P], F16)
        a2_mqk = carve(118560, [P], F16)
        a2_mkq = carve(118816, [P], F16)
        a2_raw = carve(119072, [KT, 544], F32)
        a2_rwo = carve(65536, [KT, C], F32)
        a2_in = sem("a2_in")
        a2_whi = sem("a2_whi")
        a2_wlo = sem("a2_wlo")
        a2_kp = sem("a2_kp")
        a2_khi = sem("a2_khi")
        a2_klo = sem("a2_klo")
        a2_vp = sem("a2_vp")
        a2_vok = sem("a2_vok")
        a2_qp = sem("a2_qp")
        a2_qhi = sem("a2_qhi")
        a2_qlo = sem("a2_qlo")
        a2_dma = sem("a2_dma")
        a2_dmp = sem("a2_dmp")
        a2_ms = sem("a2_ms")
        a2_md = sem("a2_md")
        a2_mc = sem("a2_mc")
        a2_mt_p = sem("a2_mt_p")
        a2_mt_a = sem("a2_mt_a")
        a2_mrow = sem("a2_mrow")
        a2_s = sem("a2_s")
        a2_e = sem("a2_e")
        a2_pv = sem("a2_pv")
        a2_ev = sem("a2_ev")
        a2_at = sem("a2_at")
        a2_o = sem("a2_o")
        a2_tr = sem("a2_tr")
        a2_thi = sem("a2_thi")
        a2_tlo = sem("a2_tlo")
        QS2 = 4 * 5
        QP2 = 4 * 3
        QDMA = 2 * QS2 + 4

        def max_units(t):
            n = (t + 1) * P
            units = []
            for first, w in ((0, min(n, 512)), (512, n - 512)):
                if w > 0:
                    units += [(h, 512 // w, first, w) for h in range(0, H2, 512 // w)]
            return units

        def steps2():
            steps = [("max", 0, u) for u in range(len(max_units(0)))] + [("row", 0)]
            todo = [("max", t, u) for t in range(1, TPB) for u in range(len(max_units(t)))]
            rows = 1
            for t in range(TPB):
                n = 8 * (t + 1)
                near = sum(m[1] == t + 1 for m in todo)
                count = 0
                for i in range(n):
                    if i == 0:
                        steps.append(("tile", t))
                    while todo and count < near * (i + 1) * 1.3 / n:
                        if todo[0][1] > t + 2 or (todo[0][1] == t + 2 and rows < t + 2 and count >= near + 2):
                            break
                        steps.append(todo.pop(0))
                        count += 1
                    if rows < t + 2 and t + 1 < TPB and count >= near + 1 and (t == 0 or i >= 14):
                        steps.append(("row", t + 1))
                        rows += 1
                    steps.append(("score", t, i))
                    if i % 4 == 1:
                        if i >= 4:
                            steps.append(("value", t, i // 4 - 1))
                        elif t:
                            steps.append(("value", t - 1, 2 * t - 1))
                            steps.append(("evacuate", t - 1))
                    if i % 4 == 3:
                        if t and i < 16:
                            steps.append((("heads", "turn", "project", "x")[i // 4], t - 1))
                        if t and i == 11:
                            steps.append(("y_sd", t - 1))
                    if t and i in (12, 13, 14):
                        steps.append((("y_norm", "x_sd", "x_norm")[i - 12], t - 1))
                while todo and todo[0][1] == t + 1:
                    steps.append(todo.pop(0))
                if rows < t + 2 and t + 1 < TPB:
                    steps.append(("row", t + 1))
                    rows += 1
            t = TPB - 1
            return steps + [("value", t, 2 * t + 1), ("evacuate", t), ("heads", t), ("turn", t), ("project", t),
                             ("y_sd", t), ("y_norm", t), ("x_sd", t), ("x_norm", t), ("x", t)]
        MU = sum(len(max_units(t)) for t in range(TPB))
        EU = 8 * sum(t + 1 for t in range(TPB))

        s3_raw = carve(0, [KT, C], F32)
        s3_h = carve(8192, [KT, C], F16)
        s3_l = carve(12288, [KT, C], F16)
        s3_s = carve(16384, [8], F32)
        s3_in = sem("s3_in")
        s3_scale = sem("s3_scale")
        s3_w = sem("s3_w")
        s3_sp = sem("s3_sp")
        s3_eps = sem("s3_eps")

        HS, PS, GS, KC = 64, 64, 8, 4
        HG = HS // GS
        GF = HG * PS
        IW = 2 * GF + 2 * P
        FT = IW // P
        CT = FT - GF // P
        SW = IW // 2
        m4_acc = carve(0, [NT, C], F32)
        m4_wh = carve(32768, [KT, IW + C], F16)
        m4_wl = carve(47104, [KT, IW + C], F16)
        m4_raw = carve(61440, [2, SW], F32)
        m4_hb = carve(66560, [CT, GW + KC - 1], F32)
        m4_xc = carve(78920, [CT, GW], F32)
        m4_sg = carve(91208, [4, GW], F32)
        m4_st = carve(99400, [GF], F32)
        m4_dtp = carve(101448, [NT * HS], F32)
        m4_dt2 = carve(105544, [NT * HS], F32)
        m4_ah = carve(109640, [NT * HS], F16)
        m4_al = carve(111688, [NT * HS], F16)
        m4_ar = carve(113736, [2, HG, P], F16)
        m4_ab = carve(117832, [2, GF], F16)
        m4_e1 = carve(119880, [HG, P], F32)
        m4_de = carve(123976, [2, 4, P], F32)
        m4_ty = carve(128072, [4, P], F32)
        m4_sq = carve(130120, [4, P], F32)
        m4_yh = carve(132168, [4, P], F16)
        m4_yl = carve(133192, [4, P], F16)
        m4_bt = carve(134216, [P], F32)
        m4_gm = carve(134728, [P], F32)
        m4_le = carve(135240, [P], F16)
        m4_gt = carve(135496, [P], F16)
        m4_on = carve(135752, [P], F16)
        m4_par = carve(136008, [CT * (KC + 1) + 8], F32)
        m4_nw = carve(136160, [4], F32)
        m4_dg = carve(136176, [NT * HG], F32)
        m4_pn = carve(136688, [CT * (KC + 1) + 8], F32)
        m4_sd = carve(136840, [1], F32)
        m4_rs = carve(136844, [1], F32)
        m4_o32 = carve(136848, [1], F32)
        m4_x12 = tmp.rearrange("p a c -> p (a c)")
        m4_e0 = xn.rearrange("p a (h t) -> p (a h) t", t=P)
        m4_e = [m4_e0, m4_e1]
        m4_u = carve(119880, [8 * HS], F32)
        m4_v = carve(121928, [8 * HS], F32)
        m4_db = carve(128072, [HS], F32)
        m4_na = carve(128328, [HS], F32)
        m4_dr = carve(130120, [KT, HS], F32)
        m4_dh = carve(131144, [KT, HS], F16)
        m4_dl = carve(131656, [KT, HS], F16)
        m4_cin = sem("m4_cin")
        m4_dw = sem("m4_dw")
        m4_dp = sem("m4_dp")
        m4_tv = sem("m4_tv")
        m4_ta = sem("m4_ta")
        m4_ri = [sem("m4_ri0"), sem("m4_ri1")]
        m4_pi = sem("m4_pi")
        m4_nwk = sem("m4_nwk")
        m4_whi = sem("m4_whi")
        m4_wlo = sem("m4_wlo")
        m4_ip = sem("m4_ip")
        m4_hbk = sem("m4_hbk")
        m4_gk = sem("m4_gk")
        m4_cy = sem("m4_cy")
        m4_cv = sem("m4_cv")
        m4_xk = sem("m4_xk")
        m4_ak = sem("m4_ak")
        m4_gp = sem("m4_gp")
        m4_sp = sem("m4_sp")
        m4_dd = sem("m4_dd")
        m4_gd = sem("m4_gd")
        m4_ek = sem("m4_ek")
        m4_dk = sem("m4_dk")
        m4_mk = sem("m4_mk")
        m4_xp = sem("m4_xp")
        m4_bk = sem("m4_bk")
        m4_x2 = sem("m4_x2")
        m4_ii = sem("m4_ii")
        m4_ia = sem("m4_ia")
        m4_sn = sem("m4_sn")
        m4_sk = sem("m4_sk")
        m4_tk = sem("m4_tk")
        m4_yk = sem("m4_yk")
        m4_yn = sem("m4_yn")
        m4_yhi = sem("m4_yhi")
        m4_ylo = sem("m4_ylo")
        m4_qk = sem("m4_qk")
        m4_qp = sem("m4_qp")
        m4_sdk = sem("m4_sdk")
        m4_rk = sem("m4_rk")
        m4_op = sem("m4_op")
        m4_ok = sem("m4_ok")

        s5_raw = carve(0, [2, KT, C], I32)
        s5_w1 = carve(16384, [KT, C], F32)
        s5_w1h = carve(24576, [KT, C], F16)
        s5_w1l = carve(28672, [KT, C], F16)
        s5_w3 = carve(32768, [KT, C], F16)
        s5_s0 = carve(36864, [KT], F32)
        s5_s2 = carve(36880, [KT], F32)
        s5_s4 = carve(36896, [C], F32)
        s5_b = carve(36896 + 2048, [C], F32)
        s5_y = carve(40992, [2, C], F32)
        s5_hh = carve(45088, [KT, GW], F16)
        s5_hl = carve(49184, [KT, GW], F16)
        s5_in = sem("s5_in")
        s5_wf = sem("s5_wf")
        s5_hi = sem("s5_hi")
        s5_w = sem("s5_w")
        s5_h = sem("s5_h")
        s5_hhi = sem("s5_hhi")
        s5_hlo = sem("s5_hlo")
        s5_p = sem("s5_p")

        INTER = 1376
        F3 = -(-INTER // P)
        FW3 = F3 * P
        A7 = 0
        g7h = carve(A7, [KT, FW3], F16)
        g7l = carve(A7 + 11264, [KT, FW3], F16)
        u7h = carve(A7 + 2 * 11264, [KT, FW3], F16)
        u7l = carve(A7 + 3 * 11264, [KT, FW3], F16)
        d7h = carve(A7 + 4 * 11264, [F3, C], F16)
        d7l = carve(A7 + 5 * 11264, [F3, C], F16)
        hid7h = carve(67584, [F3, GW], F16)
        hid7l = carve(67584 + 11264, [F3, GW], F16)
        sg7 = carve(90112, [2, GW], F32)
        hd7 = carve(94208, [2, GW], F32)
        y7 = carve(98304, [2, C], F16)
        q7 = carve(100352, [2, INTER], I32)
        w7 = carve(100352 + 11008, [INTER], F32)
        z7p = carve(116864, [172], I32)
        z7 = carve(116864 + 688, [172, 8], I32)
        s7 = carve(123056, [INTER], F16)
        sh7 = carve(125808, [1], I32)
        q7_in = [sem("q7_in0"), sem("q7_in1")]
        z7_in = sem("z7_in")
        sh7_in = sem("sh7_in")
        q7_done = sem("q7_done")
        w7_f = sem("w7_f")
        w7_h = sem("w7_h")
        w7_l = sem("w7_l")
        p7_y = sem("p7_y")
        mats7 = [("gate", g7h, g7l, INTER), ("up", u7h, u7l, INTER), ("down", d7h, d7l, C)]
        pieces7 = [(m, k, 16) for m in range(2) for k in range(KT)] + \
                  [(2, k, 16 if k < F3 - 1 else (INTER - (F3 - 1) * P) // 8) for k in range(F3)]

        D3 = C // 4
        S6 = TPB * P
        a6_raw = carve(0, [KT, 3 * D3], F32)
        a6_rwo = carve(6144, [C], F32)
        a6_wh = carve(8192, [KT, 3 * D3], F16)
        a6_wl = carve(11264, [KT, 3 * D3], F16)
        a6_oh = carve(14336, [C], F16)
        a6_ol = carve(15360, [C], F16)
        a6_b = carve(16384, [2], F32)
        a6_bv = carve(16400, [D3], F32)
        a6_bo = carve(16912, [C], F32)
        a6_qk = carve(18960, [2, GW], F32)
        a6_qh = carve(23056, [2, TOK], F16)
        a6_ql = carve(31248, [2, TOK], F16)
        a6_v = carve(39440, [GT, D3], F32)
        a6_vh = carve(41488, [NT, D3], F16)
        a6_vl = carve(45584, [NT, D3], F16)
        a6_mx = carve(49680, [2, 4], F32)
        a6_p = carve(49712, [2, S6], F32)
        a6_ph = carve(57904, [TPB, P], F16)
        a6_pl = carve(59952, [TPB, P], F16)
        a6_th = carve(62000, [P], F16)
        a6_tl = carve(62256, [P], F16)
        a6_y = carve(62512, [2, C], F32)
        a6_in = sem("a6_in")
        a6_wok = sem("a6_wok")
        a6_who = sem("a6_who")
        a6_pp = sem("a6_pp")
        a6_pf = sem("a6_pf")
        a6_pho = sem("a6_pho")
        a6_plo = sem("a6_plo")
        a6_s = sem("a6_s")
        a6_m = sem("a6_m")
        a6_e = sem("a6_e")
        a6_t = sem("a6_t")
        a6_tho = sem("a6_tho")
        a6_tlo = sem("a6_tlo")
        a6_o = sem("a6_o")
        a6_oho = sem("a6_oho")
        a6_olo = sem("a6_olo")
        a6_yp = sem("a6_yp")
        a6_inv = sem("a6_inv")
        SC6 = float(np.float32(1.0) / np.sqrt(np.float32(D3)))

        def arena_free(eng, layer):
            if layer > start:
                if layer == 1:
                    eng.wait_ge(xt_ok, 2 * NT)
                else:
                    eng.wait_ge(y_ready, NT * (layer - start - yb))

        def on(layer):
            return start <= layer < stop

        def sp_x(sp):
            xin = A["L0_attn_x"].rearrange("b (t p) c -> p (b t) c", p=P)
            for q in range(4):
                sp.dma_start(x[:, q * 4:(q + 1) * 4, :], xin[:, q * 4:(q + 1) * 4, :]).then_inc(x_in[q], 16)

        def sp_l0_attn(sp):
            sp.dma_start(w0q, A["L0_attn_Wq"].rearrange("(k p) d h -> p k d h", p=P)).then_inc(a0_in, 16)
            sp.dma_start(w0[:, :, D0:2 * D0], A["L0_attn_Wk"].rearrange("(k p) d h -> p k (d h)", p=P)).then_inc(a0_in, 16)
            sp.dma_start(w0[:, :, 2 * D0:], A["L0_attn_Wv"].rearrange("(k p) d h -> p k (d h)", p=P)).then_inc(a0_in, 16)
            row = lambda n, w: A[n].rearrange("a b -> (a b)").rearrange("(o n) -> o n", o=1).broadcast_to([P, w])
            sp.dma_start(b0q.rearrange("p d h -> p (d h)"), row("L0_attn_bq", C)).then_inc(a0_in, 16)
            sp.dma_start(b0[:, D0:2 * D0], row("L0_attn_bk", D0)).then_inc(a0_in, 16)
            sp.dma_start(b0[:, 2 * D0:], row("L0_attn_bv", D0)).then_inc(a0_in, 16)

        def sp_l0_ffn(sp):
            names = [("gate_wT", "gate_suT", "gate_sv"), ("up_wT", "up_suT", "up_sv"), ("down_wT", "down_svT", "down_su")]
            for i, (m, k, cols, _, _) in enumerate(chunks):
                if i == first_of[m]:
                    if m:
                        sp.wait_ge(w1_ps, i)
                    wn, fr, fc = names[m]
                    if m < 2:
                        sp.dma_start(suT[0:RANK, :], A[fr]).then_inc(w1_fac, 16)
                        sp.dma_start(svT[0:RANK, :], A[fc]).then_inc(w1_fac, 16)
                    else:
                        sp.dma_start(suT[0:RANK, :], A["down_sv"]).then_inc(w1_fac, 16)
                        sp.dma_start(svT[0:RANK, :], A["down_suT"]).then_inc(w1_fac, 16)
                if i >= 2:
                    sp.wait_ge(w1_eff, i - 1)
                w = cols.stop - cols.start
                sp.dma_start(raw1[:, i % 2, 0:w], A[wn][k * P:(k + 1) * P, cols]).then_inc(w1_raw[i % 2], 16)

        def sp_out(sp):
            xout = A["out"].rearrange("b (t p) c -> p (b t) c", p=P)
            for q in range(4):
                if stop > 1:
                    sp.wait_ge(x_new, (stop - start - yb - 1) * NT + (q + 1) * 4)
                else:
                    sp.wait_ge(xt_ok, 2 * NT)
                sp.dma_start(xout[:, q * 4:(q + 1) * 4, :], x[:, q * 4:(q + 1) * 4, :]).then_inc(x_out, 16)
            sp.wait_ge(x_out, 64)

        def pool_consts(pool, ch):
            ch.link(nc.gpsimd.memset(ident[:, :], 0.0))
            nc.gpsimd.affine_select(out=ident[:, :], in_=ident[:, :], compare_op=ALU.not_equal, fill=1.0, base=0,
                                    pattern=[[-1, P]], channel_multiplier=1).then_inc(consts_ok, 1)
            for i, e in enumerate((EPS, EPS * (WS * ACTS) ** 2, EPS * WS ** 2)):
                nc.gpsimd.memset(epsc[:, i:i + 1], float(e)).then_inc(consts_ok, 1)

        def pool_l0_ffn(pool):
            for i, (m, k, cols, h_, l_) in enumerate(chunks):
                w = cols.stop - cols.start
                pool.wait_ge(w1_hi, i + 1)
                nc.gpsimd.tensor_tensor(l_, we1[:, i % 2, 0:w], h_, ALU.subtract).then_inc(w1_lo, 1)

        def pe_x0(pe):
            pe.wait_ge(consts_ok, 4)
            for t in range(NT):
                Tail.pe_x(pe, t, t, first=(t == 0))

        def pe_l0_attn(pe):
            pe.wait_ge(a0_wh, 2)
            with pe.Fori(0, NG) as g:
                pe.wait_ge(xt_ok, g * GT + GT)
                pe.wait_ge(a0_lg, g + 1)
                for j in range(GT):
                    for k in range(KT):
                        cols = ds(g * GW + j * P, P)
                        last = three(pe, ps_m[:, j * QKV0:(j + 1) * QKV0], xt_hi[:, k, cols], xt_lo[:, k, cols],
                                     w0h[:, k, :], w0l[:, k, :], k == 0, k == KT - 1)
                last.then_inc(a0_qkv, 1)
                for j in range(GT):
                    Tail.pe_x(pe, g * GT + (NT + j), j)


        def pe_l0_ffn(pe):
            for i, (m, k, cols, _, _) in enumerate(chunks):
                w = cols.stop - cols.start
                if i == first_of[m]:
                    pe.wait_ge(w1_fac, 32 * (m + 1))
                if i >= 2:
                    pe.wait_ge(w1_eff, i - 1)
                if m < 2:
                    nc.tensor.matmul(ps_y[:, i % 2, 0:w], svT[0:RANK, k * P:(k + 1) * P], suT[0:RANK, cols],
                                     start=True, stop=True).then_inc(w1_ps, 1)
                else:
                    nc.tensor.matmul(ps_y[:, i % 2, 0:w], suT[0:RANK, k * P:(k + 1) * P], svT[0:RANK, 0:C],
                                     start=True, stop=True).then_inc(w1_ps, 1)
            pe_ffn(pe, 1 - start, F0, gh, gl, uh, ul, dh, dl, hid_h, hid_l, w1_lo, len(chunks), 0)

        def act_x0(act):
            act.wait_ge(consts_ok, 4)
            for t in range(NT):
                if t % 4 == 0:
                    act.wait_ge(x_in[t // 4], 16)
                Tail.act_x(act, t, t, t)
                if t:
                    Tail.act_hi(act, t - 1, t - 1)
            Tail.act_hi(act, NT - 1, NT - 1)


        def act_l0_attn(act, ch):
            act.wait_ge(a0_w, 2)
            nc.scalar.activation(w0h, w0, ACT.Copy, scale=WS).then_inc(a0_wh, 1)
            with loop(act, NG, (ch, 0)) as g:
                act.wait_ge(a0_lg, g * 1 + 2)
                nc.scalar.activation(lg0, lg0, ACT.Exp).then_inc(a0_ex, 1)
                act.wait_ge(a0_var, g + 1)
                nc.scalar.activation(sc0[:, 2, :], sc0[:, 1, :], ACT.Sqrt, bias=epsc[:, 0:1]).then_inc(a0_sd, 1)
                for j in range(GT):
                    Tail.act_x(act, g * GT + (NT + j), g * GT + j, j)
                    if j:
                        Tail.act_hi(act, g * GT + (NT + j - 1), g * GT + (j - 1))
                Tail.act_hi(act, g * GT + (NT + GT - 1), g * GT + (GT - 1))

        def act_l0_ffn(act):
            for i, (m, k, cols, h_, l_) in enumerate(chunks):
                w = cols.stop - cols.start
                act.wait_ge(w1_eff, i + 1)
                nc.scalar.activation(h_, we1[:, i % 2, 0:w], ACT.Copy).then_inc(w1_hi, 1)
            act_ffn(act, 1 - start, F0, hid_h, 0, epsc[:, 1:2], sg1, hd1)

        def dve_x0(dve, ch):
            for t in range(NT):
                if t % 4 == 0:
                    dve.wait_ge(x_in[t // 4], 16)
                Tail.dve_x(dve, ch, None, t, t, t)
                if t:
                    Tail.dve_lo(dve, t - 1, t - 1)
            Tail.dve_lo(dve, NT - 1, NT - 1)


        def dve_l0_attn(dve, ch):
            dve.wait_ge(a0_in, 96)
            nc.vector.tensor_reduce(w0[:, :, 0:D0], w0q, AXX, ALU.add).then_inc(a0_w, 1)
            nc.vector.tensor_reduce(b0[:, 0:D0], b0q, AXX, ALU.add).then_inc(a0_w, 1)
            dve.wait_ge(a0_wh, 1)
            nc.vector.scalar_tensor_tensor(out=w0l, in0=w0, scalar=WS, in1=w0h, op0=ALU.mult,
                                           op1=ALU.subtract).then_inc(a0_wh, 1)
            nc.vector.memset(sc0, 0.0).then_inc(a0_lg, 1)
            with loop(dve, NG, (ch, 16 + 2 * GT)) as g:
                dve.wait_ge(a0_qkv, g + 1)
                psq = ps_m[:, 0:GT * QKV0].rearrange("p (j w) -> p j w", j=GT)
                ch.link(nc.vector.scalar_tensor_tensor(out=qkv0, in0=psq, scalar=1.0 / WS,
                                                       in1=b0.unsqueeze(1).broadcast_to([P, GT, QKV0]),
                                                       op0=ALU.mult, op1=ALU.add))
                ch.link(nc.vector.tensor_tensor(lg0, qkv0[:, :, 0:D0].unsqueeze(3).broadcast_to([P, GT, D0, D0]),
                                                qkv0[:, :, D0:2 * D0].unsqueeze(2).broadcast_to([P, GT, D0, D0]), ALU.mult))
                ch.link(nc.vector.tensor_reduce(mx0, lg0, AXX, ALU.max))
                ch.link(nc.vector.tensor_tensor(lg0, lg0, mx0.unsqueeze(3).broadcast_to([P, GT, D0, D0]), ALU.subtract))
                nc.vector.tensor_scalar(lg0, lg0, float(D0) ** -0.5, None, ALU.mult).then_inc(a0_lg, 1)
                dve.wait_ge(a0_ex, g + 1)
                ch.link(nc.vector.tensor_reduce(sm0, lg0, AXX, ALU.add))
                ch.link(nc.vector.tensor_tensor(pv0, lg0, qkv0[:, :, 2 * D0:].unsqueeze(2).broadcast_to([P, GT, D0, D0]), ALU.mult))
                ch.link(nc.vector.tensor_reduce(o0, pv0, AXX, ALU.add))
                ch.link(nc.vector.reciprocal(sm0, sm0))
                ch.link(nc.vector.tensor_tensor(o0, o0, sm0, ALU.mult))
                ch.link(nc.vector.tensor_reduce(sc0[:, 0, :], o0, AXX, ALU.add))
                ch.link(nc.vector.tensor_scalar(sc0[:, 0, :], sc0[:, 0, :], 1.0 / D0, None, ALU.mult))
                ch.link(nc.vector.tensor_tensor(o0, o0, sc0[:, 0, :].unsqueeze(2).broadcast_to([P, GT, D0]), ALU.subtract))
                ch.link(nc.vector.tensor_tensor(sq0, o0, o0, ALU.mult))
                nc.vector.tensor_reduce(sc0[:, 3, :], sq0, AXX, ALU.add).then_inc(dve_seq, 1); ch.off += 1
                ch.wait(ch.base + ch.off)
                nc.vector.tensor_scalar(sc0[:, 1, :], sc0[:, 3, :], 1.0 / D0, None, ALU.mult).then_inc(a0_var, 1)
                dve.wait_ge(a0_sd, g + 1)
                ch.link(nc.vector.reciprocal(sc0[:, 3, :], sc0[:, 2, :]))
                ch.link(nc.vector.tensor_tensor(o0, o0, sc0[:, 3, :].unsqueeze(2).broadcast_to([P, GT, D0]), ALU.mult))
                for j in range(GT):
                    xv = x[:, g * GT + j, :].rearrange("p (d h) -> p d h", h=H0)
                    v = nc.vector.tensor_tensor(xv, xv, o0[:, j, :].unsqueeze(2).broadcast_to([P, D0, H0]), ALU.add)
                ch.off -= 0
                v.then_inc(x_sd0, 1)
                for j in range(GT):
                    if j == 0:
                        dve.wait_ge(x_sd0, g + 1)
                        alone(dve)
                    Tail.dve_x(dve, ch, None, g * GT + (NT + j), g * GT + j, j)
                    if j:
                        Tail.dve_lo(dve, g * GT + (NT + j - 1), g * GT + (j - 1))
                Tail.dve_lo(dve, g * GT + (NT + GT - 1), g * GT + (GT - 1))

        def dve_l0_ffn(dve, ch):
            for i, (m, k, cols, h_, l_) in enumerate(chunks):
                w = cols.stop - cols.start
                dve.wait_ge(w1_ps, i + 1)
                dve.wait_ge(w1_raw[i % 2], 16 * (i // 2 + 1))
                if i >= 2:
                    dve.wait_ge(w1_lo, i - 1)
                nc.vector.scalar_tensor_tensor(out=we1[:, i % 2, 0:w], in0=ps_y[:, i % 2, 0:w], scalar=WS,
                                               in1=raw1[:, i % 2, 0:w], op0=ALU.mult, op1=ALU.mult).then_inc(w1_eff, 1)
            dve_ffn(dve, ch, 1 - start, F0, hid_h, hid_l, 0, sg1, hd1)

        def sp_l1_attn(sp):
            s = 2 - start
            arena_free(sp, 2)
            sp.dma_start(a2_raw, A["L1_attn_Wqkv"].rearrange("(k p) n -> p k n", p=P)).then_inc(a2_in, 16)
            sp.dma_start(a2_rwo, A["L1_attn_Wo"].rearrange("(k p) n -> p k n", p=P)).then_inc(a2_in, 16)
            sp.dma_start(a2_qs[QR:QR + 2], A["alibi_q"]).then_inc(a2_in, 16)
            sp.dma_start(a2_ks[QR:QR + 3], A["alibi_k"]).then_inc(a2_in, 16)
            sp.dma_start(a2_id, A["ident16"]).then_inc(a2_in, 16)
            sp.dma_start(a2_mqk, A["mask_qk"]).then_inc(a2_in, 16)
            sp.dma_start(a2_mkq, A["mask_kq"]).then_inc(a2_in, 16)
            for b in range(NB):
                sp.wait_ge(a2_klo, 2 * (b + 1))
                if b:
                    sp.wait_ge(y_ready, NT * (s - yb) + TPB * b)
                for rep, src in enumerate((a2_kh, a2_kl, a2_kh, a2_kl)):
                    sp.dma_start(a2_ks[rep * D2:(rep + 1) * D2], src[0:D2]).then_inc(a2_dma, 16)
                for gg in range(2):
                    sp.wait_ge(a2_qlo, KT * (2 * b + gg + 1))
                    q_rows(sp, gg, range(0, 5), a2_dma)
                for t in range(TPB):
                    sp.wait_ge(a2_mt_a, TPB * b + t + 1)
                    sp.dma_start(a2_qs[QR + 2:QR + 3, :, t * P:(t + 1) * P], a2_mt[0:H2]).then_inc(a2_mrow, 16)

        def q_rows(eng, gg, heads, done):
            for h in heads:
                for rep, src in enumerate((a2_qh, a2_qh, a2_ql, a2_ql)):
                    eng.dma_start(a2_qs[rep * D2:(rep + 1) * D2, h:H2:8, gg * GW:(gg + 1) * GW],
                                  src[h * D2:(h + 1) * D2]).then_inc(done, 16)

        def pool_l1_attn(pool):
            s = 2 - start
            for b in range(NB):
                if b:
                    pool.wait_ge(y_ready, NT * (s - yb) + TPB * b)
                for gg in range(2):
                    pool.wait_ge(a2_qlo, KT * (2 * b + gg + 1))
                    q_rows(pool, gg, range(5, 8), a2_dmp)

        def pe_l1_attn(pe):
            s = 2 - start
            pe.wait_ge(a2_wlo, 3)
            pe.wait_ge(a2_md, 2)
            pe.wait_ge(a2_in, 16 * 7)
            um, ue, uv = Tally(), Tally(), Tally()
            ahead = [sum(len(max_units(v)) for v in range(t + 1)) for t in range(TPB)]

            def max_unit(t, u):
                h0, heads, c, w = max_units(t)[u]
                bank = um.off % 2
                pe.wait_ge(a2_md, um(1))
                for a in range(heads):
                    q = a2_qs[0:QR + 2, h0 + a, t * P:(t + 1) * P]
                    diag = c + w == (t + 1) * P
                    last = nc.tensor.matmul(psum[:, bank, a * w:(a + 1) * w], q, a2_ks[0:QR + 2, c:c + w], start=True,
                                            stop=not diag)
                    if diag:
                        last = nc.tensor.matmul(psum[:, bank, (a + 1) * w - P:(a + 1) * w], a2_id, a2_mqk, start=False,
                                                stop=True)
                last.then_inc(a2_ms, 1)
                um.add()

            def score_unit(t, i):
                k, h4 = i // 8, i % 8
                pe.wait_ge(a2_e, ue(1))
                out = psum[:, 2 + i % 2, :]
                last = nc.tensor.matmul(out, a2_ks[0:QR + 3, k * P:(k + 1) * P],
                                        a2_qs[0:QR + 3, h4 * 4:h4 * 4 + 4, t * P:(t + 1) * P], start=True, stop=(k < t))
                if k == t:
                    last = nc.tensor.matmul(out, a2_id, a2_mkq.unsqueeze(1).broadcast_to([P, 4, P]), start=False, stop=True)
                last.then_inc(a2_s, 1)
                ue.add()

            def value_units(t, g):
                uv.add()
                pe.wait_ge(a2_e, uv.base * 4 + (uv.off * 4 + 2))
                for j in range(4):
                    last = nc.tensor.matmul(psum[j * VW:(j + 1) * VW, 4 + g % 2, :], a2_v[:, g // 2, :],
                                            a2_ps[(t * (t + 1) + g) % 3][:, j, :], start=False, stop=True, skip_group_check=True)
                last.then_inc(a2_pv, 1)

            def zeros():
                for bank in (4, 5):
                    nc.tensor.matmul(psum[:, bank, :], a2_z, a2_oh[:, 0, :], start=True, stop=True, skip_group_check=True)

            with loop(pe, NB, (um, MU), (ue, EU), (uv, EU // 4)) as b:
                pe.wait_ge(xt_ok, b * TPB + (NT * s + TPB))
                for gg in range(2):
                    for k in range(KT):
                        cols = ds(b * (TPB * P) + gg * GW, GW)
                        last = three(pe, ps_y[0:D2, gg, :], a2_wh[:, k, C:C + D2], a2_wl[:, k, C:C + D2],
                                     xt_hi[:, k, cols], xt_lo[:, k, cols], k == 0, k == KT - 1)
                    last.then_inc(a2_kp, 1)
                for t in range(TPB):
                    tok = ds(b * (TPB * P) + t * P, P)
                    for k in range(KT):
                        last = three(pe, ps_m[:, t * D2:(t + 1) * D2], xt_hi[:, k, tok], xt_lo[:, k, tok],
                                     a2_wh[:, k, C + D2:], a2_wl[:, k, C + D2:], k == 0, k == KT - 1)
                last.then_inc(a2_vp, 1)
                for gg in range(2):
                    for f in range(KT):
                        if gg:
                            pe.wait_ge(a2_qlo, b * (2 * KT) + (f + 1))
                        for k in range(KT):
                            cols = ds(b * (TPB * P) + gg * GW, GW)
                            fc = slice(f * P, (f + 1) * P)
                            last = three(pe, ps_g[:, f, :], a2_wh[:, k, fc], a2_wl[:, k, fc], xt_hi[:, k, cols],
                                         xt_lo[:, k, cols], k == 0, k == KT - 1)
                        last.then_inc(a2_qp, 1)
                pe.wait_ge(a2_dma, b * (16 * QDMA) + 16 * QDMA)
                pe.wait_ge(a2_dmp, b * (32 * QP2) + 32 * QP2)
                pe.wait_ge(a2_qlo, b * (2 * KT) + 2 * KT)
                pe.wait_ge(a2_vok, b + 1)
                zeros()
                for what, t, *u in steps2():
                    i = b * TPB + t
                    if what == "max":
                        max_unit(t, *u)
                    elif what == "row":
                        if t > 3:
                            pe.wait_ge(a2_mc, b * 4 + (t - 3))
                        else:
                            pe.wait_ge(a2_md, b * MU + (ahead[t] + 2))
                        if t >= 2:
                            pe.wait_ge(y_norm, i + (NT * (s - yb) - 1))
                        nc.tensor.transpose(ps_m[0:H2, 0:P], a2_mx[:, t % 2, 0, :], ident[:, :]).then_inc(a2_mt_p, 1)
                    elif what == "tile":
                        pe.wait_ge(a2_mrow, i * 16 + 16)
                        alone(pe)
                    elif what == "score":
                        score_unit(t, *u)
                    elif what == "value":
                        if t and u[0] == 0:
                            pe.wait_ge(a2_ev, i)
                            zeros()
                        value_units(t, *u)
                    elif what == "heads":
                        pe.wait_ge(a2_ev, i + 1)
                        if t:
                            pe.wait_ge(xt_ok, i + NT * (s + 1))
                        pe.wait_ge(a2_mt_a, b * TPB + min(t + 2, TPB))
                        for bank in range(2):
                            for h in range(4):
                                last = nc.tensor.transpose(psum[:, 6 + bank, h * P:(h + 1) * P],
                                                           a2_ac[:, bank, h * P:(h + 1) * P], ident[:, :])
                        last.then_inc(a2_at, 1)
                    elif what == "turn":
                        pe.wait_ge(a2_o, i + 1)
                        for k in range(KT):
                            last = nc.tensor.transpose(ps_t[:, k, :],
                                                       a2_ar[:, 8 * k:8 * k + 8, :].rearrange("p h d -> p (h d)"),
                                                       ident[:, :])
                        last.then_inc(a2_tr, 1)
                    elif what == "project":
                        pe.wait_ge(a2_tlo, i + 1)
                        for k in range(KT):
                            last = three(pe, ps_m, a2_ah[:, k, :], a2_al[:, k, :], a2_oh[:, k, :], a2_ol[:, k, :],
                                         k == 0, k == KT - 1)
                        last.then_inc(y_ready, 1)
                    elif what == "x":
                        Tail.pe_x(pe, i + NT * (s + 1), t)

        def act_l1_attn(act):
            s = 2 - start
            act.wait_ge(a2_in, 16 * 7)
            nc.scalar.activation(a2_wh, a2_raw, ACT.Copy, scale=WS).then_inc(a2_whi, 1)
            nc.scalar.activation(a2_oh, a2_rwo, ACT.Copy, scale=WS).then_inc(a2_whi, 1)
            act.sem_inc(a2_e, 2)
            ue = Tally()
            with loop(act, NB, (ue, 8 * sum(t + 1 for t in range(TPB)))) as b:
                for gg in range(2):
                    act.wait_ge(a2_kp, b * 2 + (gg + 1))
                    nc.scalar.activation(a2_kh[0:D2, gg * GW:(gg + 1) * GW], ps_y[0:D2, gg, :], ACT.Copy,
                                         scale=1.0 / WS).then_inc(a2_khi, 1)
                act.wait_ge(a2_vp, b + 1)
                nc.scalar.activation(a2_v[:, :, 0:D2], ps_m[:, 0:TPB * D2].rearrange("p (t d) -> p t d", t=TPB), ACT.Copy,
                                     scale=1.0 / WS).then_inc(a2_vok, 1)
                for gg in range(2):
                    if gg:
                        act.wait_ge(a2_dma, b * (16 * QDMA) + 16 * (4 + QS2))
                        act.wait_ge(a2_dmp, b * (32 * QP2) + 16 * QP2)
                    for f in range(KT):
                        act.wait_ge(a2_qp, b * (2 * KT) + (gg * KT + f + 1))
                        nc.scalar.activation(a2_qh[:, f, :], ps_g[:, f, :], ACT.Copy, scale=0.25 / WS).then_inc(a2_qhi, 1)

                for what, t, *u in steps2():
                    i = b * TPB + t
                    if what == "row":
                        act.wait_ge(a2_mt_p, i + 1)
                        if t:
                            act.wait_ge(a2_mrow, i * 16)
                        nc.scalar.activation(a2_mt[0:H2], ps_m[0:H2, 0:P], ACT.Copy, scale=-1.0).then_inc(a2_mt_a, 1)
                    elif what == "score":
                        act.wait_ge(a2_s, ue(1))
                        group = t * (t + 1) + u[0] // 4
                        if group >= 3:
                            act.wait_ge(a2_pv, b * (EU // 4) + (group - 2))
                        ue.add()
                        nc.scalar.activation(a2_ps[group % 3][:, u[0] % 4, :], psum[:, 2 + u[0] % 2, :], ACT.Exp).then_inc(a2_e, 1)
                    elif what == "evacuate":
                        act.wait_ge(a2_pv, b * (EU // 4) + (t + 1) * (t + 2))
                        if t:
                            act.wait_ge(a2_at, i)
                        nc.scalar.activation(a2_ac, psum[:, 4:6, :], ACT.Copy).then_inc(a2_ev, 1)
                    elif what == "turn":
                        act.wait_ge(a2_tr, i + 1)
                        nc.scalar.activation(a2_ah, ps_t, ACT.Copy, scale=ACTS).then_inc(a2_thi, 1)
                    elif what == "y_sd":
                        Tail.act_y_sd(act, i + NT * (s - yb), t, epsc[:, 1:2])
                    elif what == "y_norm":
                        Tail.act_y_norm(act, i + NT * (s - yb), t, ps_m)
                    elif what == "x_sd":
                        Tail.act_x_sd(act, i + NT * (s + 1), t)
                    elif what == "x_norm":
                        Tail.act_x_norm(act, i + NT * (s + 1), i, t)
                    elif what == "x":
                        Tail.act_hi(act, i + NT * (s + 1), i)

        def dve_l1_attn(dve, ch):
            s = 2 - start
            dve.wait_ge(a2_whi, 2)
            nc.vector.scalar_tensor_tensor(out=a2_wl, in0=a2_raw, scalar=WS, in1=a2_wh, op0=ALU.mult,
                                           op1=ALU.subtract).then_inc(a2_wlo, 1)
            nc.vector.scalar_tensor_tensor(out=a2_ol, in0=a2_rwo, scalar=WS, in1=a2_oh, op0=ALU.mult,
                                           op1=ALU.subtract).then_inc(a2_wlo, 1)
            nc.vector.memset(a2_v, 0.0).then_inc(a2_wlo, 1)
            dve.wait_ge(a2_wlo, 3)
            nc.vector.memset(a2_v[:, :, D2:D2 + 1], 1.0)
            nc.vector.memset(a2_z, 0.0).then_inc(a2_md, 2)
            um = Tally()
            with loop(dve, NB, (um, MU), (ch, TPB * 5)) as b:
                for gg in range(2):
                    dve.wait_ge(a2_khi, b * 2 + (gg + 1))
                    w = slice(gg * GW, (gg + 1) * GW)
                    nc.vector.scalar_tensor_tensor(out=a2_kl[0:D2, w], in0=ps_y[0:D2, gg, :], scalar=1.0 / WS,
                                                   in1=a2_kh[0:D2, w], op0=ALU.mult, op1=ALU.subtract).then_inc(a2_klo, 1)
                for gg in range(2):
                    for f in range(KT):
                        dve.wait_ge(a2_qhi, b * (2 * KT) + (gg * KT + f + 1))
                        nc.vector.scalar_tensor_tensor(out=a2_ql[:, f, :], in0=ps_g[:, f, :], scalar=0.25 / WS,
                                                       in1=a2_qh[:, f, :], op0=ALU.mult,
                                                       op1=ALU.subtract).then_inc(a2_qlo, 1)

                for what, t, *u in steps2():
                    i = b * TPB + t
                    if what == "max":
                        h0, heads, c, w = max_units(t)[u[0]]
                        src = psum[:, um.off % 2, 0:heads * w].rearrange("p (h c) -> p h c", h=heads)
                        if u[0] == 0 and t >= 2:
                            dve.wait_ge(a2_mt_p, i - 1)
                            alone(dve)
                        dve.wait_ge(a2_ms, um(1))
                        nc.vector.tensor_reduce(a2_mx[:, t % 2, c // 512, h0:h0 + heads], src, AXX,
                                                ALU.max).then_inc(a2_md, 1)
                        um.add()
                    elif what == "row" and t > 3:
                        dve.wait_ge(a2_md, um(2))
                        mx = a2_mx[:, t % 2, 0, :]
                        nc.vector.tensor_tensor(mx, mx, a2_mx[:, t % 2, 1, :], ALU.max).then_inc(a2_mc, 1)
                    elif what == "heads":
                        dve.wait_ge(a2_at, i + 1)
                        v = [psum[:, 6 + bank, :].rearrange("p (h j w) -> p h j w", h=4, j=4) for bank in range(2)]
                        rd = a2_rd.rearrange("p (a h j) -> p a h j", a=2, h=4)
                        nc.vector.reciprocal(rd[:, 0], v[0][:, :, :, D2])
                        ch.link(nc.vector.reciprocal(rd[:, 1], v[1][:, :, :, D2]))
                        for bank in range(2):
                            o = a2_ar[:, bank * 16:bank * 16 + 16, :].rearrange("p (j h) d -> p h j d", h=4)
                            last = nc.vector.tensor_tensor(o, v[bank][:, :, :, 0:D2],
                                                           rd[:, bank].unsqueeze(3).broadcast_to([P, 4, 4, D2]), ALU.mult)
                        last.then_inc(a2_o, 1)
                    elif what == "turn":
                        dve.wait_ge(a2_thi, i + 1)
                        nc.vector.scalar_tensor_tensor(out=a2_al, in0=ps_t, scalar=ACTS, in1=a2_ah, op0=ALU.mult,
                                                       op1=ALU.subtract).then_inc(a2_tlo, 1)
                    elif what == "project":
                        Tail.dve_y_stats(dve, ch, i + NT * (s - yb), t, ps_m)
                    elif what == "y_sd":
                        Tail.dve_y_scale(dve, ch, i + NT * (s - yb), t)
                    elif what == "y_norm":
                        Tail.dve_add(dve, i + NT * (s - yb), i, t)
                        Tail.dve_x_stats(dve, ch, i + NT * (s - yb), i + NT * (s + 1), i, t)
                    elif what == "x_sd":
                        Tail.dve_x_scale(dve, ch, i + NT * (s + 1), t)
                    elif what == "x":
                        Tail.dve_lo(dve, i + NT * (s + 1), i)

        def sp_l1_ffn(sp):
            arena_free(sp, 3)
            sp.dma_start(s3_raw, A["L1_ffn_sign"].rearrange("(k p) n -> p k n", p=P)).then_inc(s3_in, 16)
            sp.dma_start(s3_s[:, 0:1], A["L1_ffn_scale"].broadcast_to([P, 1])).then_inc(s3_scale, 16)

        def act_l1_ffn(act):
            act.wait_ge(s3_in, 16)
            nc.scalar.activation(s3_h, s3_raw, ACT.Copy, scale=WS).then_inc(s3_w, 1)
            act.wait_ge(s3_scale, 16)
            nc.scalar.activation(s3_s[:, 1:2], s3_s[:, 0:1], ACT.Abs).then_inc(s3_sp, 1)
            act.wait_ge(s3_sp, 1)
            nc.scalar.activation(s3_s[:, 2:3], s3_s[:, 1:2], ACT.Exp, scale=-1.0).then_inc(s3_sp, 1)
            act.wait_ge(s3_sp, 2)
            nc.scalar.activation(s3_s[:, 3:4], s3_s[:, 2:3], ACT.Ln, bias=1.0).then_inc(s3_sp, 1)
            act.wait_ge(s3_eps, 4)
            act_group(act, 3 - start, 0, epsc[:, 3:4], tiles=NT)

        def dve_l1_ffn(dve, ch):
            dve.wait_ge(s3_w, 1)
            nc.vector.scalar_tensor_tensor(out=s3_l, in0=s3_raw, scalar=WS, in1=s3_h, op0=ALU.mult,
                                           op1=ALU.subtract).then_inc(s3_w, 1)
            dve.wait_ge(s3_sp, 3)
            nc.vector.scalar_tensor_tensor(out=s3_s[:, 4:5], in0=s3_s[:, 0:1], scalar=0.0, in1=s3_s[:, 3:4],
                                           op0=ALU.max, op1=ALU.add).then_inc(s3_eps, 1)
            dve.wait_ge(s3_eps, 1)
            nc.vector.reciprocal(s3_s[:, 5:6], s3_s[:, 4:5]).then_inc(s3_eps, 1)
            dve.wait_ge(s3_eps, 2)
            nc.vector.tensor_scalar(s3_s[:, 6:7], s3_s[:, 5:6], WS * EPS ** 0.5, None, ALU.mult).then_inc(s3_eps, 1)
            dve.wait_ge(s3_eps, 3)
            nc.vector.tensor_tensor(epsc[:, 3:4], s3_s[:, 6:7], s3_s[:, 6:7], ALU.mult).then_inc(s3_eps, 1)
            dve_group(dve, ch, 3 - start, 0, tiles=NT)

        def pe_l1_ffn(pe):
            pe.wait_ge(s3_w, 2)
            s = 3 - start

            def y_tile(j):
                pe.wait_ge(xt_ok, j + (NT * s + 1))
                if j >= 2:
                    pe.wait_ge(y_norm, j + (NT * (s - yb) - 1))
                tok = slice(j * P, (j + 1) * P)
                for k in range(KT):
                    last = three(pe, ps_y[:, j % 2, :], xt_hi[:, k, tok], xt_lo[:, k, tok], s3_h[:, k, :],
                                 s3_l[:, k, :], k == 0, k == KT - 1)
                last.then_inc(y_ready, 1)
            pe_group(pe, s, 0, y_tile, tiles=NT)

        HF = 4
        CG = NT
        QI, QS = 2 * KT, 3 * KT

        def sp_l2_attn(sp):
            arena_free(sp, 4)
            row = lambda n: A[n].rearrange("(o n) -> o n", o=1).broadcast_to([P, HS])
            sp.dma_start(m4_dr, A["m4_dt"]).then_inc(m4_cin, 16)
            sp.dma_start(m4_db, row("L2_attn_dt_bias")).then_inc(m4_cin, 16)
            sp.dma_start(m4_na, row("L2_attn_A_log")).then_inc(m4_cin, 16)
            for v, n in ((m4_le, "tri_le"), (m4_gt, "tri_gt"), (m4_on, "ones16")):
                sp.dma_start(v, A[n]).then_inc(m4_cin, 16)
            wi = A["m4_wi"].rearrange("g q p n -> p (g q) n")
            wo = A["m4_wo"].rearrange("g q p n -> p (g q) n")

            def fetch(q, src, at, w):
                sp.dma_start(m4_raw[:, q % 2:q % 2 + 1, 0:w], src[:, ds(at, 1), :]).then_inc(m4_ri[q % 2], 16)

            for q in range(QI):
                if q >= 2:
                    sp.wait_ge(m4_wlo, q + 1)
                fetch(q, wi, q, SW)
            with sp.Fori(0, GS) as gi:
                sp.wait_ge(m4_nwk, gi * 2 + 1)
                sp.dma_start(m4_pn.unsqueeze(1), A["m4_par"][:, ds(gi, 1), :]).then_inc(m4_pi, 16)
                for q in range(KT):
                    sp.wait_ge(m4_wlo, gi * QS + (QI + q + 1))
                    fetch(q, wo, gi * KT + q, C)
                for q in range(QI):
                    sp.wait_ge(m4_wlo, gi * QS + (QS + q + 1))
                    fetch(q, wi, gi * QI + (QI + q), SW)

        def act_piece(act, gi, j):
            act.wait_ge(m4_ri[j % 2], (gi * (QS // 2) + (j // 2 + 1)) * 16)
            q = j % QS
            if q < QI:
                v = nc.scalar.activation(m4_wh[:, q // 2, q % 2 * SW:(q % 2 + 1) * SW], m4_raw[:, j % 2, :], ACT.Copy,
                                         scale=WS)
            else:
                v = nc.scalar.activation(m4_wh[:, q - QI, IW:], m4_raw[:, j % 2, 0:C], ACT.Copy,
                                         scale=m4_nw[:, q - QI:q - QI + 1])
            v.then_inc(m4_whi, 1)

        def dve_piece(dve, gi, j):
            dve.wait_ge(m4_whi, gi * QS + (j + 1))
            q = j % QS
            if q < QI:
                wc, raw, w = (q // 2, slice(q % 2 * SW, (q % 2 + 1) * SW)), m4_raw[:, j % 2, :], WS
            else:
                wc, raw, w = (q - QI, slice(IW, IW + C)), m4_raw[:, j % 2, 0:C], m4_nw[:, q - QI:q - QI + 1]
            nc.vector.scalar_tensor_tensor(out=m4_wl[:, wc[0], wc[1]], in0=raw, scalar=w, in1=m4_wh[:, wc[0], wc[1]],
                                           op0=ALU.mult, op1=ALU.subtract).then_inc(m4_wlo, 1)

        def act_l2_attn(act):
            for c in (m4_qk, m4_ek, m4_dk, m4_sdk, m4_bk):
                act.sem_inc(c, 1)
            act.wait_ge(m4_cin, 6 * 16)
            nc.scalar.activation(m4_na, m4_na, ACT.Exp).then_inc(m4_dw, 1)
            nc.scalar.activation(m4_dh, m4_dr, ACT.Copy, scale=WS).then_inc(m4_dw, 1)
            for j in range(QI):
                act_piece(act, 0, j)
            for n in range(2):
                act.wait_ge(m4_tv, 4 * n + 1)
                nc.scalar.activation(m4_v, m4_u, ACT.Abs).then_inc(m4_ta, 1)
                act.wait_ge(m4_ta, 5 * n + 1)
                nc.scalar.activation(m4_v, m4_v, ACT.Exp, scale=-1.0).then_inc(m4_ta, 1)
                act.wait_ge(m4_ta, 5 * n + 2)
                nc.scalar.activation(m4_v, m4_v, ACT.Ln, bias=1.0).then_inc(m4_ta, 1)
                act.wait_ge(m4_tv, 4 * n + 2)
                hc = slice(n * 8 * HS, (n + 1) * 8 * HS)
                nc.scalar.activation(m4_ah[:, hc], m4_u, ACT.Copy).then_inc(m4_ta, 1)
                act.wait_ge(m4_dp, n + 3)
                nc.scalar.activation(m4_v, psum[:, 6, :], ACT.Exp).then_inc(m4_ta, 1)
                act.wait_ge(m4_tv, 4 * n + 4)

            with act.Fori(0, GS) as gi:
                act.wait_ge(m4_gd, gi * 2 + 1)
                act.wait_ge(m4_sk, gi * (CG + 2) + 1)
                nc.scalar.activation(m4_dg, psum[:, 7, 0:NT * HG], ACT.Exp).then_inc(m4_gd, 1)
                act.wait_ge(m4_nwk, gi * 2 + 3)
                act.wait_ge(m4_op, gi * CG + 1)
                for j in range(QI, QI + 2):
                    act_piece(act, gi, j)
                for x in range(HF):
                    act_before(act, gi, x, range(2 if x else 0, 6))
                    if x == 0:
                        for j in range(QI + 2, QS):
                            act_piece(act, gi, j)
                    act_gates(act, gi, x)
                    for c in range(4):
                        if c:
                            deviation(act, gi, x, c - 1)
                        square(act, gi, x, c)
                        if c < 3:
                            b_tokens(act, gi, x, c + 1)
                        if x == HF - 1:
                            if c == 0:
                                act.wait_ge(m4_ip, (gi + 1) * (HF * FT))
                            act_piece(act, gi, QS + 2 * c)
                        gated(act, gi, x, c)
                        if c < 2:
                            decays(act, gi, x, c + 2)
                        if x == HF - 1:
                            act_piece(act, gi, QS + 2 * c + 1)
                    if x < HF - 1:
                        act_before(act, gi, x + 1, range(0, 2))
                    deviation(act, gi, x, 3)
            s = 4 - start
            act_group(act, s, 0, epsc[:, 2:3], y=lambda j: m4_acc[:, j, :], tiles=NT)

        BANK = (0, 1, 2, 3, 0, 1, 2, 3, 2, 5)

        def act_before(act, gi, x, tiles):
            for i in tiles:
                if i == 0:
                    act.wait_ge(m4_cy, gi * HF + (x + 1))
                act.wait_ge(m4_ip, gi * (HF * FT) + (x * FT + i + 1))
                nc.scalar.activation(m4_hb[:, i, KC - 1:], psum[:, BANK[i], :], ACT.Copy,
                                     scale=1.0 / WS).then_inc(m4_hbk, 1)

        def act_gates(act, gi, x):
            def gate(i):
                act.wait_ge(m4_ip, gi * (HF * FT) + (x * FT + i + 1))
                nc.scalar.activation(m4_sg[:, i - CT, :], psum[:, BANK[i], :], ACT.Silu,
                                     scale=1.0 / WS).then_inc(m4_gk, 1)

            def convolved(i):
                act.wait_ge(m4_cv, gi * (HF * CT) + (x * CT + i + 1))
                nc.scalar.activation(m4_xc[:, i, :], m4_xc[:, i, :], ACT.Silu).then_inc(m4_xk, 1)
            act.wait_ge(m4_ylo, gi * CG + (x * 4 + 1))
            for i in range(3):
                convolved(i)
            gate(6)
            convolved(3)
            gate(7)
            convolved(4)
            convolved(5)
            decays(act, gi, x, 0)
            gate(8)
            b_tokens(act, gi, x, 0)
            decays(act, gi, x, 1)
            gate(9)

        def decays(act, gi, x, c):
            k = gi * CG + (x * 4 + c + 1)
            act.wait_ge(m4_sp, k + 1)
            act.wait_ge(m4_ia, k)
            nc.scalar.activation(m4_e[c % 2].rearrange("p h t -> p (h t)"),
                                 psum[:, 0:2, :].rearrange("p a t -> p (a t)"), ACT.Exp).then_inc(m4_ek, 1)
            act.wait_ge(m4_dd, k + 1)
            act.wait_ge(m4_tk, k)
            nc.scalar.activation(m4_de[:, c % 2].rearrange("p i t -> p (i t)"), psum[:, 4, :], ACT.Exp).then_inc(m4_dk, 1)

        def b_tokens(act, gi, x, c):
            k = gi * CG + (x * 4 + c + 1)
            act.wait_ge(m4_xp, k)
            act.wait_ge(m4_sn, k)
            nc.scalar.activation(m4_bt, psum[:, 3, 0:P], ACT.Copy).then_inc(m4_bk, 1)

        def square(act, gi, x, c):
            k = gi * CG + (x * 4 + c + 1)
            tok = slice(c * P, (c + 1) * P)
            act.wait_ge(m4_yk, k + 1)
            act.wait_ge(m4_qp, k)
            nc.scalar.activation(m4_sq, m4_xc[:, 0:4, tok], ACT.Square).then_inc(m4_qk, 1)

        def gated(act, gi, x, c):
            k = gi * CG + (x * 4 + c + 1)
            act.wait_ge(m4_yn, k + 1)
            act.wait_ge(m4_op, k)
            nc.scalar.activation(m4_yh, m4_sg[:, :, c * P:(c + 1) * P], ACT.Copy).then_inc(m4_yhi, 1)

        def deviation(act, gi, x, c):
            k = gi * CG + (x * 4 + c + 1)
            act.wait_ge(m4_qp, k + 1)
            act.wait_ge(m4_rk, k)
            nc.scalar.activation(m4_sd, psum[:, 7, 3 * P:3 * P + 1], ACT.Sqrt, scale=1.0 / GF,
                                 bias=epsc[:, 0:1]).then_inc(m4_sdk, 1)

        def dve_l2_attn(dve, ch):
            for c in (m4_ok, m4_mk, m4_rk, m4_yk, m4_sk, m4_nwk):
                dve.sem_inc(c, 1)
            dve.sem_inc(m4_wlo, 2)
            dve.sem_inc(m4_tk, 2)
            dve.wait_ge(m4_cin, 6 * 16)
            dve.wait_ge(m4_dw, 2)
            nc.vector.scalar_tensor_tensor(out=m4_dl, in0=m4_dr, scalar=WS, in1=m4_dh, op0=ALU.mult,
                                           op1=ALU.subtract).then_inc(m4_dw, 1)
            nc.vector.memset(m4_acc, 0.0)
            nc.vector.memset(m4_o32, 1.0)
            nc.vector.memset(m4_hb[:, :, 0:KC - 1], 0.0).then_inc(m4_cy, 1)
            for j in range(QI):
                dve_piece(dve, 0, j)
            for n in range(2):
                hc = slice(n * 8 * HS, (n + 1) * 8 * HS)
                by_tile = lambda v: v.rearrange("p (t h) -> p t h", h=HS)
                dve.wait_ge(m4_dp, n + 1)
                nc.vector.scalar_tensor_tensor(out=by_tile(m4_u), in0=by_tile(ps_m), scalar=1.0 / WS,
                                               in1=m4_db.unsqueeze(1).broadcast_to([P, 8, HS]), op0=ALU.mult,
                                               op1=ALU.add).then_inc(m4_tv, 1)
                dve.wait_ge(m4_ta, 5 * n + 3)
                ch.link(nc.vector.scalar_tensor_tensor(out=m4_dtp[:, hc], in0=m4_u, scalar=0.0, in1=m4_v, op0=ALU.max,
                                                       op1=ALU.add))
                ch.link(nc.vector.scalar_tensor_tensor(out=by_tile(m4_u), in0=by_tile(m4_dtp[:, hc]), scalar=-1.0,
                                                       in1=m4_na.unsqueeze(1).broadcast_to([P, 8, HS]), op0=ALU.mult,
                                                       op1=ALU.mult))
                nc.vector.tensor_scalar(m4_u, m4_u, -1000.0, None, ALU.max).then_inc(m4_tv, 1)
                dve.wait_ge(m4_ta, 5 * n + 4)
                nc.vector.tensor_tensor(m4_al[:, hc], m4_u, m4_ah[:, hc], ALU.subtract).then_inc(m4_tv, 1)
                dve.wait_ge(m4_ta, 5 * n + 5)
                nc.vector.tensor_tensor(m4_dt2[:, hc], m4_dtp[:, hc], m4_v, ALU.mult).then_inc(m4_tv, 1)
            dve.wait_ge(m4_tv, 8)

            with loop(dve, GS, (ch, HF * (CT * (KC - 1) + 4 * 3))) as gi:
                dve.wait_ge(m4_pi, gi * 16 + 16)
                dve.wait_ge(m4_wlo, gi * QS + (QI + 2))
                dve.wait_ge(m4_ok, gi * CG + 1)
                nc.vector.tensor_scalar(m4_par, m4_pn, 1.0, None, ALU.mult).then_inc(m4_nwk, 1)
                dve.wait_ge(m4_nwk, gi * 2 + 2)
                nc.vector.tensor_scalar(m4_nw, m4_par[:, CT * (KC + 1) + 4:], WS, None, ALU.mult).then_inc(m4_nwk, 1)
                dve.wait_ge(m4_nwk, gi * 2 + 3)
                for j in range(QI, QI + 2):
                    dve_piece(dve, gi, j)
                for x in range(HF):
                    if x % 2 == 0:
                        dve.wait_ge(m4_sn, gi * CG + (x * 4 + 1))
                        dve.wait_ge(m4_sk, gi * (CG + 2) + (x * 4 + x // 2 + 1))
                        nc.vector.memset(m4_st, 0.0).then_inc(m4_sk, 1)
                    convolve(dve, ch, gi, x)
                    if x == 0:
                        for j in range(QI + 2, QS):
                            dve_piece(dve, gi, j)
                        dve.wait_ge(m4_gd, gi * 2 + 2)
                    masked(dve, ch, gi, x, 0)
                    stepped(dve, gi, x, 0)
                    masked(dve, ch, gi, x, 1)
                    for c in range(4):
                        from_state(dve, gi, x, c)
                        state(dve, ch, gi, x, c)
                        outputs(dve, ch, gi, x, c)
                        if c < 3:
                            stepped(dve, gi, x, c + 1)
                        if x == HF - 1:
                            dve_piece(dve, gi, QS + 2 * c)
                        if c:
                            add_out(dve, gi, x, c - 1)
                        if c < 2:
                            masked(dve, ch, gi, x, c + 2)
                        if x == HF - 1:
                            dve_piece(dve, gi, QS + 2 * c + 1)
                    add_out(dve, gi, x, 3)
            s = 4 - start

            def summed(j):
                dve.wait_ge(m4_ok, GS * CG + 1)
                dve.sem_inc(y_ready, 1)
            dve_group(dve, ch, s, 0, y=lambda j: m4_acc[:, j, :], before=summed, tiles=NT)

        def convolve(dve, ch, gi, x):
            dve.wait_ge(m4_qk, gi * CG + (x * 4 + 1))
            dve.wait_ge(m4_yn, gi * CG + (x * 4 + 1))
            dve.wait_ge(m4_cy, gi * HF + (x + 1))
            for i in range(CT):
                dve.wait_ge(m4_hbk, gi * (HF * CT) + (x * CT + i + 1))
                tap = lambda j: m4_par[:, i * KC + j:i * KC + j + 1]
                out = m4_xc[:, i, :]
                ch.link(nc.vector.tensor_scalar(out, m4_hb[:, i, 0:GW], tap(0), m4_par[:, CT * KC + i:CT * KC + i + 1],
                                                ALU.mult, ALU.add))
                for j in range(1, KC):
                    v = nc.vector.scalar_tensor_tensor(out=out, in0=m4_hb[:, i, j:j + GW], scalar=tap(j), in1=out,
                                                       op0=ALU.mult, op1=ALU.add)
                    if j < KC - 1:
                        ch.link(v)
                v.then_inc(m4_cv, 1)
            dve.wait_ge(m4_cv, gi * (HF * CT) + (x + 1) * CT)
            if x % 2 == 0:
                nc.vector.tensor_scalar(m4_hb[:, :, 0:KC - 1], m4_hb[:, :, GW:GW + KC - 1], 1.0, None,
                                        ALU.mult).then_inc(m4_cy, 1)
            else:
                nc.vector.memset(m4_hb[:, :, 0:KC - 1], 0.0).then_inc(m4_cy, 1)

        def masked(dve, ch, gi, x, c):
            k = gi * CG + (x * 4 + c + 1)
            dve.wait_ge(m4_gp, k)
            dve.wait_ge(m4_mk, k)
            ch.link(nc.vector.tensor_tensor(m4_gm, psum[:, 7, P:2 * P], m4_le, ALU.mult))
            dve.wait_ge(m4_ek, k + 1)
            e = m4_e[c % 2]
            nc.vector.tensor_tensor(e, e, m4_gm.unsqueeze(1).broadcast_to([P, HG, P]), ALU.mult).then_inc(m4_mk, 1)

        def stepped(dve, gi, x, c):
            k = gi * CG + (x * 4 + c + 1)
            dve.wait_ge(m4_xp, k)
            dve.wait_ge(m4_sn, k)
            xs = psum[:, 6, :].rearrange("p (h c) -> p h c", h=HG)
            for n, d in enumerate((m4_dtp, m4_dt2)):
                steps = d[:, ds(gi * HG + (x * 4 + c) * HS, HG)]
                nc.vector.tensor_tensor(m4_x12[:, n * GF:(n + 1) * GF].rearrange("p (h c) -> p h c", h=HG), xs,
                                        steps.unsqueeze(2).broadcast_to([P, HG, PS]), ALU.mult).then_inc(m4_x2, 1)

        def from_state(dve, gi, x, c):
            k = gi * CG + (x * 4 + c + 1)
            dve.wait_ge(m4_ii, k)
            dve.wait_ge(m4_dk, k + 1)
            dve.wait_ge(m4_yk, k)
            nc.vector.tensor_tensor(m4_ty.rearrange("p i t -> p (i t)"), psum[:, 3, :],
                                    m4_de[:, c % 2].rearrange("p i t -> p (i t)"), ALU.mult).then_inc(m4_tk, 1)

        def outputs(dve, ch, gi, x, c):
            k = gi * CG + (x * 4 + c + 1)
            tok = slice(c * P, (c + 1) * P)
            flat = m4_ty.rearrange("p i t -> p (i t)")
            dve.wait_ge(m4_ia, k + 2)
            dve.wait_ge(m4_tk, k + 2)
            ch.link(nc.vector.tensor_tensor(flat, flat, psum[:, 2, :], ALU.add))
            for i in range(4):
                d = CT * (KC + 1) + i
                v = nc.vector.scalar_tensor_tensor(out=m4_xc[:, i, tok], in0=m4_xc[:, i, tok], scalar=m4_par[:, d:d + 1],
                                                   in1=m4_ty[:, i, :], op0=ALU.mult, op1=ALU.add)
            v.then_inc(m4_yk, 1)

        def state(dve, ch, gi, x, c):
            dve.wait_ge(m4_sn, gi * CG + (x * 4 + c + 2))
            dve.wait_ge(m4_sk, gi * (CG + 2) + (x * 4 + c + x // 2 + 2))
            by_head = m4_st.rearrange("p (h c) -> p h c", h=HG)
            da = m4_dg[:, (x * 4 + c) * HG:(x * 4 + c + 1) * HG]
            ch.link(nc.vector.tensor_tensor(by_head, by_head, da.unsqueeze(2).broadcast_to([P, HG, PS]), ALU.mult))
            nc.vector.tensor_tensor(m4_st, m4_st, psum[:, 6, :], ALU.add).then_inc(m4_sk, 1)

        def add_out(dve, gi, x, c):
            k = gi * CG + (x * 4 + c + 1)
            dve.wait_ge(m4_sdk, k + 1)
            dve.wait_ge(m4_ok, k)
            nc.vector.reciprocal(m4_rs, m4_sd).then_inc(m4_rk, 1)
            dve.wait_ge(m4_rk, k + 1)
            dve.wait_ge(m4_op, k + 1)
            acc = m4_acc[:, x * 4 + c, :]
            nc.vector.scalar_tensor_tensor(out=acc, in0=psum[:, 5, :], scalar=m4_rs, in1=acc, op0=ALU.mult,
                                           op1=ALU.add).then_inc(m4_ok, 1)

        def pool_l2_attn(pool):
            for c in (m4_yn, m4_ylo):
                pool.sem_inc(c, 1)
            pool.wait_ge(m4_tv, 4 + 3)

            def spread(gi, j):
                pool.wait_ge(m4_sp, gi * CG + (j + 1))
                alone(pool)
                heads = [a[:, ds(gi * HG + (j * HS), HG)].unsqueeze(2) for a in (m4_ah, m4_al)]
                for n in range(2):
                    nc.gpsimd.tensor_tensor(m4_ar[:, n], heads[n].broadcast_to([P, HG, P]),
                                            m4_le.unsqueeze(1).broadcast_to([P, HG, P]), ALU.mult).then_inc(m4_ak, 1)
                pool.wait_ge(m4_dd, gi * CG + (j + 1))
                alone(pool)
                for n in range(2):
                    nc.gpsimd.tensor_tensor(m4_ab[:, n].rearrange("p (h c) -> p h c", c=PS),
                                            heads[n].broadcast_to([P, HG, PS]),
                                            m4_on[:, 0:PS].unsqueeze(1).broadcast_to([P, HG, PS]),
                                            ALU.mult).then_inc(m4_ak, 1)

            with pool.Fori(0, GS) as gi:
                spread(gi, 0)
                for x in range(HF):
                    spread(gi, x * 4 + 1)
                    for c in range(4):
                        k = gi * CG + (x * 4 + c + 1)
                        tok = slice(c * P, (c + 1) * P)
                        if c < 2 or (c == 2 and x < HF - 1):
                            spread(gi, x * 4 + c + 2)
                        pool.wait_ge(m4_yk, k + 1)
                        pool.wait_ge(m4_gk, gi * (HF * 4) + (x * 4 + 4))
                        nc.gpsimd.tensor_tensor(m4_sg[:, :, tok], m4_xc[:, 0:4, tok], m4_sg[:, :, tok],
                                                ALU.mult).then_inc(m4_yn, 1)
                        pool.wait_ge(m4_yn, k + 1)
                        pool.wait_ge(m4_yhi, k)
                        nc.gpsimd.tensor_tensor(m4_yl, m4_sg[:, :, tok], m4_yh, ALU.subtract).then_inc(m4_ylo, 1)

        def pe_l2_attn(pe):
            s = 4 - start
            for c in (m4_op, m4_sp, m4_dd, m4_sn, m4_qp, m4_ia, m4_ia):
                pe.sem_inc(c, 1)
            pe.wait_ge(xt_ok, NT * (s + 1))
            pe.wait_ge(m4_dw, 3)
            for n in range(2):
                if n:
                    pe.wait_ge(m4_tv, 4 * n - 3)
                for j in range(8):
                    tok = slice((n * 8 + j) * P, (n * 8 + j + 1) * P)
                    for k in range(KT):
                        last = three(pe, ps_m[:, j * HS:(j + 1) * HS], xt_hi[:, k, tok], xt_lo[:, k, tok],
                                     m4_dh[:, k, :], m4_dl[:, k, :], k == 0, k == KT - 1)
                last.then_inc(m4_dp, 1)
            for n in range(2):
                hc = slice(n * 8 * HS, (n + 1) * 8 * HS)
                pe.wait_ge(m4_tv, 4 * n + 3)
                if n:
                    pe.wait_ge(m4_ta, 5 * n)
                nc.tensor.matmul(psum[:, 6, :], m4_gt, m4_ah[:, hc], start=True, stop=False)
                nc.tensor.matmul(psum[:, 6, :], m4_gt, m4_al[:, hc], start=False, stop=True).then_inc(m4_dp, 1)
            pe.wait_ge(m4_ta, 10)

            with pe.Fori(0, GS) as gi:
                pe.wait_ge(m4_sdk, gi * CG + 1)
                for n, a in enumerate((m4_ah, m4_al)):
                    v = nc.tensor.matmul(psum[:, 7, 0:NT * HG], m4_on,
                                         a.rearrange("p (t h) -> p t h", h=HS)[:, :, ds(gi * HG, HG)],
                                         start=(n == 0), stop=(n == 1))
                v.then_inc(m4_gd, 1)
                pe.wait_ge(m4_wlo, gi * QS + (QI + 2))
                for x in range(HF):
                    in_proj(pe, gi, x, range(2 if x else 0, 8))
                    between(pe, gi, x, 0)
                    in_proj(pe, gi, x, range(8, 9))
                    b_dot_c(pe, gi, x, 0)
                    to_tokens(pe, gi, x, 0)
                    between(pe, gi, x, 1)
                    b_to_tokens(pe, gi, x, 0)
                    b_dot_c(pe, gi, x, 1)
                    for c in range(4):
                        chunk(pe, gi, x, c)
                        if c:
                            out_proj(pe, gi, x, c - 1)
                        if c == 0:
                            in_proj(pe, gi, x, range(9, 10))
                        if c < 3:
                            to_tokens(pe, gi, x, c + 1)
                            b_to_tokens(pe, gi, x, c + 1)
                        if c < 2:
                            between(pe, gi, x, c + 2)
                            b_dot_c(pe, gi, x, c + 2)
                    if x < HF - 1:
                        in_proj(pe, gi, x + 1, range(0, 2))
                    out_proj(pe, gi, x, 3)
            pe_group(pe, s, 0, lambda j: None, tiles=NT)

        def in_proj(pe, gi, x, tiles):
            for i in tiles:
                if 4 <= i < 8:
                    pe.wait_ge(m4_hbk, gi * (HF * CT) + (x * CT + i - 3))
                if i == 8:
                    pe.wait_ge(m4_gk, gi * (HF * 4) + (x * 4 + 1))
                if i == 9:
                    pe.wait_ge(m4_ok, gi * CG + (x * 4 + 1))
                for k in range(KT):
                    fc = slice(i * P, (i + 1) * P)
                    tok = slice(x * GW, (x + 1) * GW)
                    last = three(pe, psum[:, BANK[i], :], m4_wh[:, k, fc], m4_wl[:, k, fc], xt_hi[:, k, tok],
                                 xt_lo[:, k, tok], k == 0, k == KT - 1)
                last.then_inc(m4_ip, 1)

        def b_dot_c(pe, gi, x, c):
            k = gi * CG + (x * 4 + c + 1)
            tok = slice(c * P, (c + 1) * P)
            if c == 0:
                pe.wait_ge(m4_gd, gi * 2 + 2)
                pe.wait_ge(m4_xk, gi * (HF * CT) + (x * CT + CT))
            pe.wait_ge(m4_sdk, gi * CG + (x * 4 + max(0, c - 2) + 1))
            pe.wait_ge(m4_mk, k)
            nc.tensor.matmul(psum[:, 7, P:2 * P], m4_xc[:, 4, tok], m4_xc[:, 5, tok], start=True,
                             stop=True).then_inc(m4_gp, 1)

        def between(pe, gi, x, c):
            k = gi * CG + (x * 4 + c + 1)
            ak = gi * (4 * CG) + (x * 4 + c) * 4
            if c == 0:
                pe.wait_ge(m4_hbk, gi * (HF * CT) + (x * CT + CT))
            pe.wait_ge(m4_ek, k)
            pe.wait_ge(m4_ak, ak + 2)
            for q in range(2):
                for n in range(2):
                    last = nc.tensor.matmul(psum[:, q, :], m4_gt, m4_ar[:, n, 4 * q:4 * q + 4, :], start=(n == 0),
                                            stop=(n == 1))
            last.then_inc(m4_sp, 1)
            pe.wait_ge(m4_dk, k)
            pe.wait_ge(m4_ak, ak + 4)
            for i in range(4):
                for n in range(2):
                    last = nc.tensor.matmul(psum[:, 4, i * P:(i + 1) * P], m4_ab[:, n, i * P:(i + 1) * P], m4_le,
                                            start=(n == 0), stop=(n == 1))
            last.then_inc(m4_dd, 1)

        def to_tokens(pe, gi, x, c):
            k = gi * CG + (x * 4 + c + 1)
            tok = slice(c * P, (c + 1) * P)
            if c == 0:
                pe.wait_ge(m4_xk, gi * (HF * CT) + (x * CT + CT))
            pe.wait_ge(m4_sk, gi * (CG + 2) + (x * 4 + c + x // 2 + 2))
            for i in range(4):
                nc.tensor.transpose(psum[:, 6, i * P:(i + 1) * P], m4_xc[:, i, tok], ident[:, :])

        def b_to_tokens(pe, gi, x, c):
            k = gi * CG + (x * 4 + c + 1)
            tok = slice(c * P, (c + 1) * P)
            pe.wait_ge(m4_tk, k + 1)
            if c == 0:
                pe.wait_ge(m4_gk, gi * (HF * 4) + (x * 4 + 3))
            nc.tensor.transpose(psum[:, 3, 0:P], m4_xc[:, 4, tok], ident[:, :]).then_inc(m4_xp, 1)

        def chunk(pe, gi, x, c):
            k = gi * CG + (x * 4 + c + 1)
            tok = slice(c * P, (c + 1) * P)
            pe.wait_ge(m4_sk, gi * (CG + 2) + (x * 4 + c + x // 2 + 2))
            pe.wait_ge(m4_bk, k + 1)
            for i in range(4):
                last = nc.tensor.matmul(psum[:, 3, i * P:(i + 1) * P], m4_st[:, i * P:(i + 1) * P], m4_xc[:, 5, tok],
                                        start=True, stop=True)
            last.then_inc(m4_ii, 1)
            pe.wait_ge(m4_mk, k + 1)
            pe.wait_ge(m4_x2, gi * (2 * CG) + (2 * (x * 4 + c) + 1))
            pe.wait_ge(m4_yk, k)
            for i in range(HG):
                e = i % 2
                last = nc.tensor.matmul(psum[e * PS:(e + 1) * PS, 2, (i // 2) * P:(i // 2 + 1) * P],
                                        m4_x12[:, i * PS:(i + 1) * PS], m4_e[c % 2][:, i, :], start=True, stop=True)
            last.then_inc(m4_ia, 1)
            pe.wait_ge(m4_x2, gi * (2 * CG) + (2 * (x * 4 + c) + 2))
            nc.tensor.matmul(psum[:, 6, :], m4_bt, m4_x12[:, GF:], start=True, stop=True).then_inc(m4_sn, 1)

        def out_proj(pe, gi, x, c):
            k = gi * CG + (x * 4 + c + 1)
            ahead = gi * CG + (x * 4 + min(c + 2, 3) + 2)
            pe.wait_ge(m4_qk, k + 1)
            pe.wait_ge(m4_sdk, k)
            pe.wait_ge(m4_mk, ahead)
            for i in range(4):
                last = nc.tensor.matmul(psum[:, 7, 3 * P:3 * P + 1], m4_sq[:, i, :], m4_o32, start=(i == 0), stop=(i == 3))
            last.then_inc(m4_qp, 1)
            pe.wait_ge(m4_ylo, k + 1)
            pe.wait_ge(m4_ok, k)
            if x == 0 and c == 0:
                pe.wait_ge(m4_wlo, gi * QS + (QS + 2))
            for i in range(4):
                last = three(pe, psum[:, 5, :], m4_yh[:, i, :], m4_yl[:, i, :], m4_wh[:, i, IW:], m4_wl[:, i, IW:],
                             i == 0, i == 3)
            last.then_inc(m4_op, 1)

        def sp_l2_ffn(sp):
            arena_free(sp, 5)
            row = lambda n: A[n].rearrange("(o n) -> o n", o=1).broadcast_to([P, C])
            sp.dma_start(s5_raw[:, 0], A["w1T"].rearrange("(k p) n -> p k n", p=P)).then_inc(s5_in, 16)
            sp.dma_start(s5_raw[:, 1], A["w3T"].rearrange("(k p) n -> p k n", p=P)).then_inc(s5_in, 16)
            sp.dma_start(s5_s0, A["scaling0_p"]).then_inc(s5_in, 16)
            sp.dma_start(s5_s2, A["scaling2_p"]).then_inc(s5_in, 16)
            sp.dma_start(s5_s4, row("L2_ffn_scaling4")).then_inc(s5_in, 16)
            sp.dma_start(s5_b, row("L2_ffn_bias")).then_inc(s5_in, 16)

        def dve_l2_ffn(dve, ch):
            dve.wait_ge(s5_in, 96)
            ch.link(nc.vector.tensor_scalar(s5_w1, s5_raw[:, 0], 2.0, -1.0, ALU.mult, ALU.add))
            for k in range(KT):
                nc.vector.tensor_scalar(s5_w1[:, k, :], s5_w1[:, k, :], s5_s0[:, k:k + 1], WS, ALU.mult,
                                        ALU.mult).then_inc(s5_wf, 1)
            nc.vector.tensor_scalar(s5_w3, s5_raw[:, 1], 2.0, -1.0, ALU.mult, ALU.add).then_inc(s5_w, 1)
            nc.vector.tensor_scalar(s5_s4, s5_s4, 1.0 / ACTS, None, ALU.mult).then_inc(s5_w, 1)
            dve.wait_ge(s5_hi, 1)
            nc.vector.tensor_tensor(s5_w1l, s5_w1, s5_w1h, ALU.subtract).then_inc(s5_w, 1)
            s = 5 - start
            dve.wait_ge(s5_w, 2)
            with loop(dve, NG, (ch, 5 * GT)) as g:
                for f in range(KT):
                    dve.wait_ge(s5_hhi, g * KT + (f + 1))
                    nc.vector.scalar_tensor_tensor(out=s5_hl[:, f, :], in0=ps_g[:, f, :], scalar=s5_s2[:, f:f + 1],
                                                   in1=s5_hh[:, f, :], op0=ALU.mult,
                                                   op1=ALU.subtract).then_inc(s5_hlo, 1)

                def affine(j):
                    dve.wait_ge(s5_p, g * GT + (j + 1))
                    ch.link(nc.vector.tensor_tensor(s5_y[:, j % 2, :], ps_y[:, j % 2, :], s5_s4, ALU.mult))
                    nc.vector.tensor_tensor(s5_y[:, j % 2, :], s5_y[:, j % 2, :], s5_b, ALU.add).then_inc(y_ready, 1)
                dve_group(dve, ch, s, g, y=lambda j: s5_y[:, j % 2, :], before=affine)

        def act_l2_ffn(act):
            act.wait_ge(s5_wf, KT)
            nc.scalar.activation(s5_w1h, s5_w1, ACT.Copy).then_inc(s5_hi, 1)
            s = 5 - start
            with act.Fori(0, NG) as g:
                for f in range(KT):
                    act.wait_ge(s5_h, g * KT + (f + 1))
                    nc.scalar.activation(s5_hh[:, f, :], ps_g[:, f, :], ACT.Copy,
                                         scale=s5_s2[:, f:f + 1]).then_inc(s5_hhi, 1)
                act_group(act, s, g, epsc[:, 0:1], y=lambda j: s5_y[:, j % 2, :])

        def pe_l2_ffn(pe):
            pe.wait_ge(s5_w, 3)
            s = 5 - start
            with pe.Fori(0, NG) as g:
                pe.wait_ge(xt_ok, g * GT + (NT * s + GT))
                for f in range(KT):
                    for k in range(KT):
                        fc = slice(f * P, (f + 1) * P)
                        last = three(pe, ps_g[:, f, :], s5_w1h[:, k, fc], s5_w1l[:, k, fc],
                                     xt_hi[:, k, ds(g * GW, GW)], xt_lo[:, k, ds(g * GW, GW)], k == 0, k == KT - 1)
                    last.then_inc(s5_h, 1)

                def y_tile(j):
                    r = g * GT + (NT * (s - yb) + j)
                    if j >= 2:
                        pe.wait_ge(y_ready, r - 1)
                    tok = slice(j * P, (j + 1) * P)
                    for k in range(KT):
                        if j == 0:
                            pe.wait_ge(s5_hlo, g * KT + (k + 1))
                        nc.tensor.matmul(ps_y[:, j % 2, :], s5_hh[:, k, tok], s5_w3[:, k, :], start=(k == 0), stop=False)
                        last = nc.tensor.matmul(ps_y[:, j % 2, :], s5_hl[:, k, tok], s5_w3[:, k, :], start=False,
                                                stop=(k == KT - 1))
                    last.then_inc(s5_p, 1)
                pe_group(pe, s, g, y_tile)

        def sp_l3_ffn(sp):
            arena_free(sp, 7)
            sp.dma_start(sh7, A["shifts"]).then_inc(sh7_in, 16)
            for i, (m, k, rows) in enumerate(pieces7):
                name, _, _, w = mats7[m]
                if i >= 2:
                    sp.wait_ge(q7_done, i - 1)
                qw = A[f"L3_ffn_{name}_qweight"]
                for j in range(8):
                    sp.dma_start(q7[j:rows * 8:8, i % 2, 0:w], qw[16 * k:16 * k + rows, :]).then_inc(q7_in[i % 2], 16)
                if i:
                    sp.wait_ge(w7_f, i)
                sp.dma_start(z7p[:, 0:w // 8], A[f"L3_ffn_{name}_zeros"][k:k + 1, :].broadcast_to([P, w // 8])).then_inc(z7_in, 16)
                sp.dma_start(s7[:, 0:w], A[f"L3_ffn_{name}_scales"][k:k + 1, :].broadcast_to([P, w])).then_inc(z7_in, 16)

        def dve_l3_ffn(dve, ch):
            for t in (g7h, g7l, u7h, u7l):
                nc.vector.memset(t[:, :, INTER:FW3], 0.0).then_inc(w7_l, 1)
            for t in (d7h, d7l):
                nc.vector.memset(t[96:P, F3 - 1, :], 0.0).then_inc(w7_l, 1)
            dve.wait_ge(sh7_in, 16)

            def piece(i):
                m, k, rows = pieces7[i]
                _, h_, l_, w = mats7[m]
                n = rows * 8
                word = q7[0:n, i % 2, 0:w]
                dve.wait_ge(z7_in, 32 * (i + 1))
                for j in range(8):
                    v = nc.vector.tensor_scalar(z7[:, 0:w // 8, j], z7p[:, 0:w // 8], 4 * j, 15, ALU.logical_shift_right,
                                                ALU.bitwise_and)
                ch.mark(v)
                dve.wait_ge(q7_in[i % 2], 128 * (i // 2 + 1))
                ch.link(nc.vector.tensor_scalar(word, word, sh7[0:n, :], 15, ALU.logical_shift_right, ALU.bitwise_and))
                if i:
                    dve.wait_ge(w7_l, 6 + i)
                z = z7[0:n, 0:w // 8, :].rearrange("p a b -> p (a b)")
                nc.vector.scalar_tensor_tensor(out=w7[0:n, 0:w], in0=word, scalar=1.0, in1=z, op0=ALU.subtract,
                                               op1=ALU.subtract).then_inc(q7_done, 1)
                dve.wait_ge(q7_done, i + 1)
                nc.vector.scalar_tensor_tensor(out=w7[0:n, 0:w], in0=w7[0:n, 0:w], scalar=WS, in1=s7[0:n, 0:w],
                                               op0=ALU.mult, op1=ALU.mult).then_inc(w7_f, 1)
                dve.wait_ge(w7_h, i + 1)
                nc.vector.tensor_tensor(l_[0:n, k, 0:w], w7[0:n, 0:w], h_[0:n, k, 0:w], ALU.subtract).then_inc(w7_l, 1)

            for i in range(2 * KT):
                piece(i)
            dve_ffn(dve, ch, 7 - start, F3, hid7h, hid7l, F0 * NG if on(1) else 0, sg7, hd7,
                    y=lambda j: y7[:, j % 2, :], last_layer=True, beside=lambda f: piece(2 * KT + f))

        def act_l3_ffn(act):
            def piece(i):
                m, k, rows = pieces7[i]
                _, h_, l_, w = mats7[m]
                n = rows * 8
                act.wait_ge(w7_f, i + 1)
                nc.scalar.activation(h_[0:n, k, 0:w], w7[0:n, 0:w], ACT.Copy).then_inc(w7_h, 1)

            for i in range(2 * KT):
                piece(i)

            def to_f16(g):
                def go(j):
                    act.wait_ge(p7_y, g * GT + (j + 1))
                    if j >= 2:
                        act.wait_ge(y_norm, g * GT + (NT * (7 - start - yb) + j - 1))
                    nc.scalar.activation(y7[:, j % 2, :], ps_y[:, j % 2, :], ACT.Copy,
                                         scale=1.0 / (WS * ACTS)).then_inc(y_ready, 1)
                return go
            act_ffn(act, 7 - start, F3, hid7h, F0 * NG if on(1) else 0, epsc[:, 0:1], sg7, hd7,
                    y=lambda j: y7[:, j % 2, :], last_layer=True, before=to_f16,
                    beside=lambda f: piece(2 * KT + f))

        def pe_l3_ffn(pe):
            pe_ffn(pe, 7 - start, F3, g7h, g7l, u7h, u7l, d7h, d7l, hid7h, hid7l, w7_l, 6 + 2 * KT,
                   F0 * NG if on(1) else 0, done=p7_y, last_layer=True, n_down=6 + len(pieces7))

        def sp_l3_attn(sp):
            arena_free(sp, 6)
            row = lambda n, a, w: A[n][a:a + w].rearrange("(o n) -> o n", o=1).broadcast_to([P, w])
            sp.dma_start(a6_raw, A["L3_attn_Wqkv"].rearrange("(k p) n -> p k n", p=P)).then_inc(a6_in, 16)
            sp.dma_start(a6_rwo, A["L3_attn_Wo"]).then_inc(a6_in, 16)
            sp.dma_start(a6_b, A["bqk_p"]).then_inc(a6_in, 16)
            sp.dma_start(a6_bv, row("L3_attn_bqkv", 2 * D3, D3)).then_inc(a6_in, 16)
            sp.dma_start(a6_bo, row("L3_attn_bo", 0, C)).then_inc(a6_in, 16)

        def dve_l3_attn(dve, ch):
            s = 6 - start
            dve.wait_ge(a6_who, 2)
            nc.vector.scalar_tensor_tensor(out=a6_wl, in0=a6_raw, scalar=WS, in1=a6_wh, op0=ALU.mult,
                                           op1=ALU.subtract).then_inc(a6_wok, 1)
            nc.vector.scalar_tensor_tensor(out=a6_ol, in0=a6_rwo, scalar=WS, in1=a6_oh, op0=ALU.mult,
                                           op1=ALU.subtract).then_inc(a6_wok, 1)
            dve.sem_inc(a6_pf, 1)
            with loop(dve, NG, (ch, 0)) as g:
                for f in range(3):
                    i = g * 3 + f
                    dve.wait_ge(a6_pp, i + 1)
                    if f < 2:
                        nc.vector.tensor_scalar(a6_qk[:, f, :], ps_g[:, f, :], 1.0 / WS, a6_b[:, f:f + 1], ALU.mult,
                                                ALU.add).then_inc(a6_pf, 1)
                        dve.wait_ge(a6_pho, i + 1)
                        nc.vector.tensor_tensor(a6_ql[:, f, ds(g * GW, GW)], a6_qk[:, f, :],
                                                a6_qh[:, f, ds(g * GW, GW)], ALU.subtract).then_inc(a6_plo, 1)
                    else:
                        nc.vector.scalar_tensor_tensor(out=a6_v, in0=ps_g[:, f, :].rearrange("p (j d) -> p j d", j=GT),
                                                       scalar=1.0 / WS, in1=a6_bv.unsqueeze(1).broadcast_to([P, GT, D3]),
                                                       op0=ALU.mult, op1=ALU.add).then_inc(a6_pf, 1)
                        dve.wait_ge(a6_pho, i + 1)
                        nc.vector.tensor_tensor(a6_vl[:, ds(g * GT, GT), :], a6_v, a6_vh[:, ds(g * GT, GT), :],
                                                ALU.subtract).then_inc(a6_plo, 1)
            with loop(dve, NG, (ch, 6 * GT)) as g:
                def maximum(j):
                    i = g * GT + j
                    b = 2 * (j % 2)
                    dve.wait_ge(a6_s, i + 1)
                    ch.link(nc.vector.tensor_reduce(a6_mx[:, j % 2, 0:1], ps_g[:, b:b + 2, :].rearrange("p a b -> p (a b)"),
                                                    AXX, ALU.max))
                    nc.vector.tensor_scalar(a6_mx[:, j % 2, 1:2], a6_mx[:, j % 2, 0:1], -SC6, None,
                                            ALU.mult).then_inc(a6_m, 1)

                def attend(j):
                    i = g * GT + j
                    if j == 0:
                        maximum(0)
                    if j < GT - 1:
                        maximum(j + 1)
                    dve.wait_ge(a6_tho, i + 1)
                    nc.vector.tensor_tensor(a6_pl.rearrange("p a b -> p (a b)"), psum[:, 6:8, :].rearrange("p a b -> p (a b)"),
                                            a6_ph.rearrange("p a b -> p (a b)"), ALU.subtract).then_inc(a6_tlo, 1)
                    dve.wait_ge(a6_oho, i + 1)
                    nc.vector.tensor_tensor(a6_tl, ps_y[:, 1, 0:P], a6_th, ALU.subtract).then_inc(a6_olo, 1)
                    dve.wait_ge(a6_e, i + 2)
                    nc.vector.reciprocal(a6_mx[:, j % 2, 3:4], a6_mx[:, j % 2, 2:3]).then_inc(dve_seq, 1)
                    ch.add()
                    ch.wait(ch())
                    nc.vector.tensor_scalar(a6_mx[:, j % 2, 1:2], a6_mx[:, j % 2, 3:4], 1.0 / WS, None,
                                            ALU.mult).then_inc(a6_inv, 1)
                    dve.wait_ge(a6_inv, i + 1)
                    dve.wait_ge(a6_yp, i + 1)
                    nc.vector.scalar_tensor_tensor(out=a6_y[:, j % 2, :], in0=ps_y[:, 0, :], scalar=a6_mx[:, j % 2, 1:2],
                                                   in1=a6_bo, op0=ALU.mult, op1=ALU.add).then_inc(y_ready, 1)
                dve_group_apart(dve, ch, s, g, y=lambda j: a6_y[:, j % 2, :], before=attend)

        def act_l3_attn(act):
            s = 6 - start
            act.wait_ge(a6_in, 80)
            nc.scalar.activation(a6_wh, a6_raw, ACT.Copy, scale=WS).then_inc(a6_who, 1)
            nc.scalar.activation(a6_oh, a6_rwo, ACT.Copy, scale=WS).then_inc(a6_who, 1)
            act.sem_inc(a6_e, 1)
            with act.Fori(0, NG) as g:
                for f in range(3):
                    act.wait_ge(a6_pf, g * 3 + (f + 2))
                    if f < 2:
                        nc.scalar.activation(a6_qh[:, f, ds(g * GW, GW)], a6_qk[:, f, :], ACT.Copy).then_inc(a6_pho, 1)
                    else:
                        nc.scalar.activation(a6_vh[:, ds(g * GT, GT), :], a6_v, ACT.Copy).then_inc(a6_pho, 1)
            with act.Fori(0, NG) as g:
                def exps(j):
                    b = 2 * (j % 2)
                    act.wait_ge(a6_m, g * GT + (j + 1))
                    nc.scalar.activation(a6_p[:, j % 2, :], ps_g[:, b:b + 2, :].rearrange("p a b -> p (a b)"), ACT.Exp,
                                         bias=a6_mx[:, j % 2, 1:2], scale=SC6,
                                         accum_out=a6_mx[:, j % 2, 2:3]).then_inc(a6_e, 1)

                def attend(j):
                    i = g * GT + j
                    if j == 0:
                        exps(0)
                    if j < GT - 1:
                        exps(j + 1)
                    act.wait_ge(a6_t, i + 1)
                    nc.scalar.activation(a6_ph.rearrange("p a b -> p (a b)"), psum[:, 6:8, :].rearrange("p a b -> p (a b)"),
                                         ACT.Copy).then_inc(a6_tho, 1)
                    act.wait_ge(a6_o, i + 1)
                    nc.scalar.activation(a6_th, ps_y[:, 1, 0:P], ACT.Copy).then_inc(a6_oho, 1)
                act_group_apart(act, s, g, epsc[:, 0:1], y=lambda j: a6_y[:, j % 2, :], before=attend)

        def pe_l3_attn(pe):
            s = 6 - start
            pe.wait_ge(a6_wok, 2)
            with pe.Fori(0, NG) as g:
                pe.wait_ge(xt_ok, g * GT + (NT * s + GT))
                pe.wait_ge(a6_pf, g * 3 + 1)
                for f in range(2):
                    for k in range(KT):
                        fc = slice(f * D3, (f + 1) * D3)
                        last = three(pe, ps_g[:, f, :], a6_wh[:, k, fc], a6_wl[:, k, fc], xt_hi[:, k, ds(g * GW, GW)],
                                     xt_lo[:, k, ds(g * GW, GW)], k == 0, k == KT - 1)
                    last.then_inc(a6_pp, 1)
                for j in range(GT):
                    tok = ds(g * GW + j * P, P)
                    for k in range(KT):
                        last = three(pe, ps_g[:, 2, j * D3:(j + 1) * D3], xt_hi[:, k, tok], xt_lo[:, k, tok],
                                     a6_wh[:, k, 2 * D3:], a6_wl[:, k, 2 * D3:], k == 0, k == KT - 1)
                last.then_inc(a6_pp, 1)
            pe.wait_ge(a6_plo, 3 * NG)
            for b in range(NB):
                with pe.Fori(0, NG // NB) as gb:
                    g = gb + b * (NG // NB)

                    def scores(j):
                        i = g * GT + j
                        bank = 2 * (j % 2)
                        tok = ds(g * GW + j * P, P)
                        for half in range(2):
                            keys = slice(b * S6 + half * 512, b * S6 + (half + 1) * 512)
                            last = three(pe, ps_g[:, bank + half, :], a6_qh[:, 0, tok], a6_ql[:, 0, tok],
                                         a6_qh[:, 1, keys], a6_ql[:, 1, keys], True, True)
                        last.then_inc(a6_s, 1)

                    def y_tile(j):
                        i = g * GT + j
                        if j == 0:
                            pe.wait_ge(a6_e, i + 1)
                            scores(0)
                        if j < GT - 1:
                            pe.wait_ge(a6_e, i + 1)
                            scores(j + 1)
                        pe.wait_ge(a6_e, i + 2)
                        pe.wait_ge(xt_ok, g * GT + (NT * (s + 1) + (0 if j == 0 else j - 1)))
                        for k in range(TPB):
                            last = nc.tensor.transpose(psum[:, 6 + k // 4, (k % 4) * P:(k % 4 + 1) * P],
                                                       a6_p[:, j % 2, k * P:(k + 1) * P], ident[:, :])
                        last.then_inc(a6_t, 1)
                        pe.wait_ge(a6_tlo, i + 1)
                        for k in range(TPB):
                            last = three(pe, ps_y[:, 1, 0:P], a6_vh[:, b * TPB + k, :], a6_vl[:, b * TPB + k, :],
                                         a6_ph[:, k, :], a6_pl[:, k, :], k == 0, k == TPB - 1)
                        last.then_inc(a6_o, 1)
                        pe.wait_ge(a6_olo, i + 1)
                        last = three(pe, ps_y[:, 0, :], a6_th, a6_tl, a6_oh, a6_ol, True, True)
                        last.then_inc(a6_yp, 1)
                    pe_group(pe, s, g, y_tile, late=1)

        block = ctx.enter_context(nc.Block())

        @block.sync
        def _(sp):
            sp_x(sp)
            if on(0):
                sp_l0_attn(sp)
            if on(1):
                sp_l0_ffn(sp)
            if on(2):
                sp_l1_attn(sp)
            if on(3):
                sp_l1_ffn(sp)
            if on(4):
                sp_l2_attn(sp)
            if on(5):
                sp_l2_ffn(sp)
            if on(6):
                sp_l3_attn(sp)
            if on(7):
                sp_l3_ffn(sp)
            sp_out(sp)

        @block.gpsimd
        def _(pool):
            ch = Chain(pool, pool_seq)
            pool_consts(pool, ch)
            if on(1):
                pool_l0_ffn(pool)
            if on(2):
                pool_l1_attn(pool)
            if on(4):
                pool_l2_attn(pool)

        @block.tensor
        def _(pe):
            pe_x0(pe)
            if on(0):
                pe_l0_attn(pe)
            if on(1):
                pe_l0_ffn(pe)
            if on(2):
                pe_l1_attn(pe)
            if on(3):
                pe_l1_ffn(pe)
            if on(4):
                pe_l2_attn(pe)
            if on(5):
                pe_l2_ffn(pe)
            if on(6):
                pe_l3_attn(pe)
            if on(7):
                pe_l3_ffn(pe)

        @block.scalar
        def _(act):
            ch = Chain(act, act_seq)
            act_x0(act)
            if on(0):
                act_l0_attn(act, ch)
            if on(1):
                act_l0_ffn(act)
            if on(2):
                act_l1_attn(act)
            if on(3):
                act_l1_ffn(act)
            if on(4):
                act_l2_attn(act)
            if on(5):
                act_l2_ffn(act)
            if on(6):
                act_l3_attn(act)
            if on(7):
                act_l3_ffn(act)

        @block.vector
        def _(dve):
            ch = Chain(dve, dve_seq)
            dve_x0(dve, ch)
            if on(0):
                dve_l0_attn(dve, ch)
            if on(1):
                dve_l0_ffn(dve, ch)
            if on(2):
                dve_l1_attn(dve, ch)
            if on(3):
                dve_l1_ffn(dve, ch)
            if on(4):
                dve_l2_attn(dve, ch)
            if on(5):
                dve_l2_ffn(dve, ch)
            if on(6):
                dve_l3_attn(dve, ch)
            if on(7):
                dve_l3_ffn(dve, ch)



def constants():
    h = np.arange(1, 33)
    slope = (2.0 ** -0.25) ** h
    slope = slope.astype(np.float32)
    hi = slope.astype(np.float16)
    lo = (slope - hi.astype(np.float32)).astype(np.float16)
    pos = (np.arange(1024) - 512).astype(np.float16)
    above = np.triu(np.ones((P, P), np.float16), 1) * np.float16(-30000)
    return {
        "alibi_q": np.ascontiguousarray(np.broadcast_to(np.stack([hi, lo])[:, :, None], (2, 32, 1024))),
        "alibi_k": np.stack([pos, pos, np.ones(1024, np.float16)]),
        "ident16": np.eye(P, dtype=np.float16),
        "mask_qk": above, "mask_kq": np.ascontiguousarray(above.T),
        "tri_le": np.triu(np.ones((P, P), np.float16)), "tri_gt": np.tril(np.ones((P, P), np.float16), -1),
        "ones16": np.ones((P, P), np.float16),
        "shifts": (np.arange(P, dtype=np.int32) % 8 * 4).reshape(P, 1),
    }


def l2_attn_arrays(i):
    w, wo = np.asarray(i["L2_attn_in_proj_w"]), np.asarray(i["L2_attn_out_proj_w"])
    inner = wo.shape[1]
    n = w.shape[1]
    gs = inner // n
    bc = (w.shape[0] - 2 * inner) // (2 * gs)
    bc -= bc % P
    gate, xw = w[:inner], w[inner:2 * inner]
    bw, cw = w[2 * inner:2 * inner + gs * bc], w[2 * inner + gs * bc:2 * inner + 2 * gs * bc]
    cwt, cb = np.asarray(i["L2_attn_conv_weight"]), np.asarray(i["L2_attn_conv_bias"])
    nw = np.asarray(i["L2_attn_norm_weight"])
    d = np.repeat(np.asarray(i["L2_attn_D"]), inner // np.asarray(i["L2_attn_D"]).shape[0])
    ws, ps = [], []
    for g in range(gs):
        f, e = slice(g * n, (g + 1) * n), slice(g * bc, (g + 1) * bc)
        m = np.concatenate([xw[f], bw[e], cw[e], gate[f]]).T
        ws.append(m.reshape(n // P, P, 2, -1).transpose(0, 2, 1, 3).reshape(-1, P, m.shape[1] // 2))
        pick = lambda v: np.concatenate([v[:inner][f], v[inner:inner + gs * bc][e], v[inner + gs * bc:][e]])
        taps = pick(cwt).reshape(-1, P, cwt.shape[1]).transpose(1, 0, 2).reshape(P, -1)
        ps.append(np.concatenate([taps, pick(cb).reshape(-1, P).T, d[f].reshape(-1, P).T, nw[f].reshape(-1, P).T],
                                 axis=1))
    dt = w[2 * inner + 2 * gs * bc:].T.reshape(n // P, P, -1).transpose(1, 0, 2)
    ws.append(np.zeros_like(ws[0]))
    return {"m4_wi": np.ascontiguousarray(np.stack(ws)),
            "m4_wo": np.ascontiguousarray(wo.T.reshape(gs, n // P, P, -1)),
             "m4_par": np.ascontiguousarray(np.stack(ps, axis=1)),
            "m4_dt": np.ascontiguousarray(dt), "L2_attn_dt_bias": i["L2_attn_dt_bias"],
            "L2_attn_A_log": i["L2_attn_A_log"]}


def lay_out(i):
    t = lambda a: np.ascontiguousarray(np.asarray(a).T)
    cols = lambda a: np.ascontiguousarray(np.asarray(a).reshape(-1, P).T)
    return {
        "L0_attn_x": i["L0_attn_x"], "L0_attn_Wq": i["L0_attn_Wq"], "L0_attn_bq": i["L0_attn_bq"],
        "L0_attn_Wk": i["L0_attn_Wk"], "L0_attn_bk": i["L0_attn_bk"], "L0_attn_Wv": i["L0_attn_Wv"],
        "L0_attn_bv": i["L0_attn_bv"],
        "gate_wT": t(i["L0_ffn_gate_w"]), "gate_suT": t(i["L0_ffn_gate_su"]), "gate_sv": i["L0_ffn_gate_sv"],
        "up_wT": t(i["L0_ffn_up_w"]), "up_suT": t(i["L0_ffn_up_su"]), "up_sv": i["L0_ffn_up_sv"],
        "L1_ffn_sign": i["L1_ffn_sign"], "L1_ffn_scale": np.asarray(i["L1_ffn_scale"]).reshape(1, 1),
        "w1T": t(i["L2_ffn_w1_bits"]), "w3T": t(i["L2_ffn_w3_bits"]),
        **{k: i[k] for k in ("L2_ffn_scaling0", "L2_ffn_scaling2", "L2_ffn_scaling4", "L2_ffn_bias", "L3_attn_Wqkv",
                             "L3_attn_bqkv", "L3_attn_Wo", "L3_attn_bo")},
        **{f"L3_ffn_{m}_{w}": i[f"L3_ffn_{m}_{w}"] for m in ("gate", "up", "down")
           for w in ("qweight", "scales", "zeros")},
        "scaling0_p": cols(i["L2_ffn_scaling0"]), "scaling2_p": cols(i["L2_ffn_scaling2"]),
        "bqk_p": cols(np.asarray(i["L3_attn_bqkv"])[:C // 2]),
        "L1_attn_Wqkv": i["L1_attn_Wqkv"], "L1_attn_Wo": i["L1_attn_Wo"],
        **constants(), **l2_attn_arrays(i),
        "down_wT": t(i["L0_ffn_down_w"]), "down_suT": t(i["L0_ffn_down_su"]), "down_sv": i["L0_ffn_down_sv"],
    }


def kernel(**inputs):
    import concourse.bacc as bacc
    from concourse.bass_utils import run_bass_kernel_spmd

    nc = bacc.Bacc("TRN2", target_bir_lowering=False, num_devices=1)
    arrays = {k: np.ascontiguousarray(v) for k, v in lay_out(inputs).items()}
    A = {k: nc.dram_tensor(k, a.shape, mybir.dt.from_np(a.dtype), kind="ExternalInput").ap()
         for k, a in arrays.items()}
    A["out"] = nc.dram_tensor("out", (2, 1024, 512), F32, kind="ExternalOutput").ap()
    build(nc, A)
    return run_bass_kernel_spmd(nc, [arrays], core_ids=[0]).results[0]["out"]
```
